# Optimizing a Trainium2 kernel written in Bass

```python
import numpy as np
import jax
import jax.numpy as jnp

def _softmax(x, axis=-1):
    return jax.nn.softmax(x, axis=axis)

def _gelu(x):
    return jax.nn.gelu(x, approximate=True)

def _silu(x):
    return jax.nn.silu(x)

def _sigmoid(x):
    return jax.nn.sigmoid(x)

def _layernorm(x, axis=-1, eps=1e-05):
    m = jnp.mean(x, axis=axis, keepdims=True)
    v = jnp.var(x, axis=axis, keepdims=True)
    return (x - m) / jnp.sqrt(v + eps)

def _scatter_add(tgt, idx, src, axis=0):
    return tgt.at[idx].add(src)

def _segment_sum(src, seg, n):
    return jax.ops.segment_sum(src, seg, n)
kernel_name = 'mk_flamingo_gated_d2_seqx_r8_d8d926'

def setup_inputs(seed: int=0):
    np.random.seed(seed)
    _w = jnp.asarray

    def _rec_inputs():
        import jax
        import jax.numpy as jnp
        _rk = jax.random.key(seed)
        x = -0.0002928 + 1 * jax.random.normal(jax.random.fold_in(_rk, 1), (16, 64, 128), jnp.float32)
        _lenS = 64 - jax.random.randint(jax.random.fold_in(_rk, 7), (16,), 0, max(1, 64 // 4) + 1, jnp.int32)
        _lenS2 = 64 - jax.random.randint(jax.random.fold_in(_rk, 8), (16,), 0, max(1, 64 // 4) + 1, jnp.int32)
        _ctx_1024P = jax.random.normal(jax.random.fold_in(_rk, 11), (16, 16, 128), jnp.float32)
        _ctx_1024c = jax.random.dirichlet(jax.random.fold_in(_rk, 511), 0.3 * jnp.ones((16,), jnp.float32), (16, 64))
        _ctx_1024t = jnp.einsum('bsk,bkd->bsd', _ctx_1024c, _ctx_1024P)
        _ctx_1024t = _ctx_1024t * jax.lax.rsqrt(jnp.mean(jnp.square(_ctx_1024t)) + 1e-12) * 0.953939
        ctx_1024 = -1.39393e-06 + 0.999914 * (_ctx_1024t + 0.3 * jax.random.normal(jax.random.fold_in(_rk, 611), (16, 64, 128), jnp.float32))
        _validS = jnp.arange(64)[None, :] < _lenS[:, None]
        _validS2 = jnp.arange(64)[None, :] < _lenS2[:, None]
        _causal = jnp.tril(jnp.ones((64, 64), dtype=bool))
        mask_BxS2_ik1 = jnp.where(jnp.broadcast_to(_validS2[:, :], (16, 64)), 1, 0).astype(jnp.int32)
        _g = jax.random.normal(jax.random.fold_in(_rk, 9001), (2, 2), jnp.float32)
        _g = jnp.sign(_g) * jnp.maximum(jnp.abs(_g), 1.0) + (_g == 0) * 1.0
        g_xattn = _g[0]
        g_ffn = _g[1]
        return (x, ctx_1024, mask_BxS2_ik1, g_xattn, g_ffn)
    x, ctx_1024, mask_BxS2_ik1, g_xattn, g_ffn = _rec_inputs()

    def _L0_xattn_setup():
        import jax, jax.numpy as jnp
        import numpy as np
        K_DIM = 128
        HEADS = 16
        key = jax.random.key(seed)
        ks = jax.random.split(key, 8)
        b, t, tc, k = (2, 256, 256, K_DIM)
        scale = 1.0 / np.sqrt(k)
        x = jax.random.normal(ks[0], (b, t, k), dtype=jnp.float32)
        context = jax.random.normal(ks[1], (b, tc, k), dtype=jnp.float32)
        Wq = jax.random.normal(ks[2], (k, k), dtype=jnp.float32) * scale
        Wk = jax.random.normal(ks[3], (k, k), dtype=jnp.float32) * scale
        Wv = jax.random.normal(ks[4], (k, k), dtype=jnp.float32) * scale
        Wo = jax.random.normal(ks[5], (k, k), dtype=jnp.float32) * scale
        bo = jax.random.normal(ks[6], (k,), dtype=jnp.float32) * 0.01
        return {'x': x, 'context': context, 'Wq': Wq, 'Wk': Wk, 'Wv': Wv, 'Wo': Wo, 'bo': bo}
    _L0_xattn_all = _L0_xattn_setup()
    _L0_xattn_in = {k: v for k, v in _L0_xattn_all.items() if k in ('Wq', 'Wk', 'Wv', 'Wo', 'bo')}
    del _L0_xattn_all

    def _L0_ffn_setup():
        import jax, jax.numpy as jnp
        import numpy as np
        B, T, C, H, E, MIN_E = (4, 256, 128, 128, 16, 2)
        IS_CAUSAL = False

        def _forward(hidden_states, sim_matrix, gates, q_proj, k_proj, v_proj, o_proj):
            b, t, c = hidden_states.shape
            n = b * t
            x = hidden_states.reshape(n, c)
            xn = x / jnp.maximum(jnp.linalg.norm(x, axis=-1, keepdims=True), 1e-12)
            sn = sim_matrix / jnp.maximum(jnp.linalg.norm(sim_matrix, axis=0, keepdims=True), 1e-12)
            logits = xn @ sn - jax.nn.sigmoid(gates)
            gated = jax.nn.relu(logits)
            hard = (gated > 0).astype(gated.dtype)
            mask = gated + jax.lax.stop_gradient(hard - gated)
            inactive = jnp.sum(hard, axis=1) == 0
            _, fb_idx = jax.lax.top_k(logits, MIN_E)
            fb = jnp.zeros((n, logits.shape[1]), gated.dtype).at[jnp.arange(n)[:, None], fb_idx].set(1.0)
            put = jax.lax.stop_gradient(inactive[:, None].astype(gated.dtype) * fb)
            mask = mask * (1.0 - put) + put
            masked = jnp.where(mask > 0, gated, -jnp.inf)
            w = jax.nn.softmax(masked, axis=-1)

            def moe_proj(p):
                y = jnp.einsum('nc,ech->neh', x, p)
                return jnp.einsum('ne,neh->nh', w, y)
            q = moe_proj(q_proj).reshape(b, t, -1)
            k = moe_proj(k_proj).reshape(b, t, -1)
            v = moe_proj(v_proj).reshape(b, t, -1)
            h = q.shape[-1]
            scores = jnp.einsum('bth,bsh->bts', q, k) / jnp.sqrt(jnp.asarray(h, q.dtype))
            if IS_CAUSAL and t > 1:
                causal = jnp.tril(jnp.ones((t, t), bool))
                scores = jnp.where(causal[None], scores, -jnp.inf)
            attn = jax.nn.softmax(scores, axis=-1)
            o = jnp.einsum('bts,bsh->bth', attn, v).reshape(n, h)
            z = jnp.einsum('ne,nh->enh', w, o)
            out = jnp.einsum('enh,ehc->nc', z, o_proj)
            return out.reshape(b, t, c)
        key = jax.random.key(seed)
        ks = jax.random.split(key, 6)
        lim_qkv = float(np.sqrt(6.0 / (C + H)))
        inp = {'hidden_states': jax.random.normal(ks[0], (B, T, C), jnp.float32), 'sim_matrix': jax.random.normal(ks[1], (C, E), jnp.float32), 'gates': jnp.zeros((E,), jnp.float32), 'q_proj': jax.random.uniform(ks[2], (E, C, H), jnp.float32, -lim_qkv, lim_qkv), 'k_proj': jax.random.uniform(ks[3], (E, C, H), jnp.float32, -lim_qkv, lim_qkv), 'v_proj': jax.random.uniform(ks[4], (E, C, H), jnp.float32, -lim_qkv, lim_qkv), 'o_proj': jax.random.uniform(ks[5], (E, H, C), jnp.float32, -lim_qkv, lim_qkv)}
        return inp
    _L0_ffn_all = _L0_ffn_setup()
    _L0_ffn_in = {k: v for k, v in _L0_ffn_all.items() if k in ('sim_matrix', 'gates', 'q_proj', 'k_proj', 'v_proj', 'o_proj')}
    del _L0_ffn_all

    def _L1_xattn_setup():
        import jax, jax.numpy as jnp
        import numpy as np
        NEG_INF = -10000000000.0
        key = jax.random.key(seed)
        k1, k2, k3, k4 = jax.random.split(key, 4)
        B, Lq, Lk, D = (8, 256, 256, 128)
        hidden = jax.random.normal(k1, (B, Lq, D), dtype=jnp.float32)
        keys = jax.random.normal(k2, (B, Lk, D), dtype=jnp.float32)
        values = jax.random.normal(k3, (B, Lk, D), dtype=jnp.float32)
        mask = jax.random.randint(k4, (B, Lk), 0, 2, dtype=jnp.int32)
        return {'hidden': hidden, 'keys': keys, 'values': values, 'mask': mask}
    _L1_xattn_all = _L1_xattn_setup()
    _L1_xattn_in = {k: v for k, v in _L1_xattn_all.items() if k in ()}
    del _L1_xattn_all

    def _L1_ffn_setup():
        import jax, jax.numpy as jnp
        import numpy as np
        TOP_K = 8
        CAPACITY = 64

        def _silu(x):
            return x * jax.nn.sigmoid(x)
        key = jax.random.key(seed)
        ks = jax.random.split(key, 7)
        B, S, H, E, I, Is = (2, 128, 128, 64, 64, 256)
        s = 0.05
        return {'hidden_states': jax.random.normal(ks[0], (B, S, H), jnp.float32), 'gate_w': jax.random.normal(ks[1], (H, E), jnp.float32) * s, 'shared_gate_w': jax.random.normal(ks[2], (H, 1), jnp.float32) * s, 'shared_gate_up_w': jax.random.normal(ks[3], (H, 2 * Is), jnp.float32) * s, 'shared_down_w': jax.random.normal(ks[4], (Is, H), jnp.float32) * s, 'expert_gate_up_w': jax.random.normal(ks[5], (E, H, 2 * I), jnp.float32) * s, 'expert_down_w': jax.random.normal(ks[6], (E, I, H), jnp.float32) * s}
    _L1_ffn_all = _L1_ffn_setup()
    _L1_ffn_in = {k: v for k, v in _L1_ffn_all.items() if k in ('gate_w', 'shared_gate_w', 'shared_gate_up_w', 'shared_down_w', 'expert_gate_up_w', 'expert_down_w')}
    del _L1_ffn_all
    return {'x': x, 'ctx_1024': ctx_1024, 'mask_BxS2_ik1': mask_BxS2_ik1, 'g_xattn': g_xattn, 'g_ffn': g_ffn, 'L0_xattn_Wq': _L0_xattn_in['Wq'], 'L0_xattn_Wk': _L0_xattn_in['Wk'], 'L0_xattn_Wv': _L0_xattn_in['Wv'], 'L0_xattn_Wo': _L0_xattn_in['Wo'], 'L0_xattn_bo': _L0_xattn_in['bo'], 'L0_ffn_sim_matrix': _L0_ffn_in['sim_matrix'], 'L0_ffn_gates': _L0_ffn_in['gates'], 'L0_ffn_q_proj': _L0_ffn_in['q_proj'], 'L0_ffn_k_proj': _L0_ffn_in['k_proj'], 'L0_ffn_v_proj': _L0_ffn_in['v_proj'], 'L0_ffn_o_proj': _L0_ffn_in['o_proj'], 'L1_ffn_gate_w': _L1_ffn_in['gate_w'], 'L1_ffn_shared_gate_w': _L1_ffn_in['shared_gate_w'], 'L1_ffn_shared_gate_up_w': _L1_ffn_in['shared_gate_up_w'], 'L1_ffn_shared_down_w': _L1_ffn_in['shared_down_w'], 'L1_ffn_expert_gate_up_w': _L1_ffn_in['expert_gate_up_w'], 'L1_ffn_expert_down_w': _L1_ffn_in['expert_down_w']}

def reference(x, ctx_1024, mask_BxS2_ik1, g_xattn, g_ffn, L0_xattn_Wq, L0_xattn_Wk, L0_xattn_Wv, L0_xattn_Wo, L0_xattn_bo, L0_ffn_sim_matrix, L0_ffn_gates, L0_ffn_q_proj, L0_ffn_k_proj, L0_ffn_v_proj, L0_ffn_o_proj, L1_ffn_gate_w, L1_ffn_shared_gate_w, L1_ffn_shared_gate_up_w, L1_ffn_shared_down_w, L1_ffn_expert_gate_up_w, L1_ffn_expert_down_w):
    import jax
    import jax.numpy as jnp

    def _L0_xattn_ref(x, context, Wq, Wk, Wv, Wo, bo):
        import jax, jax.numpy as jnp
        import numpy as np
        K_DIM = 128
        HEADS = 16
        b, t, e = x.shape
        tc = context.shape[1]
        h = HEADS
        s = e // h
        q = (x @ Wq.T).reshape(b, t, h, s)
        k_ = (context @ Wk.T).reshape(b, tc, h, s)
        v = (context @ Wv.T).reshape(b, tc, h, s)
        inv4 = e ** (-0.25)
        q = q * inv4
        k_ = k_ * inv4
        dot = jnp.einsum('bthd,bchd->bhtc', q, k_)
        attn = jax.nn.softmax(dot, axis=-1)
        out = jnp.einsum('bhtc,bchd->bthd', attn, v).reshape(b, t, e)
        return out @ Wo.T + bo

    def _L0_ffn_ref(hidden_states, sim_matrix, gates, q_proj, k_proj, v_proj, o_proj):
        import jax, jax.numpy as jnp
        import numpy as np
        B, T, C, H, E, MIN_E = (4, 256, 128, 128, 16, 2)
        IS_CAUSAL = False

        def _forward(hidden_states, sim_matrix, gates, q_proj, k_proj, v_proj, o_proj):
            b, t, c = hidden_states.shape
            n = b * t
            x = hidden_states.reshape(n, c)
            xn = x / jnp.maximum(jnp.linalg.norm(x, axis=-1, keepdims=True), 1e-12)
            sn = sim_matrix / jnp.maximum(jnp.linalg.norm(sim_matrix, axis=0, keepdims=True), 1e-12)
            logits = xn @ sn - jax.nn.sigmoid(gates)
            gated = jax.nn.relu(logits)
            hard = (gated > 0).astype(gated.dtype)
            mask = gated + jax.lax.stop_gradient(hard - gated)
            inactive = jnp.sum(hard, axis=1) == 0
            _, fb_idx = jax.lax.top_k(logits, MIN_E)
            fb = jnp.zeros((n, logits.shape[1]), gated.dtype).at[jnp.arange(n)[:, None], fb_idx].set(1.0)
            put = jax.lax.stop_gradient(inactive[:, None].astype(gated.dtype) * fb)
            mask = mask * (1.0 - put) + put
            masked = jnp.where(mask > 0, gated, -jnp.inf)
            w = jax.nn.softmax(masked, axis=-1)

            def moe_proj(p):
                y = jnp.einsum('nc,ech->neh', x, p)
                return jnp.einsum('ne,neh->nh', w, y)
            q = moe_proj(q_proj).reshape(b, t, -1)
            k = moe_proj(k_proj).reshape(b, t, -1)
            v = moe_proj(v_proj).reshape(b, t, -1)
            h = q.shape[-1]
            scores = jnp.einsum('bth,bsh->bts', q, k) / jnp.sqrt(jnp.asarray(h, q.dtype))
            if IS_CAUSAL and t > 1:
                causal = jnp.tril(jnp.ones((t, t), bool))
                scores = jnp.where(causal[None], scores, -jnp.inf)
            attn = jax.nn.softmax(scores, axis=-1)
            o = jnp.einsum('bts,bsh->bth', attn, v).reshape(n, h)
            z = jnp.einsum('ne,nh->enh', w, o)
            out = jnp.einsum('enh,ehc->nc', z, o_proj)
            return out.reshape(b, t, c)
        return _forward(hidden_states, sim_matrix, gates, q_proj, k_proj, v_proj, o_proj)

    def _L1_xattn_ref(hidden, keys, values, mask):
        import jax, jax.numpy as jnp
        import numpy as np
        NEG_INF = -10000000000.0
        scores = jnp.einsum('bqd,bkd->bqk', hidden, keys)
        scores = jnp.where(mask[:, None, :] == 0, NEG_INF, scores)
        weights = jax.nn.softmax(scores, axis=2)
        context = jnp.einsum('bqk,bkd->bqd', weights, values)
        return context

    def _L1_ffn_ref(hidden_states, gate_w, shared_gate_w, shared_gate_up_w, shared_down_w, expert_gate_up_w, expert_down_w):
        import jax, jax.numpy as jnp
        import numpy as np
        TOP_K = 8
        CAPACITY = 64

        def _silu(x):
            return x * jax.nn.sigmoid(x)
        B, S, H = hidden_states.shape
        x = hidden_states.reshape(-1, H)
        T = x.shape[0]
        E = gate_w.shape[1]
        Is = shared_gate_up_w.shape[1] // 2
        I = expert_gate_up_w.shape[2] // 2
        gu = x @ shared_gate_up_w
        shared = _silu(gu[:, :Is]) * gu[:, Is:] @ shared_down_w
        shared = shared * jax.nn.sigmoid(x @ shared_gate_w)
        logits = x @ gate_w
        probs = jax.nn.softmax(logits.astype(jnp.float32), axis=-1)
        w, idx = jax.lax.top_k(probs, TOP_K)
        w = (w / jnp.sum(w, axis=-1, keepdims=True)).astype(x.dtype)
        e_flat = idx.reshape(-1)
        w_flat = w.reshape(-1)
        A = e_flat.shape[0]
        tok = jnp.arange(A) // TOP_K
        onehot = jax.nn.one_hot(e_flat, E, dtype=jnp.int32)
        pos = jnp.take_along_axis(jnp.cumsum(onehot, axis=0) - 1, e_flat[:, None], axis=1)[:, 0]
        slot = jnp.minimum(pos, CAPACITY)
        buf = jnp.zeros((E, CAPACITY + 1, H), x.dtype).at[e_flat, slot].set(x[tok])
        gu_e = jnp.einsum('ech,ehf->ecf', buf, expert_gate_up_w)
        act = _silu(gu_e[..., :I]) * gu_e[..., I:]
        out_e = jnp.einsum('eci,eih->ech', act, expert_down_w)
        y = out_e[e_flat, slot] * w_flat[:, None]
        y = jnp.where((pos < CAPACITY)[:, None], y, jnp.zeros_like(y))
        y = y.reshape(T, TOP_K, H).sum(axis=1)
        return (y + shared).reshape(B, S, H)
    x = x + jnp.tanh(g_xattn[0]) * _L0_xattn_ref(_layernorm(x, axis=-1), ctx_1024, L0_xattn_Wq, L0_xattn_Wk, L0_xattn_Wv, L0_xattn_Wo, L0_xattn_bo)
    x = x + jnp.tanh(g_ffn[0]) * _L0_ffn_ref(_layernorm(x, axis=-1), L0_ffn_sim_matrix, L0_ffn_gates, L0_ffn_q_proj, L0_ffn_k_proj, L0_ffn_v_proj, L0_ffn_o_proj)
    x = x + jnp.tanh(g_xattn[1]) * _L1_xattn_ref(_layernorm(x, axis=-1), ctx_1024, ctx_1024, mask_BxS2_ik1)
    x = x + jnp.tanh(g_ffn[1]) * _L1_ffn_ref(_layernorm(x, axis=-1), L1_ffn_gate_w, L1_ffn_shared_gate_w, L1_ffn_shared_gate_up_w, L1_ffn_shared_down_w, L1_ffn_expert_gate_up_w, L1_ffn_expert_down_w)
    return x

_drawn_inputs = setup_inputs


def setup_inputs(seed=0):
    import zlib

    import numpy as np

    out = dict(_drawn_inputs(seed))
    spreads = {'g_ffn': (-1.0, 0.6), 'L0_ffn_gates': (0.0, 0.1)}
    factors = {'L1_ffn_gate_w': 5.544,
     'L1_ffn_shared_gate_w': 35.026,
     'L1_ffn_expert_gate_up_w': 5.272,
     'L1_ffn_expert_down_w': 5.264,
     'L1_ffn_shared_gate_up_w': 3.673,
     'L1_ffn_shared_down_w': 3.682}
    for name, (base, spread) in spreads.items():
        noise = np.random.default_rng([zlib.crc32(name.encode()), seed]).standard_normal(out[name].shape)
        drawn = base * np.exp(spread * noise) if base else spread * noise
        out[name] = jnp.asarray(drawn.astype(out[name].dtype))
    for name, factor in factors.items():
        out[name] = (out[name] * factor).astype(out[name].dtype)
    return out
```

```python
from contextlib import ExitStack

import concourse.bass as bass
from concourse import mybir

F32 = mybir.dt.float32
F16 = mybir.dt.float16
BF16 = mybir.dt.bfloat16
I32 = mybir.dt.int32
U32 = mybir.dt.uint32
ALU = mybir.AluOpType
ACT = mybir.ActivationFunctionType
AX = mybir.AxisListType

P = 128
SEQ = 64
BATCH = 16
TOKENS = SEQ * BATCH
TILES = TOKENS // P
HALVES = 2
TPH = TILES // HALVES
HT = TPH * P
HEADS = 16
HD = P // HEADS
PAIRS = HEADS // 2
E0 = 16
E1 = 64
EP = E1 // 2
CAP = 64
INNER = 64
SHARED = 256
GRP = 4
NGRP = EP // GRP
EPS = 1e-5
TINY = 1e-24
NEG = 1e10
BIG = 512.0
LOW = -3.0e38
LO_SCALE = 2048.0
NCONST = 12
NSEL = 5
GD, GD_EXP = 30, 18
CD, CD_EXP = 18, 9


def program(nc, d):
    ctx = ExitStack()
    with ctx:
        def sb(name, shape, dt=F32):
            return ctx.enter_context(nc.sbuf_tensor(name, shape, dt))

        def sem(name):
            return ctx.enter_context(nc.semaphore(name))

        xres = sb("xres", [P, TILES, P])
        hn = sb("hn", [P, TILES, P])
        hT = sb("hT", [P, TOKENS])
        ctxT = sb("ctxT", [P, TOKENS])
        ctxk2 = sb("ctxk2", [P, BATCH * P])
        ctxk = ctxk2[0:SEQ, :].rearrange("p (b c) -> p b c", b=BATCH)
        wq, wk, wv, wo = (sb(n, [P, P]) for n in ("wq", "wk", "wv", "wo"))
        bo = sb("bo", [P, P])
        gates4 = sb("gates4", [P, 4])
        tg = sb("tg", [P, 4])
        simm = sb("simm", [P, E0])
        sim2 = sb("sim2", [P, E0])
        gt0 = sb("gt0", [P, E0])
        sig0 = sb("sig0", [P, E0])
        maski = sb("maski", [P, TILES, SEQ], I32)
        maskfn = sb("maskfn", [P, 2 * TILES * SEQ])
        maskf = maskfn[:, 0:TILES * SEQ].rearrange("p (t k) -> p t k", t=TILES)
        maskn = maskfn[:, TILES * SEQ:].rearrange("p (t k) -> p t k", t=TILES)
        proj = sb("proj", [P, 4, E0, P])
        gw = sb("gw", [P, E1 + 1])
        sgu = sb("sgu", [P, 2 * SHARED])
        sdn = sb("sdn", [P, 2, P])
        big = sb("big", [P, TILES * EP * CAP * 2], F16)
        kexp = big[:, :].bitcast(F32).rearrange("p (b h k) -> p b h k", b=BATCH, h=HEADS)
        disp = big[:, :].rearrange("p (t q s) -> p t q s", t=TILES, q=EP)
        dispT = sb("dispT", [P, EP, TOKENS], F16)
        work = dispT[:, :, :].rearrange("p q n -> p (q n)").bitcast(F32)
        ident = sb("ident", [P, P])
        ident16 = sb("ident16", [P, P], F16)
        idlow16 = sb("idlow16", [P, P], F16)
        ones = sb("ones", [P, P])
        ones16 = sb("ones16", [P, P], F16)
        upper16 = sb("upper16", [P, P], F16)
        headm = sb("headm", [P, HEADS])
        halfm = sb("halfm", [P, 2])
        parity = sb("parity", [P, 2])
        selc = sb("selc", [3 * E0, E0])
        identb = sb("identb", [P, P], BF16)
        io16 = sb("io16", [P, E0])
        slotc = sb("slotc", [P, CAP, 2], F16)
        selw = sb("selw", [E0 * 3, E0, P], BF16)
        mhalf = sb("mhalf", [P, E0])

        banks = [ctx.enter_context(nc.psum_tensor(f"bank{i}", [P, 512], F32)) for i in range(8)]

        o = 0

        def take(n):
            nonlocal o
            o += n
            return work[:, o - n:o]
        qT = take(TOKENS)
        kT = take(TOKENS)
        vblk = take(BATCH * PAIRS * 18).rearrange("p (n h d) -> p n h d", h=2, d=9)
        prob = take(2 * HEADS * SEQ).rearrange("p (r n) -> p r n", r=2)
        probT = take(HEADS * SEQ)
        ohead = take(P)
        oheadT = take(P)
        rsum = take(HEADS)
        smax = take(2 * HEADS).rearrange("p (r h) -> p r h", r=2)
        assert o <= work.shape[1]
        o = 0
        z = take(2 * HT).rearrange("p (r n) -> p r n", r=2)
        qkvT = take(3 * HT).rearrange("p (r n) -> p r n", r=3)
        vk = take(8 * P).rearrange("p (b n) -> p b n", b=8)
        att = take(TPH * SEQ).rearrange("p (t k) -> p t k", t=TPH)
        attT = take(HT)
        oT = take(HT)
        accT = take(HT)
        room = proj[:, :, :, :].rearrange("p i e c -> p (i e c)")
        o = 0

        def take_c(n):
            nonlocal o
            o += n
            return room[:, o - n:o]
        xh = take_c(TILES * P).bitcast(F16).rearrange("p (t k c) -> p t k c", t=TILES, k=2)
        xeT = take_c(2 * GRP * P).rearrange("p (r q n) -> p r q n", r=2, q=GRP)
        eo = take_c(GRP * P)
        er = take_c(GRP * P)
        e3 = take_c(3 * GRP * P).bitcast(BF16).rearrange("p (r k q n) -> p r k q n", r=2, k=3, q=GRP)
        sth = take_c(HT)
        shg = take_c(2 * HT).rearrange("p (f n) -> p f n", f=2)
        yT = take_c(TOKENS)
        wc3 = take_c(TILES * E1 * 3 // 2).bitcast(BF16).rearrange("p (t e k) -> p t e k", t=TILES, k=3)
        assert o <= room.shape[1]
        stats = sb("stats", [P, TPH, 6])
        mv = sb("mv", [P, TILES, 2])
        ve = sb("ve", [P, TPH])
        rstd = sb("rstd", [P, TILES])
        sq = sb("sq", [P, P])
        ss = sb("ss", [P, TPH])
        rn = sb("rn", [P, TPH])
        lg = sb("lg", [P, TPH, E0])
        top = sb("top", [P, TPH, 8])
        topi = sb("topi", [P, TPH, 8], U32)
        topf = sb("topf", [P, TPH, 8])
        ga = sb("ga", [P, TPH, E0])
        gb = sb("gb", [P, TPH, E0])
        gc = sb("gc", [P, TPH, E0])
        fbk = sb("fbk", [P, TPH, E0])
        g1 = sb("g1", [P, TPH])
        g2 = sb("g2", [P, TPH])
        w3 = sb("w3", [P, TILES, 3 * E0], BF16)
        wT = sb("wT", [3 * E0, TOKENS], BF16)
        amax = sb("amax", [P, TPH])
        asum = sb("asum", [P, TPH])
        lgc = sb("lgc", [P, TILES, E1 + 1])
        rep = sb("rep", [P, TPH, E1])
        topc = sb("topc", [P, TPH, 8])
        chosen = sb("chosen", [P, TILES, E1], F16)
        wex = sb("wex", [P, TPH, E1])
        wres = sb("wres", [P, TPH, E1])
        csum = sb("csum", [P, TPH])
        post = sb("post", [P, TPH, E1])
        pos16 = sb("pos16", [P, TILES, E1], F16)
        sg = sb("sg", [P, TILES])
        wslot2 = sb("wslot2", [P, EP, 2])
        wslot = sb("wslot", [P, EP])
        gx = sb("gx", [P, 2, 2 * P], F16)
        th = sb("th", [P, GRP * CAP])
        ab = sb("ab", [P, GRP * CAP])
        actb = maskfn[:, :].rearrange("p (r q c e) -> p r q c e", r=2, q=GRP, c=CAP)
        wguR = ctxk2[:, :].rearrange("p (r e f) -> p r e f", r=2, e=2 * GRP)
        wdR = ctxT[:, :].rearrange("p (r q h) -> p r q h", r=2, q=GRP)

        ld = {n: sem("ld_" + n) for n in ("x", "ctxT", "wqkv", "misc", "mask", "ctxk", "proj", "gw", "shared")}
        ld_exp = [sem(f"ld_exp{i}") for i in range(2)]
        S = {}

        def s(name):
            if name not in S:
                S[name] = sem(name)
            return S[name]
        names = """consts ln_stats ln_aggr ln_var ln_rstd ln_out hT_ps hT_sb tanh_g
            kT_ps kT_sb v_ps v_sb kexp_d kexp_a kexp_p q_ps q_sb sc_ps sc_max sc_sub sc_exp pT_ps pT_sb pv_ps pv_rec
            pv_sb oT_ps oT_sb y_ps y_out xb
            sim2 sn_ps sn_pre sn g_act g_dve sq_sum rnorm lg_ps gd w3 wT_ps wT_sb wb_ps z_sb qkv_ps qkv_sb v2_ps v2_sb
            at_ps at_d at_exp at_sb aT_ps aT_sb ob_ps ob_sb acc_ps acc_sb tr_ps tr_out
            mask_f la_ps la_d la_exp lT_ps lT_sb lo_ps lo_out
            cl_ps cl_sb cd cexp ctanh pos_ps pos_sb disp xh_hi xh_r xh_lo dT_ps dT_sb dT_sbA ws_ps ws_sb ga_ps ga_sb xe_ps xe_sb
            up_ps up_th up_a up_act dn_ps dn_v dn_h1 dn_r1 dn_h2 dn_r2 sc_y yT_sb yt_ps
            sh_ps sh_th sh_a sh_act sd_ps sd_out fin out""".split()
        for n in names:
            s(n)

        block = ctx.enter_context(nc.Block())

        def seq(b):
            return slice(b * SEQ, (b + 1) * SEQ)

        def half(h):
            return slice(h * HT, (h + 1) * HT)

        def tile(t):
            return slice(t * P, (t + 1) * P)

        @block.sync
        def _(sp):
            sp.dma_start(ctxT[:, :], d["ctxT"]).then_inc(ld["ctxT"], 16)
            sp.dma_start(wk[:, :], d["WkT"]).then_inc(ld["wqkv"], 16)
            sp.dma_start(wv[:, :], d["WvT"]).then_inc(ld["wqkv"], 16)
            sp.dma_start(xres[:, :, :], d["x"].rearrange("(t p) c -> p t c", p=P)).then_inc(ld["x"], 16)
            sp.dma_start(wq[:, :], d["WqT"]).then_inc(ld["wqkv"], 16)
            sp.dma_start(wo[:, :], d["WoT"]).then_inc(ld["wqkv"], 16)
            sp.dma_start(bo[:, :], d["bo"].partition_broadcast(P)).then_inc(ld["misc"], 16)
            sp.dma_start(gates4[:, 0:2], d["g_xattn"].partition_broadcast(P)).then_inc(ld["misc"], 16)
            sp.dma_start(gates4[:, 2:4], d["g_ffn"].partition_broadcast(P)).then_inc(ld["misc"], 16)
            sp.dma_start(gt0[:, :], d["gates"].partition_broadcast(P)).then_inc(ld["misc"], 16)
            sp.dma_start(simm[:, :], d["sim"]).then_inc(ld["misc"], 16)
            for i, n in enumerate(("q", "k", "v", "o")):
                sp.dma_start(proj[:, i, :, :], d[n + "_proj"].rearrange("e c h -> c e h")).then_inc(ld["proj"], 16)
            m = d["mask"].rearrange("(t b) k -> b t k", b=2)
            for b in range(2):
                sp.dma_start(maski[seq(b), :, :], m[b].partition_broadcast(SEQ)).then_inc(ld["mask"], 16)
            sp.dma_start(ctxk[:, :, :], d["ctx"].rearrange("(b k) c -> k b c", k=SEQ)).then_inc(ld["ctxk"], 16)
            sp.dma_start(gw[:, 0:E1], d["gate_w"]).then_inc(ld["gw"], 16)
            sp.dma_start(gw[:, E1:E1 + 1], d["sgate_w"]).then_inc(ld["gw"], 16)
            sp.dma_start(sgu[:, :], d["sgu"]).then_inc(ld["shared"], 16)
            sp.dma_start(sdn[:, :, :], d["sdn"].rearrange("(f p) h -> p f h", p=P)).then_inc(ld["shared"], 16)
            sp.wait_ge(s("lo_ps"), 2)
            for g in range(NGRP):
                if g >= 2:
                    sp.wait_ge(s("up_ps"), g - 1)
                    sp.wait_ge(s("dn_ps"), g - 1)
                sp.dma_start(wguR[:, g % 2, :, :], d["egu"][2 * GRP * g:2 * GRP * (g + 1)]
                             .rearrange("e c f -> c e f")).then_inc(ld_exp[g % 2], 16)
                sp.dma_start(wdR[:, g % 2, :, :], d["edn"][2 * GRP * g:2 * GRP * (g + 1)]
                             .rearrange("(q e) i h -> (e i) q h", e=2)).then_inc(ld_exp[g % 2], 16)
            for h in range(HALVES):
                sp.wait_ge(s("fin"), TPH * (h + 1))
                sp.dma_start(d["out"][half(h), :].rearrange("(t p) c -> p t c", p=P),
                             xres[:, TPH * h:TPH * (h + 1), :]).then_inc(s("out"), 16)
            sp.wait_ge(s("out"), 16 * HALVES)

        @block.gpsimd
        def _(pool):
            done = [0]

            def const(ins):
                ins.then_inc(s("consts"), 1)
                done[0] += 1

            def settle():
                pool.wait_ge(s("consts"), done[0])
            for x, v in ((ident, 0.0), (ones, 1.0), (ones16, 1.0), (upper16, 1.0), (mhalf, -0.5)):
                const(nc.gpsimd.memset(x[:, :], v))
            const(nc.gpsimd.iota(slotc[:, :, :], [[1, CAP], [0, 2]], base=0, channel_multiplier=0,
                                 allow_small_or_imprecise_dtypes=True))
            const(nc.gpsimd.iota(io16[:, :], [[1, E0]], base=0, channel_multiplier=0,
                                 allow_small_or_imprecise_dtypes=True))
            settle()
            const(nc.gpsimd.affine_select(out=ident[:, :], in_=ident[:, :], compare_op=ALU.not_equal, fill=1.0,
                                          base=0, pattern=[[-1, P]], channel_multiplier=1))
            const(nc.gpsimd.affine_select(out=upper16[:, :], in_=upper16[:, :], compare_op=ALU.is_gt, fill=0.0,
                                          base=0, pattern=[[1, P]], channel_multiplier=-1))
            settle()
            const(nc.gpsimd.tensor_copy(ident16[:, :], ident[:, :]))
            const(nc.gpsimd.tensor_copy(identb[:, :], ident[:, :]))
            const(nc.gpsimd.tensor_scalar(idlow16[:, :], ident[:, :], 1.0 / LO_SCALE, None, ALU.mult))
            assert done[0] == NCONST, done[0]

            pool.wait_ge(s("sel"), NSEL)
            for h in range(HALVES):
                pool.wait_ge(s("kT_sb"), h + 1)
                for hd in range(2, HEADS, 3):
                    nc.gpsimd.tensor_scalar(kexp[:, 8 * h:8 * h + 8, hd, :],
                                            kT[:, half(h)].rearrange("p (b k) -> p b k", k=SEQ),
                                            headm[:, hd:hd + 1], None, ALU.mult).then_inc(s("kexp_p"), 1)

            def rsqrt_ln(n):
                h = n % 2
                if n:
                    pool.wait_ge(s("ln_rstd"), n)
                pool.wait_ge(s("ln_aggr"), TPH * (n + 1))
                nc.gpsimd.tensor_scalar(ve[:, :], mv[:, TPH * h:TPH * (h + 1), 1], EPS, None,
                                        ALU.add).then_inc(s("ln_var"), 1)
                pool.wait_ge(s("ln_var"), n + 1)
                nc.gpsimd.tensor_tensor(rstd[:, TPH * h:TPH * (h + 1)], ve[:, :], mhalf[:, 0:TPH],
                                        ALU.pow).then_inc(s("ln_rstd"), 1)
            rsqrt_ln(0)
            rsqrt_ln(1)
            pool.wait_ge(s("sn_pre"), 1)
            nc.gpsimd.tensor_tensor(sim2[:, :], sim2[:, :], mhalf[:, :], ALU.pow).then_inc(s("sn_pre"), 1)
            pool.wait_ge(s("sn_pre"), 2)
            nc.gpsimd.tensor_tensor(simm[:, :], simm[:, :], sim2[:, :], ALU.mult).then_inc(s("sn"), 1)
            for h in range(HALVES):
                rsqrt_ln(2 + h)
                pool.wait_ge(s("sq_sum"), TPH * (h + 1))
                nc.gpsimd.tensor_scalar(rn[:, :], ss[:, :], TINY, None, ALU.max).then_inc(s("rnorm"), 1)
                pool.wait_ge(s("rnorm"), 2 * h + 1)
                nc.gpsimd.tensor_tensor(rn[:, :], rn[:, :], mhalf[:, 0:TPH], ALU.pow).then_inc(s("rnorm"), 1)
            for n in range(4, 8):
                rsqrt_ln(n)

        @block.scalar
        def _(act):
            A = nc.scalar.activation

            def copy(out, in_):
                return A(out, in_, ACT.Copy)

            act.wait_ge(ld["misc"], 5 * 16)
            A(tg[:, :], gates4[:, :], ACT.Tanh).then_inc(s("tanh_g"), 1)
            A(sig0[:, :], gt0[:, :], ACT.Tanh, scale=0.5).then_inc(s("g_act"), 1)

            for h in range(HALVES):
                act.wait_ge(s("kT_ps"), h + 1)
                copy(kT[:, half(h)], banks[h][:, :]).then_inc(s("kT_sb"), 1)
            act.wait_ge(s("sel"), NSEL)
            act.wait_ge(s("kT_sb"), 2)
            for h in range(HALVES):
                for hd in range(1, HEADS, 3):
                    A(kexp[:, 8 * h:8 * h + 8, hd, :], kT[:, half(h)].rearrange("p (b k) -> p b k", k=SEQ),
                      ACT.Copy, scale=headm[:, hd:hd + 1]).then_inc(s("kexp_a"), 1)
                act.wait_ge(s("hT_ps"), h + 1)
                copy(hT[:, half(h)], banks[6 + h][:, :]).then_inc(s("hT_sb"), 1)
                act.wait_ge(s("q_ps"), h + 1)
                copy(qT[:, half(h)], banks[h][:, :]).then_inc(s("q_sb"), 1)

            def a_exp(t):
                act.wait_ge(s("sc_sub"), t + 1)
                if t >= 2:
                    act.wait_ge(s("pT_ps"), t - 1)
                A(prob[:, t % 2, :], prob[:, t % 2, :], ACT.Exp, scale=float(P) ** -0.5).then_inc(s("sc_exp"), 1)

            def a_pT(t):
                act.wait_ge(s("pT_ps"), t + 1)
                if t >= 1:
                    act.wait_ge(s("pv_ps"), t)
                for k in range(2):
                    copy(probT[:, 512 * k:512 * (k + 1)], banks[4 + k][:, :]).then_inc(s("pT_sb"), 1)

            def a_oT(t):
                act.wait_ge(s("oT_ps"), t + 1)
                if t >= 1:
                    act.wait_ge(s("y_ps"), t)
                copy(oheadT[:, :], banks[7][:, 0:P]).then_inc(s("oT_sb"), 1)
            for t in range(TILES + 2):
                if 1 <= t <= TILES:
                    a_exp(t - 1)
                    a_pT(t - 1)
                if t >= 2:
                    a_oT(t - 2)

            def ln_T(n):
                act.wait_ge(s("hT_ps"), n + 1)
                copy(hT[:, half(n % 2)], banks[2 + 3 * (n % 2)][:, :]).then_inc(s("hT_sb"), 1)

            def gate(h):
                act.wait_ge(s("ln_out"), TPH * (3 + h))
                for t in range(TPH):
                    if h or t:
                        act.wait_ge(s("sq_sum"), h * TPH + t)
                    if h and t == 0:
                        act.wait_ge(s("rnorm"), 2 * h)
                    A(sq[:, :], hn[:, TPH * h + t, :], ACT.Square,
                      accum_out=ss[:, t:t + 1]).then_inc(s("sq_sum"), 1)
                ln_T(2 + h)
                act.wait_ge(s("gd"), GD * h + GD_EXP)
                A(gc[:, :, :], gc[:, :, :], ACT.Exp).then_inc(s("g_act"), 1)
                act.wait_ge(s("wT_ps"), h + 1)
                copy(wT[:, half(h)], banks[3 + 3 * h][0:3 * E0, 0:HT // 2].bitcast(BF16)).then_inc(s("wT_sb"), 1)

            def qkv(h):
                act.wait_ge(s("zuse"), 2 * E0 * h + E0)
                if h:
                    act.wait_ge(s("v2_ps"), h)
                    act.wait_ge(s("at_ps"), h)
                for i in range(3):
                    copy(qkvT[:, i, :], banks[2 + 3 * h + i][:, :]).then_inc(s("qkv_sb"), 1)

            def attn(h):
                act.wait_ge(s("v2_ps"), h + 1)
                for i in range(2):
                    copy(vk[0:SEQ, 4 * i:4 * i + 4, :].rearrange("p b n -> p (b n)"),
                         banks[2 + 3 * h + i][0:SEQ, :]).then_inc(s("v2_sb"), 1)
                act.wait_ge(s("at_d"), 5 * h + 2)
                A(att[:, :, :], att[:, :, :], ACT.Exp, scale=float(P) ** -0.5).then_inc(s("at_exp"), 1)
                act.wait_ge(s("aT_ps"), h + 1)
                copy(attT[0:SEQ, :], banks[4 + 3 * h][0:SEQ, :]).then_inc(s("aT_sb"), 1)
                act.wait_ge(s("ob_ps"), h + 1)
                copy(oT[:, :], banks[2 + 3 * h][:, :]).then_inc(s("ob_sb"), 1)

            def outp(h):
                act.wait_ge(s("zuse"), 2 * E0 * (h + 1))
                copy(accT[:, :], banks[3 + 3 * h][:, :]).then_inc(s("acc_sb"), 1)

            gate(0)
            gate(1)
            for h in range(HALVES):
                qkv(h)
                attn(h)
                outp(h)
            for h in range(HALVES):
                ln_T(4 + h)
                act.wait_ge(s("la_d"), 5 * h + 4)
                A(att[:, :, :], att[:, :, :], ACT.Exp).then_inc(s("la_exp"), 1)
                act.wait_ge(s("lT_ps"), h + 1)
                copy(attT[0:SEQ, :], banks[3 + 3 * h][0:SEQ, :]).then_inc(s("lT_sb"), 1)
            for h in range(HALVES):
                ln_T(6 + h)
                act.wait_ge(s("cl_sb"), 2 * h + 1)
                A(sg[:, TPH * h:TPH * (h + 1)], lgc[:, TPH * h:TPH * (h + 1), E1], ACT.Tanh,
                  scale=0.5).then_inc(s("ctanh"), 1)
                act.wait_ge(s("cd"), CD * h + CD_EXP)
                A(wex[:, :, :], wex[:, :, :], ACT.Exp).then_inc(s("cexp"), 1)
                act.wait_ge(s("xh_r"), TPH * (h + 1))
                A(xh[:, TPH * h:TPH * (h + 1), 1, :], hn[:, TPH * h:TPH * (h + 1), :], ACT.Copy,
                  scale=LO_SCALE).then_inc(s("xh_lo"), 1)
            for k in range(2 * HALVES):
                act.wait_ge(s("sh_ps"), k + 1)
                if k:
                    act.wait_ge(s("sh_a"), k)
                A(sth[:, :], banks[4 * (k % 2)][:, :], ACT.Tanh, scale=0.5).then_inc(s("sh_th"), 1)
            for n in range(TILES * EP // 8):
                if n % 2:
                    act.wait_ge(s("dT_ps"), n + 1)
                    t, q = n // (EP // 8), n % (EP // 8)
                    copy(dispT[:, 8 * q:8 * q + 8, tile(t)],
                         banks[n % 2][:, :].bitcast(F16).rearrange("p (q n) -> p q n", q=8)).then_inc(s("dT_sbA"), 1)
            for g in range(NGRP):
                for q in range(GRP):
                    n = g * GRP + q
                    act.wait_ge(s("ga_ps"), n + 1)
                    if n >= 2:
                        act.wait_ge(s("xe_ps"), n - 1)
                    copy(gx[:, n % 2, :], banks[n % 2][:, 0:2 * P]).then_inc(s("ga_sb"), 1)
                act.wait_ge(s("xe_ps"), GRP * (g + 1))
                if g >= 2:
                    act.wait_ge(s("up_ps"), g - 1)
                copy(xeT[:, g % 2, :, :].rearrange("p q n -> p (q n)"), banks[2][:, :]).then_inc(s("xe_sb"), 1)
                act.wait_ge(s("up_ps"), g + 1)
                if g:
                    act.wait_ge(s("up_a"), g)
                A(th[:, :], banks[3][:, 0:256], ACT.Tanh, scale=0.5).then_inc(s("up_th"), 1)
            for h in range(HALVES):
                act.wait_ge(s("sc_g"), NGRP)
                copy(yT[:, half(h)], banks[5 + h][:, :]).then_inc(s("yT_sb"), 1)

        @block.vector
        def _(dve):
            V = nc.vector

            def ln(n):
                h = n % 2
                if n:
                    dve.wait_ge(s("ln_aggr"), TPH * n)
                for t in range(TPH):
                    V.bn_stats(stats[:, t, :], xres[:, TPH * h + t, :]).then_inc(s("ln_stats"), 1)
                for t in range(TPH):
                    dve.wait_ge(s("ln_stats"), TPH * n + t + 1)
                    V.bn_aggr(mv[:, TPH * h + t, :], stats[:, t, :]).then_inc(s("ln_aggr"), 1)

            def ln_apply(n):
                h = n % 2
                dve.wait_ge(s("ln_rstd"), n + 1)
                if n >= 2:
                    dve.wait_ge(s("hT_ps"), n - 1)
                for t in range(TPH * h, TPH * (h + 1)):
                    V.tensor_scalar(hn[:, t, :], xres[:, t, :], mv[:, t, 0:1], rstd[:, t:t + 1],
                                    ALU.subtract, ALU.mult).then_inc(s("ln_out"), 1)

            dve.wait_ge(s("consts"), NCONST)
            for out, eye in ((headm[:, :], ident[:, :].rearrange("p (h d) -> p h d", d=HD)),
                             (halfm[:, :], ident[:, :].rearrange("p (h d) -> p h d", h=2)),
                             (parity[:, :], ident[:, :].rearrange("p (c e) -> p e c", e=2)),
                             (selc[:, :], ident[0:3 * E0, 0:3 * E0].rearrange("p (k e) -> p e k", e=E0))):
                V.tensor_reduce(out, eye, AX.X, ALU.add).then_inc(s("sel"), 1)
            dve.wait_ge(s("sel"), 4)
            V.tensor_copy(selw[:, :, :], selc[:, :, None].to_broadcast([3 * E0, E0, P])).then_inc(s("sel"), 1)
            dve.wait_ge(ld["x"], 16)
            ln(0)
            ln(1)
            dve.wait_ge(s("kT_sb"), 1)
            for h in range(HALVES):
                dve.wait_ge(s("kT_sb"), h + 1)
                for hd in range(0, HEADS, 3):
                    V.tensor_scalar(kexp[:, 8 * h:8 * h + 8, hd, :],
                                    kT[:, half(h)].rearrange("p (b k) -> p b k", k=SEQ),
                                    headm[:, hd:hd + 1], None, ALU.mult).then_inc(s("kexp_d"), 1)
                if h == 0:
                    ln_apply(0)
                    ln_apply(1)
            V.tensor_copy(vblk[:, :, :, 8], halfm[:, None, :].to_broadcast([P, BATCH * PAIRS, 2])).then_inc(s("v_sb"), 1)
            for k in range(4):
                dve.wait_ge(s("v_ps"), k + 1)
                for i in range(2):
                    V.tensor_scalar(vblk[:, 32 * k:32 * k + 32, i, 0:HD],
                                    banks[2 + k][:, :].rearrange("p (n h d) -> p n h d", h=2, d=HD)[:, :, i, :],
                                    halfm[:, i:i + 1], None, ALU.mult).then_inc(s("v_sb"), 1)
            dve.wait_ge(s("tanh_g"), 1)
            V.tensor_scalar(bo[:, :], bo[:, :], tg[:, 0:1], None, ALU.mult).then_inc(s("xb"), 1)
            dve.wait_ge(s("xb"), 1)
            V.tensor_tensor(xres[:, :, :], xres[:, :, :], bo[:, None, :].to_broadcast([P, TILES, P]),
                            ALU.add).then_inc(s("xb"), 1)
            dve.wait_ge(ld["misc"], 5 * 16)
            V.tensor_tensor(sim2[:, :], simm[:, :], simm[:, :], ALU.mult).then_inc(s("sim2"), 1)
            dve.wait_ge(s("g_act"), 1)
            V.tensor_scalar(sig0[:, :], sig0[:, :], 0.5, 0.5, ALU.mult, ALU.add).then_inc(s("g_dve"), 1)

            def a_soft(t):
                b = 2 * (t % 2)
                if t >= 2:
                    dve.wait_ge(s("pT_ps"), t - 1)
                    dve.wait_ge(s("sc_sub"), t - 1)
                for k in range(2):
                    dve.wait_ge(s("sc_ps"), t + 1)
                    V.tensor_reduce(smax[:, t % 2, 8 * k:8 * k + 8], banks[b + k][:, :].rearrange("p (h k) -> p h k", k=SEQ),
                                    AX.X, ALU.max).then_inc(s("sc_max"), 1)
                for k in range(2):
                    dve.wait_ge(s("sc_max"), 2 * t + 1 + k)
                    ins = V.tensor_tensor(prob[:, t % 2, 512 * k:512 * (k + 1)].rearrange("p (h k) -> p h k", k=SEQ),
                                          banks[b + k][:, :].rearrange("p (h k) -> p h k", k=SEQ),
                                          smax[:, t % 2, 8 * k:8 * k + 8, None].to_broadcast([P, 8, SEQ]), ALU.subtract)
                    if k:
                        ins.then_inc(s("sc_sub"), 1)

            def a_norm(t):
                dve.wait_ge(s("pv_ps"), t + 1)
                po = banks[6][:, 0:HEADS * 9].rearrange("p (h d) -> p h d", d=9)
                if t:
                    dve.wait_ge(s("pv_sb"), t)
                V.reciprocal(rsum[:, :], po[:, :, 8]).then_inc(s("pv_rec"), 1)
                dve.wait_ge(s("pv_rec"), t + 1)
                if t >= 1:
                    dve.wait_ge(s("oT_ps"), t)
                V.tensor_tensor(ohead[:, :].rearrange("p (h d) -> p h d", d=HD), po[:, :, 0:HD],
                                rsum[:, :, None].to_broadcast([P, HEADS, HD]), ALU.mult).then_inc(s("pv_sb"), 1)

            def a_res(t):
                dve.wait_ge(s("y_ps"), t + 1)
                dve.wait_ge(s("xb"), 2)
                V.scalar_tensor_tensor(xres[:, t, :], banks[7][:, P:2 * P], tg[:, 0:1], xres[:, t, :],
                                       ALU.mult, ALU.add).then_inc(s("y_out"), 1)
            for t in range(TILES + 2):
                if t < TILES:
                    a_soft(t)
                if 1 <= t <= TILES:
                    a_norm(t - 1)
                if t >= 2:
                    a_res(t - 2)
                if t == 0:
                    dve.wait_ge(s("sn_ps"), 1)
                    V.tensor_scalar(sim2[:, :], banks[7][:, 256:256 + E0], TINY, None, ALU.max).then_inc(s("sn_pre"), 1)

            gdn = [0]

            def gstep(ins):
                ins.then_inc(s("gd"), 1)
                gdn[0] += 1
                return gdn[0]

            def gate(h):
                b3 = banks[4 + 3 * h]
                dve.wait_ge(s("y_out"), TPH * (h + 1))
                ln(2 + h)
                ln_apply(2 + h)
                dve.wait_ge(s("rnorm"), 2 * h + 2)
                dve.wait_ge(s("lg_ps"), h + 1)
                dve.wait_ge(s("g_dve"), 1)
                if h:
                    dve.wait_ge(s("gd"), GD * h)
                for t in range(TPH):
                    gstep(V.scalar_tensor_tensor(lg[:, t, :], b3[:, E0 * t:E0 * (t + 1)], rn[:, t:t + 1], sig0[:, :],
                                                 ALU.mult, ALU.subtract))
                dve.wait_ge(s("gd"), gdn[0])
                for t in range(TPH):
                    gstep(V.max(top[:, t, :], lg[:, t, :]))
                gstep(V.tensor_scalar(ga[:, :, :], lg[:, :, :], 0.0, None, ALU.is_gt))
                gstep(V.tensor_scalar(gb[:, :, :], lg[:, :, :], 0.0, None, ALU.max))
                dve.wait_ge(s("gd"), gdn[0])
                for t in range(TPH):
                    gstep(V.max_index(topi[:, t, :], top[:, t, :], lg[:, t, :]))
                gstep(V.tensor_scalar(g1[:, :], top[:, :, 0], 0.0, None, ALU.is_le))
                gstep(V.tensor_scalar(g2[:, :], top[:, :, 0], 0.0, None, ALU.max))
                dve.wait_ge(s("gd"), gdn[0])
                gstep(V.tensor_copy(topf[:, :, :], topi[:, :, :]))
                gstep(V.tensor_tensor(gc[:, :, :], gb[:, :, :], g2[:, :, None].to_broadcast([P, TPH, E0]),
                                      ALU.subtract))
                assert gdn[0] == GD * h + GD_EXP
                dve.wait_ge(s("gd"), gdn[0])
                gstep(V.tensor_tensor(gb[:, :, :], io16[:, None, :].to_broadcast([P, TPH, E0]),
                                      topf[:, :, 0:1].to_broadcast([P, TPH, E0]), ALU.is_equal))
                gstep(V.tensor_tensor(fbk[:, :, :], io16[:, None, :].to_broadcast([P, TPH, E0]),
                                      topf[:, :, 1:2].to_broadcast([P, TPH, E0]), ALU.is_equal))
                dve.wait_ge(s("gd"), gdn[0])
                gstep(V.tensor_tensor(gb[:, :, :], gb[:, :, :], fbk[:, :, :], ALU.add))
                dve.wait_ge(s("gd"), gdn[0])
                gstep(V.tensor_tensor(gb[:, :, :], gb[:, :, :], g1[:, :, None].to_broadcast([P, TPH, E0]), ALU.mult))
                dve.wait_ge(s("gd"), gdn[0])
                gstep(V.tensor_tensor(gb[:, :, :], gb[:, :, :], ga[:, :, :], ALU.add))
                dve.wait_ge(s("gd"), gdn[0])
                dve.wait_ge(s("g_act"), 2 + h)
                gstep(V.tensor_tensor(gb[:, :, :], gb[:, :, :], gc[:, :, :], ALU.mult))
                dve.wait_ge(s("gd"), gdn[0])
                gstep(V.tensor_reduce(g1[:, :], gb[:, :, :], AX.X, ALU.add))
                dve.wait_ge(s("gd"), gdn[0])
                gstep(V.reciprocal(g2[:, :], g1[:, :]))
                dve.wait_ge(s("gd"), gdn[0])
                gstep(V.tensor_tensor(gb[:, :, :], gb[:, :, :], g2[:, :, None].to_broadcast([P, TPH, E0]), ALU.mult))
                part = [w3[:, TPH * h:TPH * (h + 1), i * E0:(i + 1) * E0] for i in range(3)]
                dve.wait_ge(s("gd"), gdn[0])
                gstep(V.tensor_copy(part[0], gb[:, :, :]))
                dve.wait_ge(s("gd"), gdn[0])
                gstep(V.tensor_tensor(gb[:, :, :], gb[:, :, :], part[0], ALU.subtract))
                dve.wait_ge(s("gd"), gdn[0])
                gstep(V.tensor_copy(part[1], gb[:, :, :]))
                dve.wait_ge(s("gd"), gdn[0])
                V.tensor_tensor(part[2], gb[:, :, :], part[1], ALU.subtract).then_inc(s("w3"), 1)
                assert gdn[0] == GD * (h + 1), gdn[0]

            def scaled(n, src):
                dve.wait_ge(s("wb_ps"), n + 1)
                if n >= 2:
                    dve.wait_ge(s("zuse"), n - 1)
                V.tensor_tensor(z[:, n % 2, :], banks[n % 2][:, :], src, ALU.mult).then_inc(s("z_sb"), 1)

            def attn(h):
                b = banks[4 + 3 * h]
                a = b[:, 0:TPH * SEQ].rearrange("p (t k) -> p t k", k=SEQ)
                n = 5 * h
                dve.wait_ge(s("at_ps"), h + 1)
                if h:
                    dve.wait_ge(s("at_d"), n)
                V.tensor_reduce(amax[:, :], a, AX.X, ALU.max).then_inc(s("at_d"), 1)
                dve.wait_ge(s("at_d"), n + 1)
                if h:
                    dve.wait_ge(s("aT_ps"), h)
                V.tensor_tensor(att[:, :, :], a, amax[:, :, None].to_broadcast([P, TPH, SEQ]),
                                ALU.subtract).then_inc(s("at_d"), 1)
                dve.wait_ge(s("at_exp"), h + 1)
                V.tensor_reduce(asum[:, :], att[:, :, :], AX.X, ALU.add).then_inc(s("at_d"), 1)
                dve.wait_ge(s("at_d"), n + 3)
                V.reciprocal(amax[:, :], asum[:, :]).then_inc(s("at_d"), 1)
                dve.wait_ge(s("at_d"), n + 4)
                V.tensor_tensor(att[:, :, :], att[:, :, :], amax[:, :, None].to_broadcast([P, TPH, SEQ]),
                                ALU.mult).then_inc(s("at_d"), 1)

            def residual(h, bank, gate_col, done):
                for t in range(TPH):
                    V.scalar_tensor_tensor(xres[:, TPH * h + t, :], bank[:, tile(t)], tg[:, gate_col:gate_col + 1],
                                           xres[:, TPH * h + t, :], ALU.mult, ALU.add).then_inc(done, 1)

            gate(0)
            gate(1)
            dve.wait_ge(ld["mask"], 32)
            V.tensor_copy(maskf[:, :, :], maski[:, :, :]).then_inc(s("mask_f"), 1)
            dve.wait_ge(s("mask_f"), 1)
            V.tensor_scalar(maskf[:, :, :], maskf[:, :, :], 0.0, None, ALU.not_equal).then_inc(s("mask_f"), 1)
            dve.wait_ge(s("mask_f"), 2)
            V.tensor_scalar(maskn[:, :, :], maskf[:, :, :], -1.0, NEG, ALU.add, ALU.mult).then_inc(s("mask_f"), 1)
            n = 0
            for h in range(HALVES):
                for e in range(E0):
                    if e == 0:
                        dve.wait_ge(s("hT_sb"), 3 + h)
                    scaled(n, hT[:, half(h)])
                    n += 1
                attn(h)
                dve.wait_ge(s("ob_sb"), h + 1)
                for e in range(E0):
                    scaled(n, oT[:, :])
                    n += 1
                dve.wait_ge(s("tr_ps"), h + 1)
                residual(h, banks[4 + 3 * h], 2, s("tr_out"))
            for h in range(HALVES):
                dve.wait_ge(s("tr_out"), TPH * (h + 1))
                ln(4 + h)
                ln_apply(4 + h)
                n = 5 * h
                b = banks[4 + 3 * h]
                a = b[:, 0:TPH * SEQ].rearrange("p (t k) -> p t k", k=SEQ)
                ts = slice(TPH * h, TPH * (h + 1))
                dve.wait_ge(s("la_ps"), h + 1)
                dve.wait_ge(s("mask_f"), 3)
                if h:
                    dve.wait_ge(s("lT_ps"), h)
                V.tensor_tensor(att[:, :, :], a, maskf[:, ts, :], ALU.mult).then_inc(s("la_d"), 1)
                dve.wait_ge(s("la_d"), n + 1)
                V.tensor_tensor(att[:, :, :], att[:, :, :], maskn[:, ts, :], ALU.add).then_inc(s("la_d"), 1)
                dve.wait_ge(s("la_d"), n + 2)
                V.tensor_reduce(amax[:, :], att[:, :, :], AX.X, ALU.max).then_inc(s("la_d"), 1)
                dve.wait_ge(s("la_d"), n + 3)
                V.tensor_tensor(att[:, :, :], att[:, :, :], amax[:, :, None].to_broadcast([P, TPH, SEQ]),
                                ALU.subtract).then_inc(s("la_d"), 1)
                dve.wait_ge(s("la_exp"), h + 1)
                V.tensor_reduce(asum[:, :], att[:, :, :], AX.X, ALU.add).then_inc(s("la_d"), 1)
                dve.wait_ge(s("la_d"), n + 5)
                V.reciprocal(amax[:, :], asum[:, :]).then_inc(s("lrec"), 1)
                dve.wait_ge(s("lrec"), 2 * h + 1)
                V.tensor_scalar(asum[:, :], amax[:, :], tg[:, 1:2], None, ALU.mult).then_inc(s("lrec"), 1)
                dve.wait_ge(s("lrec"), 2 * h + 2)
                dve.wait_ge(s("lo_ps"), h + 1)
                for t in range(TPH):
                    V.scalar_tensor_tensor(xres[:, TPH * h + t, :], banks[2 + 3 * h][:, tile(t)], asum[:, t:t + 1],
                                           xres[:, TPH * h + t, :], ALU.mult, ALU.add).then_inc(s("lo_out"), 1)
            cdn = [0]

            def cstep(ins):
                ins.then_inc(s("cd"), 1)
                cdn[0] += 1

            def cwait():
                dve.wait_ge(s("cd"), cdn[0])
            for h in range(HALVES):
                ts = slice(TPH * h, TPH * (h + 1))
                dve.wait_ge(s("lo_out"), TPH * (h + 1))
                ln(6 + h)
                ln_apply(6 + h)
                dve.wait_ge(s("cl_ps"), h + 1)
                V.tensor_copy(lgc[:, ts, :], banks[3 + 3 * h][:, 0:TPH * (E1 + 1)]
                              .rearrange("p (t e) -> p t e", t=TPH)).then_inc(s("cl_sb"), 1)
                dve.wait_ge(s("cl_sb"), 2 * h + 1)
                cwait()
                for t in range(TPH):
                    cstep(V.max(topc[:, t, :], lgc[:, TPH * h + t, 0:E1]))
                cwait()
                for t in range(TPH):
                    cstep(V.match_replace(rep[:, t, :], topc[:, t, :], lgc[:, TPH * h + t, 0:E1], LOW))
                cstep(V.tensor_tensor(wex[:, :, :], lgc[:, ts, 0:E1], topc[:, :, 0:1].to_broadcast([P, TPH, E1]),
                                      ALU.subtract))
                assert cdn[0] == CD * h + CD_EXP
                cwait()
                V.tensor_tensor(chosen[:, ts, :], rep[:, :, :], lgc[:, ts, 0:E1],
                                ALU.not_equal).then_inc(s("cl_sb"), 1)
                V.tensor_copy(xh[:, ts, 0, :], hn[:, ts, :]).then_inc(s("xh_hi"), 1)
                dve.wait_ge(s("xh_hi"), h + 1)
                dve.wait_ge(s("hT_ps"), 7 + h)
                for t in range(TPH * h, TPH * (h + 1)):
                    V.tensor_tensor(hn[:, t, :], hn[:, t, :], xh[:, t, 0, :], ALU.subtract).then_inc(s("xh_r"), 1)
                dve.wait_ge(s("cl_sb"), 2 * h + 2)
                dve.wait_ge(s("cexp"), h + 1)
                cstep(V.tensor_tensor(wex[:, :, :], wex[:, :, :], chosen[:, ts, :], ALU.mult))
                cwait()
                cstep(V.tensor_reduce(csum[:, :], wex[:, :, :], AX.X, ALU.add))
                cwait()
                cstep(V.reciprocal(g1[:, :], csum[:, :]))
                cwait()
                cstep(V.tensor_tensor(wex[:, :, :], wex[:, :, :], g1[:, :, None].to_broadcast([P, TPH, E1]), ALU.mult))
                cwait()
                cstep(V.tensor_copy(wc3[:, ts, :, 0], wex[:, :, :]))
                cwait()
                cstep(V.tensor_tensor(wres[:, :, :], wex[:, :, :], wc3[:, ts, :, 0], ALU.subtract))
                cwait()
                cstep(V.tensor_copy(wc3[:, ts, :, 1], wres[:, :, :]))
                cwait()
                cstep(V.tensor_tensor(wc3[:, ts, :, 2], wres[:, :, :], wc3[:, ts, :, 1], ALU.subtract))
                dve.wait_ge(s("pos_ps"), h + 1)
                cstep(V.scalar_tensor_tensor(post[:, :, :], chosen[:, ts, :], -BIG,
                                             banks[4 + 3 * h][:, 0:TPH * E1].rearrange("p (t e) -> p t e", t=TPH),
                                             ALU.mult, ALU.add))
                cwait()
                V.tensor_scalar(pos16[:, ts, :], post[:, :, :], BIG, float(2 * CAP), ALU.add,
                                ALU.min).then_inc(s("pos_sb"), 1)
                dve.wait_ge(s("pos_sb"), h + 1)
                for t in range(TPH * h, TPH * (h + 1)):
                    V.tensor_tensor(disp[:, t, :, :].rearrange("p q (c e) -> p q c e", e=2),
                                    slotc[:, None, :, :].to_broadcast([P, EP, CAP, 2]),
                                    pos16[:, t, :].rearrange("p (q e) -> p q e", e=2)[:, :, None, :]
                                    .to_broadcast([P, EP, CAP, 2]), ALU.is_equal).then_inc(s("disp"), 1)
                assert cdn[0] == CD * (h + 1), cdn[0]
            dve.wait_ge(s("ctanh"), 2)
            V.tensor_scalar(sg[:, :], sg[:, :], 0.5, 0.5, ALU.mult, ALU.add).then_inc(s("sgv"), 1)
            dve.wait_ge(s("sgv"), 1)
            V.tensor_scalar(sg[:, :], sg[:, :], tg[:, 3:4], None, ALU.mult).then_inc(s("sgv"), 1)
            for k in range(2 * HALVES):
                h, f = k // 2, k % 2
                dve.wait_ge(s("sh_th"), k + 1)
                if h and f == 0:
                    dve.wait_ge(s("sd_ps"), h)
                V.scalar_tensor_tensor(shg[:, f, :], sth[:, :], 1.0, banks[4 * (k % 2)][:, :], ALU.add,
                                       ALU.mult).then_inc(s("sh_a"), 1)
                dve.wait_ge(s("sh_a"), k + 1)
                V.scalar_tensor_tensor(shg[:, f, :], shg[:, f, :], 0.5, banks[4 * (k % 2) + 1][:, :], ALU.mult,
                                       ALU.mult).then_inc(s("sh_act"), 1)
                if f == 1:
                    dve.wait_ge(s("sd_ps"), h + 1)
                    for t in range(TPH):
                        T = TPH * h + t
                        dve.wait_ge(s("sgv"), 2)
                        V.scalar_tensor_tensor(xres[:, T, :], banks[2][:, tile(t)], sg[:, T:T + 1], xres[:, T, :],
                                               ALU.mult, ALU.add).then_inc(s("sd_out"), 1)
            for n in range(TILES * EP // 8):
                if n % 2 == 0:
                    dve.wait_ge(s("dT_ps"), n + 1)
                    t, q = n // (EP // 8), n % (EP // 8)
                    V.tensor_copy(dispT[:, 8 * q:8 * q + 8, tile(t)],
                                  banks[n % 2][:, :].bitcast(F16).rearrange("p (q n) -> p q n", q=8))\
                        .then_inc(s("dT_sb"), 1)
            dve.wait_ge(s("ws_ps"), 1)
            V.tensor_reduce(wslot2[:, :, :], banks[4][:, 0:EP * 6].rearrange("p (q e k) -> p q e k", e=2, k=3),
                            AX.X, ALU.add).then_inc(s("ws_sb"), 1)
            dve.wait_ge(s("ws_sb"), 1)
            V.tensor_scalar(wslot[:, :], wslot2[:, :, 0], parity[:, 0:1], None, ALU.mult).then_inc(s("ws_sb"), 1)
            dve.wait_ge(s("ws_sb"), 2)
            V.scalar_tensor_tensor(wslot[:, :], wslot2[:, :, 1], parity[:, 1:2], wslot[:, :], ALU.mult,
                                   ALU.add).then_inc(s("ws_sb"), 1)
            V.memset(actb[:, :, :, :, :], 0.0).then_inc(s("ws_sb"), 1)
            dve.wait_ge(s("ws_sb"), 4)

            def finish(g):
                r = g % 2
                dve.wait_ge(s("dn_ps"), g + 1)
                if g >= 2:
                    dve.wait_ge(s("sc_g"), g - 1)
                for q in range(GRP):
                    V.tensor_scalar(eo[:, tile(q)], banks[4][:, tile(q)], wslot[:, GRP * g + q:GRP * g + q + 1], None,
                                    ALU.mult).then_inc(s("dn_v"), 1)
                p3 = [e3[:, r, i, :, :].rearrange("p q n -> p (q n)") for i in range(3)]
                dve.wait_ge(s("dn_v"), GRP * (g + 1))
                V.tensor_copy(p3[0], eo[:, :]).then_inc(s("dn_h1"), 1)
                dve.wait_ge(s("dn_h1"), g + 1)
                V.tensor_tensor(er[:, :], eo[:, :], p3[0], ALU.subtract).then_inc(s("dn_r1"), 1)
                dve.wait_ge(s("dn_r1"), g + 1)
                V.tensor_copy(p3[1], er[:, :]).then_inc(s("dn_h2"), 1)
                dve.wait_ge(s("dn_h2"), g + 1)
                V.tensor_tensor(p3[2], er[:, :], p3[1], ALU.subtract).then_inc(s("dn_r2"), 1)
            for g in range(NGRP):
                r = g % 2
                dve.wait_ge(s("up_th"), g + 1)
                if g:
                    dve.wait_ge(s("up_act"), 2 * g)
                V.scalar_tensor_tensor(ab[:, :], th[:, :], 1.0, banks[3][:, 0:256], ALU.add,
                                       ALU.mult).then_inc(s("up_a"), 1)
                dve.wait_ge(s("up_a"), g + 1)
                if g >= 2:
                    dve.wait_ge(s("dn_ps"), g - 1)
                for i in range(2):
                    V.scalar_tensor_tensor(actb[seq(i), r, :, :, i],
                                           ab[seq(i), :].rearrange("p (q c) -> p q c", q=GRP), 0.5,
                                           banks[3][seq(i), 256:512].rearrange("p (q c) -> p q c", q=GRP),
                                           ALU.mult, ALU.mult).then_inc(s("up_act"), 1)
                finish(g)
            for t in range(TILES):
                dve.wait_ge(s("yt_ps"), t // TPH + 1)
                dve.wait_ge(s("sd_out"), TILES)
                V.scalar_tensor_tensor(xres[:, t, :], banks[t // TPH][:, tile(t % TPH)], tg[:, 3:4], xres[:, t, :],
                                       ALU.mult, ALU.add).then_inc(s("fin"), 1)

        @block.tensor
        def _(pe):
            def mm(out, lhsT, rhs, start=True, stop=True):
                return nc.tensor.matmul(out, lhsT, rhs, start=start, stop=stop)

            pe.wait_ge(ld["ctxT"], 16)
            pe.wait_ge(ld["wqkv"], 4 * 16)
            for h in range(HALVES):
                mm(banks[h][:, :], wk[:, :], ctxT[:, half(h)]).then_inc(s("kT_ps"), 1)
            for k in range(4):
                for j in range(4):
                    b = 4 * k + j
                    for i in range(2):
                        last = mm(banks[2 + k][seq(i), tile(j)], ctxT[:, seq(b)], wv[:, :])
                last.then_inc(s("v_ps"), 1)
            pe.wait_ge(s("consts"), NCONST)

            def lnT(n, bank):
                for t in range(TPH):
                    T = TPH * (n % 2) + t
                    pe.wait_ge(s("ln_out"), TPH * n + t + 1)
                    last = nc.tensor.transpose(bank[:, tile(t)], hn[:, T, :], ident[:, :])
                last.then_inc(s("hT_ps"), 1)
            for h in range(HALVES):
                lnT(h, banks[6 + h])
                pe.wait_ge(s("hT_sb"), h + 1)
                pe.wait_ge(s("kT_sb"), h + 1)
                mm(banks[h][:, :], wq[:, :], hT[:, half(h)]).then_inc(s("q_ps"), 1)
            pe.wait_ge(s("sim2"), 1)
            mm(banks[7][:, 256:256 + E0], ones[:, :], sim2[:, :]).then_inc(s("sn_ps"), 1)

            def scores(t):
                b0 = 2 * (t % 2)
                n = t // TPH + 1
                pe.wait_ge(s("kexp_d"), 6 * n)
                pe.wait_ge(s("kexp_a"), 5 * n)
                pe.wait_ge(s("kexp_p"), 5 * n)
                pe.wait_ge(s("q_sb"), 2)
                if t < 2:
                    pe.wait_ge(s("v_sb"), 9)
                else:
                    pe.wait_ge(s("sc_sub"), t - 1)
                for k in range(2):
                    for i in range(2):
                        b = 2 * t + i
                        last = mm(banks[b0 + k][seq(i), :], qT[:, seq(b)], kexp[:, b, 8 * k:8 * k + 8, :])
                last.then_inc(s("sc_ps"), 1)

            def probs_T(t):
                pe.wait_ge(s("sc_exp"), t + 1)
                if t:
                    pe.wait_ge(s("pT_sb"), 2 * t)
                for j in range(PAIRS):
                    last = nc.tensor.transpose(banks[4 + j // 4][:, tile(j % 4)], prob[:, t % 2, tile(j)], ident[:, :])
                last.then_inc(s("pT_ps"), 1)

            def pv(t):
                pe.wait_ge(s("pT_sb"), 2 * (t + 1))
                pe.wait_ge(s("v_sb"), 9)
                if t:
                    pe.wait_ge(s("pv_sb"), t)
                for j in range(PAIRS):
                    for i in range(2):
                        b = 2 * t + i
                        last = mm(banks[6][seq(i), 18 * j:18 * j + 18], probT[:, j * P + i * SEQ:j * P + (i + 1) * SEQ],
                                  vblk[:, b * PAIRS + j, :, :].rearrange("p h d -> p (h d)"))
                last.then_inc(s("pv_ps"), 1)

            def project(t):
                pe.wait_ge(s("pv_sb"), t + 1)
                if t:
                    pe.wait_ge(s("y_out"), t)
                else:
                    pe.wait_ge(s("sn_pre"), 1)
                nc.tensor.transpose(banks[7][:, 0:P], ohead[:, :], ident[:, :]).then_inc(s("oT_ps"), 1)
                pe.wait_ge(s("oT_sb"), t + 1)
                mm(banks[7][:, P:2 * P], oheadT[:, :], wo[:, :]).then_inc(s("y_ps"), 1)
            for t in range(TILES + 2):
                if t < TILES:
                    scores(t)
                if 1 <= t <= TILES:
                    probs_T(t - 1)
                    pv(t - 1)
                if t >= 2:
                    project(t - 2)

            def gate(h):
                base = 2 + 3 * h
                if h == 0:
                    pe.wait_ge(s("pT_sb"), 2 * TILES)
                    pe.wait_ge(s("sc_sub"), TILES)
                else:
                    pe.wait_ge(s("y_out"), TILES)
                lnT(2 + h, banks[base])
                pe.wait_ge(s("hT_sb"), 3 + h)
                pe.wait_ge(s("sn"), 1)
                for t in range(TPH):
                    last = mm(banks[base + 2][:, E0 * t:E0 * (t + 1)], hT[:, tile(TPH * h + t)], simm[:, :])
                last.then_inc(s("lg_ps"), 1)
                pe.wait_ge(s("w3"), h + 1)
                out = banks[base + 1][0:3 * E0, 0:HT // 2].bitcast(BF16)
                for t in range(TPH):
                    last = nc.tensor.transpose(out[:, tile(t)], w3[:, TPH * h + t, :], identb[:, :])
                last.then_inc(s("wT_ps"), 1)
            gate(0)
            gate(1)
            cnt = [0]

            def spread(h, e):
                n = cnt[0]
                cnt[0] += 1
                pe.wait_ge(s("wT_sb"), h + 1)
                pe.wait_ge(s("sel"), NSEL)
                if n >= 2:
                    pe.wait_ge(s("z_sb"), n - 1)
                mm(banks[n % 2][:, :], selw[:, e, :], wT[:, half(h)]).then_inc(s("wb_ps"), 1)

            used = [0]
            for h in range(HALVES):
                base = 2 + 3 * h
                pe.wait_ge(ld["proj"], 4 * 16)
                spread(h, 0)
                spread(h, 1)
                for e in range(E0):
                    n = used[0]
                    used[0] += 1
                    pe.wait_ge(s("z_sb"), n + 1)
                    if e == 0:
                        pe.wait_ge(s("gd"), GD * (h + 1))
                    for i in range(3):
                        last = mm(banks[base + i][:, :], proj[:, i, e, :], z[:, n % 2, :], start=e == 0,
                                  stop=e == E0 - 1)
                    last.then_inc(s("zuse"), 1)
                    if e + 2 < E0:
                        spread(h, e + 2)
                pe.wait_ge(s("qkv_sb"), 3 * (h + 1))
                for i in range(8):
                    last = nc.tensor.transpose(banks[base + i // 4][0:SEQ, tile(i % 4)], qkvT[:, 2, seq(i)],
                                               ident[:, :])
                last.then_inc(s("v2_ps"), 1)
                for t in range(TPH):
                    for i in range(2):
                        last = mm(banks[base + 2][seq(i), SEQ * t:SEQ * (t + 1)], qkvT[:, 0, seq(2 * t + i)],
                                  qkvT[:, 1, seq(2 * t + i)])
                last.then_inc(s("at_ps"), 1)
                pe.wait_ge(s("at_d"), 5 * (h + 1))
                for t in range(TPH):
                    last = nc.tensor.transpose(banks[base + 2][0:SEQ, tile(t)], att[:, t, :], ident[:, :])
                last.then_inc(s("aT_ps"), 1)
                pe.wait_ge(s("aT_sb"), h + 1)
                pe.wait_ge(s("v2_sb"), 2 * (h + 1))
                for b in range(8):
                    last = mm(banks[base][:, seq(b)], vk[0:SEQ, b, :], attT[0:SEQ, seq(b)])
                last.then_inc(s("ob_ps"), 1)
                spread(h, 0)
                spread(h, 1)
                for e in range(E0):
                    n = used[0]
                    used[0] += 1
                    pe.wait_ge(s("z_sb"), n + 1)
                    ins = mm(banks[base + 1][:, :], proj[:, 3, e, :], z[:, n % 2, :], start=e == 0, stop=e == E0 - 1)
                    ins.then_inc(s("zuse"), 1)
                    if e + 2 < E0:
                        spread(h, e + 2)
                pe.wait_ge(s("acc_sb"), h + 1)
                for t in range(TPH):
                    last = nc.tensor.transpose(banks[base + 2][:, tile(t)], accT[:, tile(t)], ident[:, :])
                last.then_inc(s("tr_ps"), 1)
            for h in range(HALVES):
                base = 2 + 3 * h
                lnT(4 + h, banks[base])
                pe.wait_ge(s("hT_sb"), 5 + h)
                pe.wait_ge(s("tr_out"), TPH * (h + 1))
                for t in range(TPH):
                    for i in range(2):
                        b = 2 * (TPH * h + t) + i
                        last = mm(banks[base + 2][seq(i), SEQ * t:SEQ * (t + 1)], hT[:, seq(b)], ctxT[:, seq(b)])
                last.then_inc(s("la_ps"), 1)
                pe.wait_ge(s("la_exp"), h + 1)
                pe.wait_ge(ld["ctxk"], 16)
                for t in range(TPH):
                    last = nc.tensor.transpose(banks[base + 1][0:SEQ, tile(t)], att[:, t, :], ident[:, :])
                last.then_inc(s("lT_ps"), 1)
                pe.wait_ge(s("lT_sb"), h + 1)
                for t in range(TPH):
                    for i in range(2):
                        b = 2 * (TPH * h + t) + i
                        last = mm(banks[base][seq(i), tile(t)], attT[0:SEQ, seq(2 * t + i)], ctxk[:, b, :])
                last.then_inc(s("lo_ps"), 1)
            pe.wait_ge(ld["gw"], 32)
            for h in range(HALVES):
                base = 2 + 3 * h
                lnT(6 + h, banks[base])
                pe.wait_ge(s("hT_sb"), 7 + h)
                for t in range(TPH):
                    last = mm(banks[base + 1][:, (E1 + 1) * t:(E1 + 1) * (t + 1)], hT[:, tile(TPH * h + t)], gw[:, :])
                last.then_inc(s("cl_ps"), 1)
                pe.wait_ge(s("cl_sb"), 2 * h + 2)
                for t in range(TPH):
                    T = TPH * h + t
                    out = banks[base + 2][:, E1 * t:E1 * (t + 1)]
                    for k in range(T):
                        mm(out, ones16[:, :], chosen[:, k, :], start=k == 0, stop=False)
                    last = mm(out, upper16[:, :], chosen[:, T, :], start=T == 0, stop=True)
                last.then_inc(s("pos_ps"), 1)
            pe.wait_ge(ld["shared"], 32)
            pe.wait_ge(s("cd"), 2 * CD)
            for k in range(2 * HALVES):
                h, f = k // 2, k % 2
                b = 4 * (k % 2)
                if k >= 2:
                    pe.wait_ge(s("sh_act"), k - 1)
                mm(banks[b][:, :], sgu[:, f * P:(f + 1) * P], hT[:, half(h)])
                mm(banks[b + 1][:, :], sgu[:, SHARED + f * P:SHARED + (f + 1) * P],
                   hT[:, half(h)]).then_inc(s("sh_ps"), 1)
                if f == 1:
                    pe.wait_ge(s("sh_act"), k + 1)
                    if h:
                        pe.wait_ge(s("sd_out"), TPH)
                    for t in range(TPH):
                        for j in range(2):
                            last = mm(banks[2][:, tile(t)], shg[:, j, tile(t)], sdn[:, j, :], start=j == 0,
                                      stop=j == 1)
                    last.then_inc(s("sd_ps"), 1)
            for n in range(TILES * EP // 8):
                t, q = n // (EP // 8), n % (EP // 8)
                if n >= 2:
                    pe.wait_ge(s("dT_sb") if n % 2 == 0 else s("dT_sbA"), n // 2)
                pe.wait_ge(s("disp"), t + 1)
                out = banks[n % 2][:, :].bitcast(F16)
                for j in range(8):
                    last = nc.tensor.transpose(out[:, tile(j)], disp[:, t, 8 * q + j, :], ident16[:, :])
                last.then_inc(s("dT_ps"), 1)
            for q in range(EP):
                for t in range(TILES):
                    last = mm(banks[4][:, 6 * q:6 * q + 6], disp[:, t, q, :],
                              wc3[:, t, 2 * q:2 * q + 2, :].rearrange("p e k -> p (e k)"), start=t == 0,
                              stop=t == TILES - 1)
            last.then_inc(s("ws_ps"), 1)
            pe.wait_ge(s("xh_lo"), 2)
            pe.wait_ge(s("dT_sb"), 16)
            pe.wait_ge(s("dT_sbA"), 16)
            pe.wait_ge(s("sd_out"), TILES)

            def gather(n):
                if n >= 2:
                    pe.wait_ge(s("ga_sb"), n - 1)
                for t in range(TILES):
                    last = mm(banks[n % 2][:, 0:2 * P], disp[:, t, n, :], xh[:, t, :, :].rearrange("p k c -> p (k c)"),
                              start=t == 0, stop=t == TILES - 1)
                last.then_inc(s("ga_ps"), 1)

            def slots_T(n):
                g, q = n // GRP, n % GRP
                pe.wait_ge(s("ga_sb"), n + 1)
                if q == 0 and g:
                    pe.wait_ge(s("xe_sb"), g)
                mm(banks[2][:, tile(q)], gx[:, n % 2, 0:P], ident16[:, :], stop=False)
                mm(banks[2][:, tile(q)], gx[:, n % 2, P:2 * P], idlow16[:, :], start=False).then_inc(s("xe_ps"), 1)

            def up(g):
                pe.wait_ge(ld_exp[g % 2], 32 * (g // 2 + 1))
                pe.wait_ge(s("xe_sb"), g + 1)
                if g:
                    pe.wait_ge(s("up_act"), 2 * g)
                for q in range(GRP):
                    for i in range(2):
                        x = xeT[:, g % 2, q, :].rearrange("p (c e) -> p c e", e=2)[:, :, i]
                        w = wguR[:, g % 2, 2 * q + i, :]
                        mm(banks[3][seq(i), SEQ * q:SEQ * (q + 1)], w[:, 0:INNER], x)
                        last = mm(banks[3][seq(i), 256 + SEQ * q:256 + SEQ * (q + 1)], w[:, INNER:P], x)
                last.then_inc(s("up_ps"), 1)

            def down(g):
                pe.wait_ge(s("up_act"), 2 * (g + 1))
                if g:
                    pe.wait_ge(s("dn_v"), GRP * g)
                else:
                    pe.wait_ge(s("ws_sb"), 4)
                for q in range(GRP):
                    last = mm(banks[4][:, tile(q)], actb[:, g % 2, q, :, :].rearrange("p c e -> p (c e)"),
                              wdR[:, g % 2, q, :])
                last.then_inc(s("dn_ps"), 1)

            def scatter(g):
                pe.wait_ge(s("dn_r2"), g + 1)
                for h in range(HALVES):
                    for q in range(GRP):
                        for i in range(3):
                            last = mm(banks[5 + h][:, :], e3[:, g % 2, i, q, :], dispT[:, GRP * g + q, half(h)],
                                      start=g == 0 and q == 0 and i == 0, stop=g == NGRP - 1 and q == GRP - 1 and i == 2)
                last.then_inc(s("sc_g"), 1)
            gather(0)
            for g in range(NGRP + 1):
                if g < NGRP:
                    for q in range(GRP):
                        n = g * GRP + q
                        if n + 1 < EP:
                            gather(n + 1)
                        slots_T(n)
                    up(g)
                if g:
                    scatter(g - 1)
                if g < NGRP:
                    down(g)
            pe.wait_ge(s("ga_sb"), EP)
            for h in range(HALVES):
                pe.wait_ge(s("yT_sb"), h + 1)
                for t in range(TPH):
                    last = nc.tensor.transpose(banks[h][:, tile(t)], yT[:, tile(TPH * h + t)], ident[:, :])
                last.then_inc(s("yt_ps"), 1)


def kernel(**inputs):
    import numpy as np
    import concourse.bacc as bacc
    from concourse.bass_utils import run_bass_kernel_spmd

    a = {k: np.asarray(v) for k, v in inputs.items()}
    x, c = a["x"].reshape(TOKENS, P), a["ctx_1024"].reshape(TOKENS, P)
    laid = {
        "x": x, "ctx": c, "ctxT": c.T, "mask": a["mask_BxS2_ik1"], "g_xattn": a["g_xattn"], "g_ffn": a["g_ffn"],
        "WqT": a["L0_xattn_Wq"].T, "WkT": a["L0_xattn_Wk"].T, "WvT": a["L0_xattn_Wv"].T, "WoT": a["L0_xattn_Wo"].T,
        "bo": a["L0_xattn_bo"], "sim": a["L0_ffn_sim_matrix"], "gates": a["L0_ffn_gates"],
        "q_proj": a["L0_ffn_q_proj"], "k_proj": a["L0_ffn_k_proj"], "v_proj": a["L0_ffn_v_proj"],
        "o_proj": a["L0_ffn_o_proj"], "gate_w": a["L1_ffn_gate_w"], "sgate_w": a["L1_ffn_shared_gate_w"],
        "sgu": a["L1_ffn_shared_gate_up_w"], "sdn": a["L1_ffn_shared_down_w"], "egu": a["L1_ffn_expert_gate_up_w"],
        "edn": a["L1_ffn_expert_down_w"],
    }
    laid = {k: np.ascontiguousarray(v) for k, v in laid.items()}
    nc = bacc.Bacc("TRN2", target_bir_lowering=False, num_devices=1, dynamic_dma_scratch_size=1024)
    d = {k: nc.dram_tensor("in_" + k, v.shape, mybir.dt.from_np(v.dtype), kind="ExternalInput").ap()
         for k, v in laid.items()}
    d["out"] = nc.dram_tensor("out_0", (TOKENS, P), F32, kind="ExternalOutput").ap()
    program(nc, d)
    r = run_bass_kernel_spmd(nc, [{"in_" + k: v for k, v in laid.items()}], core_ids=[0])
    return r.results[0]["out_0"].reshape(BATCH, SEQ, P)
```

```python
from contextlib import ExitStack

import concourse.bass as bass
from concourse import mybir

F32 = mybir.dt.float32
F16 = mybir.dt.float16
F32R = mybir.dt.float32r
BF16 = mybir.dt.bfloat16
I32 = mybir.dt.int32
U32 = mybir.dt.uint32
ALU = mybir.AluOpType
ACT = mybir.ActivationFunctionType
AX = mybir.AxisListType

P = 128
SEQ = 64
BATCH = 16
TOKENS = SEQ * BATCH
TILES = TOKENS // P
HALVES = 2
TPH = TILES // HALVES
HT = TPH * P
HEADS = 16
HD = P // HEADS
PAIRS = HEADS // 2
E0 = 16
E1 = 64
EP = E1 // 2
CAP = 64
INNER = 64
SHARED = 256
GRP = 4
NGRP = EP // GRP
EPS = 1e-5
TINY = 1e-24
NEG = 1e10
BIG = 512.0
LOW = -3.0e38
LO_SCALE = 2048.0
NCONST = 9
NSEL = 9
NSPLIT = E0 * P // 512
CHUNKS = PAIRS // 2
KD = 5
LN_HALF = (0, 1, 0, 1, 0, 0, 1, 1)
LN_PREV = (None, None, 0, 1, 2, 4, 3, 6)
SPLIT_AT = (0, 3, 5, 8, 3 * NSPLIT)
LG_BANK = (1, 7)
WT_BANK = (0, 6)
ZR = 4
ZSP = 3
DG = 2
EPR = 2 * GRP


def spread_bank(n):
    if n < 2 * E0:
        return n % 2
    return ((0, 1, 2, 4) if n < 3 * E0 else (0, 1, 5, 7))[n % 4]


def spread_before(n):
    if n < 2:
        return None
    if n < 2 * E0 + 2:
        return n - 2
    return n - 4 if n % 4 < 2 or (n % E0 >= 4) else None
GD, GD_EXP = 30, 18
CD, CD_EXP = 17, 9


def program(nc, d):
    ctx = ExitStack()
    with ctx:
        def sb(name, shape, dt=F32):
            return ctx.enter_context(nc.sbuf_tensor(name, shape, dt))

        def sem(name):
            return ctx.enter_context(nc.semaphore(name))

        xres = sb("xres", [P, TILES, P])
        hn = sb("hn", [P, TILES, P])
        hT = sb("hT", [P, TOKENS])
        ctxT = sb("ctxT", [P, TOKENS])
        ctxk2 = sb("ctxk2", [P, BATCH * P])
        ctxk = ctxk2[0:SEQ, :].rearrange("p (b c) -> p b c", b=BATCH)
        wq, wk, wv = (sb(n, [P, P]) for n in ("wq", "wk", "wv"))
        wo = sb("wo", [P, 2, P])
        bo = sb("bo", [P, P])
        gates4 = sb("gates4", [P, 4])
        tg = sb("tg", [P, 4])
        simm = sb("simm", [P, E0])
        sim2 = sb("sim2", [P, E0])
        gt0 = sb("gt0", [P, E0])
        sig0 = sb("sig0", [P, E0])
        maski = sb("maski", [P, TILES, SEQ], I32)
        maskfn = sb("maskfn", [P, 2 * TILES * SEQ])
        maskf = maskfn[:, 0:TILES * SEQ].rearrange("p (t k) -> p t k", t=TILES)
        maskn = maskfn[:, TILES * SEQ:].rearrange("p (t k) -> p t k", t=TILES)
        gw = sb("gw", [P, E1 + 1])
        sgu = sb("sgu", [P, 2 * SHARED])
        sdn = sb("sdn", [P, 2, P])
        big = sb("big", [P, TILES * EP * CAP * 2], F16)
        bigf = big[:, :].bitcast(F32)
        KSIZE = BATCH * PAIRS * SEQ
        kexp = bigf[:, 0:KSIZE].rearrange("p (c b j k) -> p c b j k", b=4, j=PAIRS, k=SEQ)
        raw = bigf[:, KSIZE:KSIZE + 2 * E0 * P].rearrange("p (r n) -> p r n", r=2)
        qexp = bigf[:, KSIZE + 2 * E0 * P:KSIZE + 2 * E0 * P + 2 * TOKENS].rearrange("p (b e q) -> p b e q", b=BATCH, e=2)
        oexp = bigf[:, 0:E0 * P].rearrange("p (e c) -> p e c", e=E0)
        disp = big[:, :].rearrange("p (g t q s) -> p g t q s", g=EP // DG, t=TILES, q=DG)
        split = sb("split", [P, 2 * 3 * E0 * P], F32R)
        wsp = split[:, :].rearrange("p (k i n) -> p k i n", k=2, i=3)
        dispT = split[:, 0:EPR * TOKENS].rearrange("p (r n) -> p r n", r=EPR)
        esp = split[:, EPR * TOKENS:EPR * (TOKENS + 2 * P)].rearrange("p (r k n) -> p r k n", r=EPR, k=2)
        z = bigf[:, E0 * P:E0 * P + ZR * HT].rearrange("p (r n) -> p r n", r=ZR)
        zsp = sb("zsp", [P, ZSP, 2, HT], F32R)
        work = sb("work", [P, 4 * HT * TPH])
        ident = sb("ident", [P, P])
        ident16 = sb("ident16", [P, P], F16)
        ones = sb("ones", [P, P])
        ones16 = sb("ones16", [P, P], F16)
        upper16 = sb("upper16", [P, P], F16)
        headm = sb("headm", [P, HEADS])
        pairm = sb("pairm", [P, PAIRS])
        oddm = sb("oddm", [P, 2])
        halfm = sb("halfm", [P, 2])
        parity = sb("parity", [P, 2])
        selc = sb("selc", [3 * E0, E0])
        identb = sb("identb", [P, P], BF16)
        io16 = sb("io16", [P, E0])
        slotc = sb("slotc", [P, CAP, 2], F16)
        selw = sb("selw", [E0 * 3, E0, P], BF16)
        mhalf = sb("mhalf", [P, E0])

        banks = [ctx.enter_context(nc.psum_tensor(f"bank{i}", [P, 512], F32)) for i in range(8)]

        o = 0

        def take(n):
            nonlocal o
            o += n
            return work[:, o - n:o]
        kT = take(TOKENS)
        vblk = take(BATCH * CHUNKS * 36).rearrange("p (n i e d) -> p n i e d", i=2, e=2, d=9)
        prob = take(2 * HEADS * SEQ).rearrange("p (r n) -> p r n", r=2)
        probT = take(HEADS * SEQ)
        ohead = take(P)
        oheadT = take(P)
        rsum = take(HEADS)
        smax = take(2 * HEADS).rearrange("p (r h) -> p r h", r=2)
        assert o <= work.shape[1]
        o = 0
        qkvT = take(3 * HT).rearrange("p (r n) -> p r n", r=3)
        vk = take(8 * P).rearrange("p (b n) -> p b n", b=8)
        att = take(TPH * SEQ).rearrange("p (t k) -> p t k", t=TPH)
        attT = take(HT)
        oT = take(2 * HT).rearrange("p (r n) -> p r n", r=2)
        accT = take(HT)
        room = work

        def take_c(n):
            nonlocal o
            o += n
            return room[:, o - n:o]
        xh = take_c(TILES * P).bitcast(F16).rearrange("p (t k c) -> p t k c", t=TILES, k=2)
        sth = take_c(HT)
        shg = take_c(2 * HT).rearrange("p (f n) -> p f n", f=2)
        wc3 = take_c(TILES * E1 * 3 // 2).bitcast(BF16).rearrange("p (t e k) -> p t e k", t=TILES, k=3)
        assert o <= room.shape[1]
        o = 0
        xeT = take_c(2 * GRP * P).rearrange("p (r q n) -> p r q n", r=2, q=GRP)
        yT = take_c(TOKENS)
        stats = sb("stats", [P, TPH, 6])
        mv = sb("mv", [P, TILES, 2])
        ve = sb("ve", [P, TPH])
        rstd = sb("rstd", [P, TILES])
        negm = sb("negm", [P, TILES])
        shift = sb("shift", [P, TILES])
        sq = sb("sq", [P, P])
        ss = sb("ss", [P, TPH])
        rn = sb("rn", [P, TPH])
        lg = sb("lg", [P, TPH, E0])
        top = sb("top", [P, TPH, 8])
        topi = sb("topi", [P, TPH, 8], U32)
        topf = sb("topf", [P, TPH, 8])
        ga = sb("ga", [P, TPH, E0])
        gb = sb("gb", [P, TPH, E0])
        gc = sb("gc", [P, TPH, E0])
        fbk = sb("fbk", [P, TPH, E0])
        g1 = sb("g1", [P, TPH])
        g2 = sb("g2", [P, TPH])
        w3 = sb("w3", [P, TILES, 3 * E0], BF16)
        wT = sb("wT", [3 * E0, TOKENS], BF16)
        amax = sb("amax", [P, TPH])
        asum = sb("asum", [P, TPH])
        lgc = sb("lgc", [P, TILES, E1 + 1])
        rep = sb("rep", [P, TPH, E1])
        topc = sb("topc", [P, TPH, 8])
        chosen = sb("chosen", [P, TILES, E1], F16)
        wex = sb("wex", [P, TPH, E1])
        wres = sb("wres", [P, TPH, E1])
        csum = sb("csum", [P, TPH])
        post = sb("post", [P, TPH, E1])
        pos16 = sb("pos16", [P, EP // DG, TILES, 2 * DG], F16)
        sg = sb("sg", [P, TILES])
        wslot2 = sb("wslot2", [P, EP, 2])
        wslot = sb("wslot", [P, EP])
        xlow = sb("xlow", [P, GRP * P])
        th = sb("th", [P, GRP * CAP])
        ab = sb("ab", [P, GRP * CAP])
        actb = maskfn[:, :].rearrange("p (r q c e) -> p r q c e", r=2, q=GRP, c=CAP)
        wguR = ctxk2[:, :].rearrange("p (r e f) -> p r e f", r=2, e=2 * GRP)
        wdR = ctxT[:, :].rearrange("p (r q h) -> p r q h", r=2, q=GRP)

        ld = {n: sem("ld_" + n) for n in ("x", "ctxT", "wkv", "wqo", "misc", "mask", "ctxk", "oexp", "gw", "shared")}
        ld_raw = [sem(f"ld_raw{i}") for i in range(3)]
        ld_exp = [sem(f"ld_exp{i}") for i in range(2)]
        S = {}

        def s(name):
            if name not in S:
                S[name] = sem(name)
            return S[name]

        block = ctx.enter_context(nc.Block())

        def seq(b):
            return slice(b * SEQ, (b + 1) * SEQ)

        def half(h):
            return slice(h * HT, (h + 1) * HT)

        def tile(t):
            return slice(t * P, (t + 1) * P)

        @block.sync
        def _(sp):
            sp.dma_start(ctxT[:, :], d["ctxT"]).then_inc(ld["ctxT"], 16)
            sp.dma_start(wk[:, :], d["WkT"]).then_inc(ld["wkv"], 16)
            sp.dma_start(wv[:, :], d["WvT"]).then_inc(ld["wkv"], 16)
            sp.dma_start(xres[:, :, :], d["x"].rearrange("(t p) c -> p t c", p=P)).then_inc(ld["x"], 16)
            sp.dma_start(wq[:, :], d["WqT"]).then_inc(ld["wqo"], 16)
            for i in range(2):
                sp.dma_start(wo[seq(i), :, :], d["WoT"]).then_inc(ld["wqo"], 16)
            sp.dma_start(bo[:, :], d["bo"].partition_broadcast(P)).then_inc(ld["misc"], 16)
            sp.dma_start(gates4[:, 0:2], d["g_xattn"].partition_broadcast(P)).then_inc(ld["misc"], 16)
            sp.dma_start(gates4[:, 2:4], d["g_ffn"].partition_broadcast(P)).then_inc(ld["misc"], 16)
            sp.dma_start(gt0[:, :], d["gates"].partition_broadcast(P)).then_inc(ld["misc"], 16)
            sp.dma_start(simm[:, :], d["sim"]).then_inc(ld["misc"], 16)
            m = d["mask"].rearrange("(t b) k -> b t k", b=2)
            for i in range(3):
                if i == 2:
                    sp.wait_ge(s("split_lo"), NSPLIT)
                sp.dma_start(raw[:, i % 2, :].rearrange("p (e h) -> p e h", e=E0),
                             d["qkv"[i] + "_proj"].rearrange("e c h -> c e h")).then_inc(ld_raw[i], 16)
            for b in range(2):
                sp.dma_start(maski[seq(b), :, :], m[b].partition_broadcast(SEQ)).then_inc(ld["mask"], 16)
            sp.dma_start(ctxk[:, :, :], d["ctx"].rearrange("(b k) c -> k b c", k=SEQ)).then_inc(ld["ctxk"], 16)
            sp.dma_start(gw[:, 0:E1], d["gate_w"]).then_inc(ld["gw"], 16)
            sp.dma_start(gw[:, E1:E1 + 1], d["sgate_w"]).then_inc(ld["gw"], 16)
            sp.dma_start(sgu[:, :], d["sgu"]).then_inc(ld["shared"], 16)
            sp.dma_start(sdn[:, :, :], d["sdn"].rearrange("(f p) h -> p f h", p=P)).then_inc(ld["shared"], 16)
            sp.wait_ge(s("sc_ps"), 2 * TILES)
            sp.dma_start(oexp[:, :, :], d["o_proj"].rearrange("e h c -> h e c")).then_inc(ld["oexp"], 16)
            sp.wait_ge(s("lo_ps"), 2)
            for g in range(NGRP):
                if g >= 2:
                    sp.wait_ge(s("up_ps"), g - 1)
                    sp.wait_ge(s("dn_ps"), g - 1)
                sp.dma_start(wguR[:, g % 2, :, :], d["egu"][2 * GRP * g:2 * GRP * (g + 1)]
                             .rearrange("e c f -> c e f")).then_inc(ld_exp[g % 2], 16)
                sp.dma_start(wdR[:, g % 2, :, :], d["edn"][2 * GRP * g:2 * GRP * (g + 1)]
                             .rearrange("(q e) i h -> (e i) q h", e=2)).then_inc(ld_exp[g % 2], 16)
            for h in range(HALVES):
                sp.wait_ge(s("fin"), TPH * (h + 1))
                sp.dma_start(d["out"][half(h), :].rearrange("(t p) c -> p t c", p=P),
                             xres[:, TPH * h:TPH * (h + 1), :]).then_inc(s("out"), 16)
            sp.wait_ge(s("out"), 16 * HALVES)

        @block.gpsimd
        def _(pool):
            done = [0]

            def const(ins):
                ins.then_inc(s("consts"), 1)
                done[0] += 1

            def settle():
                pool.wait_ge(s("consts"), done[0])
            const(nc.gpsimd.memset(ident[:, :], 0.0))
            settle()
            const(nc.gpsimd.affine_select(out=ident[:, :], in_=ident[:, :], compare_op=ALU.not_equal, fill=1.0,
                                          base=0, pattern=[[-1, P]], channel_multiplier=1))
            for x, v in ((ones, 1.0), (ones16, 1.0), (upper16, 1.0), (mhalf, -0.5)):
                const(nc.gpsimd.memset(x[:, :], v))
            const(nc.gpsimd.iota(slotc[:, :, :], [[1, CAP], [0, 2]], base=0, channel_multiplier=0,
                                 allow_small_or_imprecise_dtypes=True))
            const(nc.gpsimd.iota(io16[:, :], [[1, E0]], base=0, channel_multiplier=0,
                                 allow_small_or_imprecise_dtypes=True))
            settle()
            const(nc.gpsimd.affine_select(out=upper16[:, :], in_=upper16[:, :], compare_op=ALU.is_gt, fill=0.0,
                                          base=0, pattern=[[1, P]], channel_multiplier=-1))

            def rsqrt_ln(n):
                ts = slice(TPH * LN_HALF[n], TPH * (LN_HALF[n] + 1))
                pool.wait_ge(s("ln_var"), n + 1)
                nc.gpsimd.tensor_tensor(rstd[:, ts], ve[:, :], mhalf[:, 0:TPH], ALU.pow).then_inc(s("ln_rstd"), 1)
                pool.wait_ge(s("ln_rstd"), n + 1)
                pool.wait_ge(s("ln_neg"), n + 1)
                nc.gpsimd.tensor_tensor(shift[:, ts], negm[:, ts], rstd[:, ts], ALU.mult).then_inc(s("ln_shift"), 1)

            def norms(h):
                pool.wait_ge(s("sq_sum"), TPH * (h + 1))
                if h:
                    pool.wait_ge(s("gd"), GD * h)
                nc.gpsimd.tensor_scalar(rn[:, :], ss[:, :], TINY, None, ALU.max).then_inc(s("rnorm"), 1)
                pool.wait_ge(s("rnorm"), 2 * h + 1)
                nc.gpsimd.tensor_tensor(rn[:, :], rn[:, :], mhalf[:, 0:TPH], ALU.pow).then_inc(s("rnorm"), 1)

            def low_parts(i):
                for k in range(NSPLIT):
                    n = NSPLIT * i + k
                    pool.wait_ge(s("split_hi"), n + 1)
                    cut = slice(512 * k, 512 * (k + 1))
                    nc.gpsimd.tensor_tensor(wsp[:, 1, i, cut], raw[:, i % 2, cut], wsp[:, 0, i, cut].bitcast(F32),
                                            ALU.subtract).then_inc(s("split_lo"), 1)
            rsqrt_ln(0)
            rsqrt_ln(1)
            for i in range(3):
                low_parts(i)
                if i == 0:
                    pool.wait_ge(s("sn_pre"), 1)
                    nc.gpsimd.tensor_tensor(sim2[:, :], sim2[:, :], mhalf[:, :], ALU.pow).then_inc(s("sn_pre"), 1)
                    pool.wait_ge(s("sn_pre"), 2)
                    nc.gpsimd.tensor_tensor(simm[:, :], simm[:, :], sim2[:, :], ALU.mult).then_inc(s("sn"), 1)
            rsqrt_ln(2)
            norms(0)
            rsqrt_ln(3)
            norms(1)
            def low_tokens(h):
                ts = slice(TPH * h, TPH * (h + 1))
                pool.wait_ge(s("xh_hi"), h + 1)
                pool.wait_ge(s("hT_ps"), 6 + 2 * h)
                nc.gpsimd.tensor_tensor(hn[:, ts, :], hn[:, ts, :], xh[:, ts, 0, :], ALU.subtract).then_inc(s("xh_r"), 1)
            for n in range(4, 8):
                rsqrt_ln(n)
                if n > 5:
                    low_tokens(n - 6)
            pool.wait_ge(s("la_d"), 7)
            nc.gpsimd.memset(actb[:, :, :, :, :], 0.0).then_inc(s("act0"), 1)

        @block.scalar
        def _(act):
            A = nc.scalar.activation

            def copy(out, in_):
                return A(out, in_, ACT.Copy)

            def keys(c):
                for hd in range(KD, PAIRS):
                    A(kexp[:, c, :, hd, :], kT[:, 4 * SEQ * c:4 * SEQ * (c + 1)].rearrange("p (b k) -> p b k", k=SEQ),
                      ACT.Copy, scale=pairm[:, hd:hd + 1]).then_inc(s("kexp_a"), 1)

            def high_part(n):
                i, k = n // NSPLIT, n % NSPLIT
                act.wait_ge(ld_raw[i], 16)
                cut = slice(512 * k, 512 * (k + 1))
                copy(wsp[:, 0, i, cut], raw[:, i % 2, cut]).then_inc(s("split_hi"), 1)

            def ln_apply(n):
                h = LN_HALF[n]
                act.wait_ge(s("ln_shift"), n + 1)
                if n >= 2:
                    act.wait_ge(s("hT_ps"), LN_PREV[n] + 1)
                for t in range(TPH * h, TPH * (h + 1)):
                    A(hn[:, t, :], xres[:, t, :], ACT.Identity, bias=shift[:, t:t + 1],
                      scale=rstd[:, t:t + 1]).then_inc(s("ln_out"), 1)

            def k_out(h):
                act.wait_ge(s("kT_ps"), h + 1)
                copy(kT[:, half(h)], banks[h][:, :]).then_inc(s("kT_sb"), 1)

            def h_out(h):
                act.wait_ge(s("hT_ps"), h + 1)
                copy(hT[:, half(h)], banks[6 + h][:, :]).then_inc(s("hT_sb"), 1)

            def q_out(h):
                act.wait_ge(s("q_ps"), h + 1)
                for i in range(2):
                    A(qexp[:, 8 * h:8 * (h + 1), i, :], banks[6 * h][:, :].rearrange("p (b q) -> p b q", q=SEQ), ACT.Copy,
                      scale=oddm[:, i:i + 1]).then_inc(s("q_sb"), 1)
            k_out(0)
            act.wait_ge(s("sel"), NSEL)
            act.wait_ge(s("kT_sb"), 1)
            keys(0)
            ln_apply(0)
            k_out(1)
            h_out(0)
            q_out(0)
            ln_apply(1)
            h_out(1)
            q_out(1)
            act.wait_ge(ld["misc"], 5 * 16)
            A(tg[:, :], gates4[:, :], ACT.Tanh).then_inc(s("tanh_g"), 1)
            A(sig0[:, :], gt0[:, :], ACT.Tanh, scale=0.5).then_inc(s("g_act"), 1)
            act.wait_ge(s("kT_sb"), 2)

            def a_exp(t):
                act.wait_ge(s("sc_sub"), 2 * (t + 1))
                A(prob[:, t % 2, :], prob[:, t % 2, :], ACT.Exp, scale=float(P) ** -0.5).then_inc(s("sc_exp"), 1)

            def a_pT(t):
                act.wait_ge(s("pT_ps"), t + 1)
                if t >= 1:
                    act.wait_ge(s("pv_ps"), t)
                for k in range(2):
                    copy(probT[:, 512 * k:512 * (k + 1)], banks[4 + k][:, :]).then_inc(s("pT_sb"), 1)

            def a_oT(t):
                act.wait_ge(s("oT_ps"), t + 1)
                if t >= 1:
                    act.wait_ge(s("y_ps"), t)
                copy(oheadT[:, :], banks[7][:, 0:P]).then_inc(s("oT_sb"), 1)

            def ln_T(n, bank):
                act.wait_ge(s("hT_ps"), n + 1)
                copy(hT[:, half(LN_HALF[n])], bank[:, :]).then_inc(s("hT_sb"), 1)

            def squares(h):
                act.wait_ge(s("ln_out"), TPH * (3 + h))
                if h:
                    act.wait_ge(s("rnorm"), 1)
                for t in range(TPH):
                    if h or t:
                        act.wait_ge(s("sq_sum"), h * TPH + t)
                    A(sq[:, :], hn[:, TPH * h + t, :], ACT.Square,
                      accum_out=ss[:, t:t + 1]).then_inc(s("sq_sum"), 1)

            def gate_exp(h):
                act.wait_ge(s("gd"), GD * h + GD_EXP)
                A(gc[:, :, :], gc[:, :, :], ACT.Exp).then_inc(s("g_act"), 1)

            def gate_T(h):
                act.wait_ge(s("wT_ps"), h + 1)
                copy(wT[:, half(h)], banks[WT_BANK[h]][0:3 * E0, 0:HT // 2].bitcast(BF16)).then_inc(s("wT_sb"), 1)

            for t in range(TILES + 2):
                if 1 <= t <= TILES:
                    a_exp(t - 1)
                    if t == 1:
                        keys(1)
                    a_pT(t - 1)
                if t in (2, 4):
                    keys(1 + t // 2)
                if t >= 2:
                    a_oT(t - 2)
                if 1 <= t <= 4:
                    for n in range(SPLIT_AT[t - 1], SPLIT_AT[t]):
                        high_part(n)
                if t == TILES - 2:
                    ln_apply(2)
                if t == TILES - 1:
                    squares(0)
                    ln_T(2, banks[0])
                if t == TILES:
                    gate_exp(0)
            gate_T(0)

            def high(n):
                act.wait_ge(s("z_sb"), n + 1)
                if n >= ZSP:
                    act.wait_ge(s("zuse"), n - ZSP + 1)
                copy(zsp[:, n % ZSP, 0, :], z[:, n % ZR, :]).then_inc(s("z_hi"), 1)

            def qkv_out(h):
                act.wait_ge(s("zuse"), E0 * (h + 1))
                if h:
                    act.wait_ge(s("at_ps"), h)
                for i in range(3):
                    copy(qkvT[:, i, :], banks[2 + 3 * h + i][:, :]).then_inc(s("qkv_sb"), 1)

            def attn_v(h):
                act.wait_ge(s("v2_ps"), h + 1)
                if h:
                    act.wait_ge(s("ob_ps"), h)
                for i in range(2):
                    copy(vk[0:SEQ, 4 * i:4 * i + 4, :].rearrange("p b n -> p (b n)"),
                         banks[2 + 3 * h + i][0:SEQ, :]).then_inc(s("v2_sb"), 1)

            def attn_exp(h):
                act.wait_ge(s("at_d"), 5 * h + 2)
                A(att[:, :, :], att[:, :, :], ACT.Exp, scale=float(P) ** -0.5).then_inc(s("at_exp"), 1)

            def attn_T(h):
                act.wait_ge(s("aT_ps"), h + 1)
                if h:
                    act.wait_ge(s("ob_ps"), h)
                copy(attT[0:SEQ, :], banks[4 + 3 * h][0:SEQ, :]).then_inc(s("aT_sb"), 1)

            def attn_o(h):
                act.wait_ge(s("ob_ps"), h + 1)
                copy(oT[:, h, :], banks[2 + 3 * h][:, :]).then_inc(s("ob_sb"), 1)

            def out_T(h):
                act.wait_ge(s("zuse"), E0 * (3 + h))
                if h:
                    act.wait_ge(s("tr_ps"), h)
                copy(accT[:, :], banks[3 + 3 * h][:, :]).then_inc(s("acc_sb"), 1)

            def l_exp(h):
                act.wait_ge(s("la_d"), 5 * h + 4)
                A(att[:, :, :], att[:, :, :], ACT.Exp).then_inc(s("la_exp"), 1)

            def l_T(h):
                act.wait_ge(s("lT_ps"), h + 1)
                if h:
                    act.wait_ge(s("lo_ps"), h)
                copy(attT[0:SEQ, :], banks[3 + 3 * h][0:SEQ, :]).then_inc(s("lT_sb"), 1)

            def router_a(h):
                act.wait_ge(s("cl_sb"), 2 * h + 1)
                A(sg[:, TPH * h:TPH * (h + 1)], lgc[:, TPH * h:TPH * (h + 1), E1], ACT.Tanh,
                  scale=0.5).then_inc(s("ctanh"), 1)
                act.wait_ge(s("cd"), CD * h + CD_EXP)
                A(wex[:, :, :], wex[:, :, :], ACT.Exp).then_inc(s("cexp"), 1)

            def router_x(h):
                ts = slice(TPH * h, TPH * (h + 1))
                act.wait_ge(s("ln_out"), TPH * (6 + 2 * h))
                copy(xh[:, ts, 0, :], hn[:, ts, :]).then_inc(s("xh_hi"), 1)

            def router_b(h):
                act.wait_ge(s("xh_r"), h + 1)
                A(xh[:, TPH * h:TPH * (h + 1), 1, :], hn[:, TPH * h:TPH * (h + 1), :], ACT.Copy,
                  scale=LO_SCALE).then_inc(s("xh_lo"), 1)

            def shared(k):
                act.wait_ge(s("sh_ps"), k + 1)
                if k:
                    act.wait_ge(s("sh_a"), k)
                A(sth[:, :], banks[3 * (k // 2)][:, :], ACT.Tanh, scale=0.5).then_inc(s("sh_th"), 1)
            for n in range(4 * E0):
                if n < 2 * E0:
                    high(n)
                if n == 0:
                    ln_apply(3)
                if n == 1:
                    squares(1)
                if n == 4:
                    ln_T(3, banks[5])
                if n == 7:
                    gate_exp(1)
                if n == 10:
                    gate_T(1)
                if n == E0 + 1:
                    qkv_out(0)
                if n == E0 + 4:
                    attn_v(0)
                if n == E0 + 5:
                    attn_exp(0)
                if n == E0 + 6:
                    attn_T(0)
                if n == E0 + 12:
                    attn_o(0)
                if n == 2 * E0 + 1:
                    qkv_out(1)
                if n == 2 * E0 + 3:
                    attn_v(1)
                    attn_exp(1)
                if n == 2 * E0 + 6:
                    attn_T(1)
                    attn_o(1)
                if n == 3 * E0 + 1:
                    out_T(0)
                if n == 3 * E0 + 6:
                    ln_apply(4)
                    ln_T(4, banks[2])
                if n == 3 * E0 + 9:
                    l_exp(0)
                if n == 3 * E0 + 13:
                    l_T(0)
            out_T(1)
            ln_apply(5)
            ln_T(5, banks[2])
            ln_apply(6)
            router_x(0)
            ln_T(6, banks[5])
            router_a(0)
            l_exp(1)
            router_b(0)
            l_T(1)
            shared(0)
            ln_apply(7)
            router_x(1)
            ln_T(7, banks[5])
            shared(1)
            router_b(1)
            router_a(1)
            shared(2)
            shared(3)
            def disp_T(n):
                act.wait_ge(s("dT_ps"), n + 1)
                if n >= EPR:
                    act.wait_ge(s("sc_g"), n - EPR + 1)
                copy(dispT[:, n % EPR, :], banks[7][:, :].bitcast(F16)).then_inc(s("dT_sb"), 1)

            def high_out(g):
                act.wait_ge(s("dn_ps"), g + 1)
                act.wait_ge(s("ws_sb"), 3 * (g + 1))
                if g >= 2:
                    act.wait_ge(s("sc_g"), GRP * (g - 1))
                for n in range(GRP * g, GRP * (g + 1)):
                    A(esp[:, n % EPR, 0, :], banks[4][:, tile(n % GRP)], ACT.Copy,
                      scale=wslot[:, n:n + 1]).then_inc(s("dn_hi"), 1)

            def tokens(g):
                act.wait_ge(s("ga_ps"), 2 * (g + 1))
                if g:
                    act.wait_ge(s("xe_sb"), g)
                A(xlow[:, :], banks[1][:, :], ACT.Copy, scale=1.0 / LO_SCALE).then_inc(s("xl_sb"), 1)
            tokens(0)
            for g in range(NGRP):
                disp_T(GRP * g)
                act.wait_ge(s("up_ps"), g + 1)
                if g:
                    act.wait_ge(s("up_a"), g)
                A(th[:, :], banks[3][:, 0:256], ACT.Tanh, scale=0.5).then_inc(s("up_th"), 1)
                disp_T(GRP * g + 1)
                disp_T(GRP * g + 2)
                high_out(g)
                if g + 1 < NGRP:
                    tokens(g + 1)
            for h in range(HALVES):
                act.wait_ge(s("sc_g"), EP)
                copy(yT[:, half(h)], banks[5 + h][:, :]).then_inc(s("yT_sb"), 1)

        @block.vector
        def _(dve):
            V = nc.vector

            def ln(n):
                h = LN_HALF[n]
                if n:
                    dve.wait_ge(s("ln_aggr"), TPH * n)
                for t in range(TPH):
                    V.bn_stats(stats[:, t, :], xres[:, TPH * h + t, :]).then_inc(s("ln_stats"), 1)
                for t in range(TPH):
                    dve.wait_ge(s("ln_stats"), TPH * n + t + 1)
                    V.bn_aggr(mv[:, TPH * h + t, :], stats[:, t, :]).then_inc(s("ln_aggr"), 1)
                dve.wait_ge(s("ln_aggr"), TPH * (n + 1))
                if n:
                    dve.wait_ge(s("ln_rstd"), n)
                V.tensor_scalar(ve[:, :], mv[:, TPH * h:TPH * (h + 1), 1], EPS, None, ALU.add).then_inc(s("ln_var"), 1)
                V.tensor_scalar(negm[:, TPH * h:TPH * (h + 1)], mv[:, TPH * h:TPH * (h + 1), 0], -1.0, None,
                                ALU.mult).then_inc(s("ln_neg"), 1)

            def keys(c):
                dve.wait_ge(s("kT_sb"), c // 2 + 1)
                for hd in range(KD):
                    V.tensor_scalar(kexp[:, c, :, hd, :],
                                    kT[:, 4 * SEQ * c:4 * SEQ * (c + 1)].rearrange("p (b k) -> p b k", k=SEQ),
                                    pairm[:, hd:hd + 1], None, ALU.mult).then_inc(s("kexp_d"), 1)

            dve.wait_ge(s("consts"), 2)
            for out, eye in ((headm[:, :], ident[:, :].rearrange("p (h d) -> p h d", d=HD)),
                             (halfm[:, :], ident[:, :].rearrange("p (h d) -> p h d", h=2)),
                             (parity[:, :], ident[:, :].rearrange("p (c e) -> p e c", e=2)),
                             (selc[:, :], ident[0:3 * E0, 0:3 * E0].rearrange("p (k e) -> p e k", e=E0))):
                V.tensor_reduce(out, eye, AX.X, ALU.add).then_inc(s("sel"), 1)
            V.tensor_copy(ident16[:, :], ident[:, :]).then_inc(s("sel"), 1)
            V.tensor_copy(identb[:, :], ident[:, :]).then_inc(s("sel"), 1)
            dve.wait_ge(s("sel"), 4)
            V.tensor_reduce(pairm[:, :], headm[:, :].rearrange("p (j e) -> p j e", e=2), AX.X, ALU.add).then_inc(s("sel"), 1)
            V.tensor_reduce(oddm[:, :], headm[:, :].rearrange("p (j e) -> p e j", e=2), AX.X, ALU.add).then_inc(s("sel"), 1)
            V.tensor_copy(selw[:, :, :], selc[:, :, None].to_broadcast([3 * E0, E0, P])).then_inc(s("sel"), 1)
            dve.wait_ge(ld["x"], 16)
            ln(0)
            dve.wait_ge(s("sel"), NSEL)
            keys(0)
            ln(1)
            V.tensor_copy(vblk[:, :, :, :, 8], halfm[:, None, :, None].to_broadcast([P, BATCH * CHUNKS, 2, 2]))\
                .then_inc(s("v_sb"), 1)
            for k in range(4):
                dve.wait_ge(s("v_ps"), k + 1)
                for i in range(2):
                    V.tensor_scalar(vblk[:, 4 * CHUNKS * k:4 * CHUNKS * (k + 1), i, :, 0:HD],
                                    banks[2 + k][:, :].rearrange("p (n i e d) -> p n i e d", i=2, e=2, d=HD)[:, :, i, :, :],
                                    halfm[:, i:i + 1], None, ALU.mult).then_inc(s("v_sb"), 1)
            dve.wait_ge(ld["misc"], 5 * 16)
            V.tensor_tensor(sim2[:, :], simm[:, :], simm[:, :], ALU.mult).then_inc(s("sim2"), 1)

            def a_soft(t):
                b = 2 * (t % 2)
                if t >= 2:
                    dve.wait_ge(s("pT_ps"), t - 1)
                    dve.wait_ge(s("sc_sub"), 2 * (t - 1))
                for k in range(2):
                    dve.wait_ge(s("sc_ps"), 2 * t + k + 1)
                    V.tensor_reduce(smax[:, t % 2, 8 * k:8 * k + 8],
                                    banks[b + k][:, :].rearrange("p (h k) -> p h k", k=SEQ),
                                    AX.X, ALU.max).then_inc(s("sc_max"), 1)
                    dve.wait_ge(s("sc_max"), 2 * t + 1 + k)
                    V.tensor_tensor(prob[:, t % 2, 512 * k:512 * (k + 1)].rearrange("p (h k) -> p h k", k=SEQ),
                                    banks[b + k][:, :].rearrange("p (h k) -> p h k", k=SEQ),
                                    smax[:, t % 2, 8 * k:8 * k + 8, None].to_broadcast([P, 8, SEQ]),
                                    ALU.subtract).then_inc(s("sc_sub"), 1)

            def a_norm(t):
                dve.wait_ge(s("pv_ps"), t + 1)
                if t:
                    dve.wait_ge(s("pv_sb"), 2 * t)
                po = banks[6][:, 0:2 * HEADS * 9].rearrange("p (n e d) -> p n e d", e=2, d=9)
                for i in range(2):
                    V.reciprocal(rsum[seq(i), :], po[seq(i), :, i, 8]).then_inc(s("pv_rec"), 1)
                if t >= 1:
                    dve.wait_ge(s("oT_ps"), t)
                for i in range(2):
                    dve.wait_ge(s("pv_rec"), 2 * t + i + 1)
                    V.tensor_tensor(ohead[seq(i), :].rearrange("p (n d) -> p n d", d=HD), po[seq(i), :, i, 0:HD],
                                    rsum[seq(i), :, None].to_broadcast([SEQ, HEADS, HD]),
                                    ALU.mult).then_inc(s("pv_sb"), 1)

            def a_res(t):
                dve.wait_ge(s("y_ps"), t + 1)
                dve.wait_ge(s("xb"), 2)
                V.scalar_tensor_tensor(xres[:, t, :], banks[7][:, P:2 * P], tg[:, 0:1], xres[:, t, :],
                                       ALU.mult, ALU.add).then_inc(s("y_out"), 1)

            gdn = [0]

            def gstep(ins):
                ins.then_inc(s("gd"), 1)
                gdn[0] += 1

            def gwait():
                dve.wait_ge(s("gd"), gdn[0])

            def gate_a(h):
                b3 = banks[LG_BANK[h]]
                dve.wait_ge(s("rnorm"), 2 * h + 2)
                dve.wait_ge(s("lg_ps"), h + 1)
                dve.wait_ge(s("g_dve"), 1)
                gwait()
                for t in range(TPH):
                    gstep(V.scalar_tensor_tensor(lg[:, t, :], b3[:, E0 * t:E0 * (t + 1)], rn[:, t:t + 1], sig0[:, :],
                                                 ALU.mult, ALU.subtract))
                gwait()
                for t in range(TPH):
                    gstep(V.max(top[:, t, :], lg[:, t, :]))
                gstep(V.tensor_scalar(ga[:, :, :], lg[:, :, :], 0.0, None, ALU.is_gt))
                gstep(V.tensor_scalar(gb[:, :, :], lg[:, :, :], 0.0, None, ALU.max))
                gwait()
                for t in range(TPH):
                    gstep(V.max_index(topi[:, t, :], top[:, t, :], lg[:, t, :]))
                gstep(V.tensor_scalar(g1[:, :], top[:, :, 0], 0.0, None, ALU.is_le))
                gstep(V.tensor_scalar(g2[:, :], top[:, :, 0], 0.0, None, ALU.max))
                gwait()
                gstep(V.tensor_copy(topf[:, :, :], topi[:, :, :]))
                gstep(V.tensor_tensor(gc[:, :, :], gb[:, :, :], g2[:, :, None].to_broadcast([P, TPH, E0]),
                                      ALU.subtract))
                assert gdn[0] == GD * h + GD_EXP

            def gate_b(h):
                gwait()
                gstep(V.tensor_tensor(gb[:, :, :], io16[:, None, :].to_broadcast([P, TPH, E0]),
                                      topf[:, :, 0:1].to_broadcast([P, TPH, E0]), ALU.is_equal))
                gstep(V.tensor_tensor(fbk[:, :, :], io16[:, None, :].to_broadcast([P, TPH, E0]),
                                      topf[:, :, 1:2].to_broadcast([P, TPH, E0]), ALU.is_equal))
                gwait()
                gstep(V.tensor_tensor(gb[:, :, :], gb[:, :, :], fbk[:, :, :], ALU.add))
                gwait()
                gstep(V.tensor_tensor(gb[:, :, :], gb[:, :, :], g1[:, :, None].to_broadcast([P, TPH, E0]), ALU.mult))
                gwait()
                gstep(V.tensor_tensor(gb[:, :, :], gb[:, :, :], ga[:, :, :], ALU.add))
                gwait()
                dve.wait_ge(s("g_act"), 2 + h)
                gstep(V.tensor_tensor(gb[:, :, :], gb[:, :, :], gc[:, :, :], ALU.mult))
                gwait()
                gstep(V.tensor_reduce(g1[:, :], gb[:, :, :], AX.X, ALU.add))
                gwait()
                gstep(V.reciprocal(g2[:, :], g1[:, :]))
                gwait()
                gstep(V.tensor_tensor(gb[:, :, :], gb[:, :, :], g2[:, :, None].to_broadcast([P, TPH, E0]), ALU.mult))
                part = [w3[:, TPH * h:TPH * (h + 1), i * E0:(i + 1) * E0] for i in range(3)]
                gwait()
                gstep(V.tensor_copy(part[0], gb[:, :, :]))
                gwait()
                gstep(V.tensor_tensor(gb[:, :, :], gb[:, :, :], part[0], ALU.subtract))
                gwait()
                gstep(V.tensor_copy(part[1], gb[:, :, :]))
                gwait()
                V.tensor_tensor(part[2], gb[:, :, :], part[1], ALU.subtract).then_inc(s("w3"), 1)
                assert gdn[0] == GD * (h + 1), gdn[0]

            for t in range(TILES + 2):
                if t < TILES:
                    a_soft(t)
                if t == TILES:
                    gate_a(0)
                if 1 <= t <= TILES:
                    a_norm(t - 1)
                if t >= 2:
                    a_res(t - 2)
                if t == 1:
                    dve.wait_ge(s("sn_ps"), 1)
                    V.tensor_scalar(sim2[:, :], banks[7][:, 256:256 + E0], TINY, None, ALU.max).then_inc(s("sn_pre"), 1)
                if t == 0:
                    dve.wait_ge(s("tanh_g"), 1)
                    V.tensor_scalar(bo[:, :], bo[:, :], tg[:, 0:1], None, ALU.mult).then_inc(s("xb"), 1)
                    dve.wait_ge(s("g_act"), 1)
                    V.tensor_scalar(sig0[:, :], sig0[:, :], 0.5, 0.5, ALU.mult, ALU.add).then_inc(s("g_dve"), 1)
                    dve.wait_ge(s("xb"), 1)
                    dve.wait_ge(s("ln_out"), TILES)
                    V.tensor_tensor(xres[:, :, :], xres[:, :, :], bo[:, None, :].to_broadcast([P, TILES, P]),
                                    ALU.add).then_inc(s("xb"), 1)
                if t in (0, 2, 4):
                    keys(1 + t // 2)
                if t == TPH + 1:
                    dve.wait_ge(s("y_out"), TPH)
                    ln(2)
                if t == TILES:
                    gate_b(0)
            dve.wait_ge(s("y_out"), TILES)
            ln(3)

            def scaled(n):
                dve.wait_ge(s("wb_ps"), n + 1)
                if ZR <= n < 2 * E0 + ZR:
                    dve.wait_ge(s("z_lo"), n - ZR + 1)
                if n >= 2 * E0 + ZR:
                    dve.wait_ge(s("zuse"), n - ZR + 1)
                h = (n // E0) % 2
                if n in (0, E0):
                    dve.wait_ge(s("hT_sb"), 3 + h)
                if n in (2 * E0, 3 * E0):
                    dve.wait_ge(s("ob_sb"), h + 1)
                src = hT[:, half(h)] if n < 2 * E0 else oT[:, h, :]
                V.tensor_tensor(z[:, n % ZR, :], banks[spread_bank(n)][:, :], src, ALU.mult).then_inc(s("z_sb"), 1)

            def low(n):
                dve.wait_ge(s("z_hi"), n + 1)
                V.tensor_tensor(zsp[:, n % ZSP, 1, :], z[:, n % ZR, :], zsp[:, n % ZSP, 0, :].bitcast(F32),
                                ALU.subtract).then_inc(s("z_lo"), 1)

            def attn_a(h):
                a = banks[4 + 3 * h][:, 0:TPH * SEQ].rearrange("p (t k) -> p t k", k=SEQ)
                n = 5 * h
                dve.wait_ge(s("at_ps"), h + 1)
                if h:
                    dve.wait_ge(s("at_d"), n)
                V.tensor_reduce(amax[:, :], a, AX.X, ALU.max).then_inc(s("at_d"), 1)
                dve.wait_ge(s("at_d"), n + 1)
                if h:
                    dve.wait_ge(s("aT_ps"), h)
                V.tensor_tensor(att[:, :, :], a, amax[:, :, None].to_broadcast([P, TPH, SEQ]),
                                ALU.subtract).then_inc(s("at_d"), 1)

            def attn_b(h):
                n = 5 * h
                dve.wait_ge(s("at_exp"), h + 1)
                V.tensor_reduce(asum[:, :], att[:, :, :], AX.X, ALU.add).then_inc(s("at_d"), 1)
                dve.wait_ge(s("at_d"), n + 3)
                V.reciprocal(amax[:, :], asum[:, :]).then_inc(s("at_d"), 1)
                dve.wait_ge(s("at_d"), n + 4)
                V.tensor_tensor(att[:, :, :], att[:, :, :], amax[:, :, None].to_broadcast([P, TPH, SEQ]),
                                ALU.mult).then_inc(s("at_d"), 1)

            def residual(h):
                dve.wait_ge(s("tr_ps"), h + 1)
                for t in range(TPH):
                    V.scalar_tensor_tensor(xres[:, TPH * h + t, :], banks[4 + 3 * h][:, tile(t)], tg[:, 2:3],
                                           xres[:, TPH * h + t, :], ALU.mult, ALU.add).then_inc(s("tr_out"), 1)
                dve.wait_ge(s("tr_out"), TPH * (h + 1))

            def mask():
                dve.wait_ge(ld["mask"], 32)
                V.tensor_copy(maskf[:, :, :], maski[:, :, :]).then_inc(s("mask_f"), 1)
                dve.wait_ge(s("mask_f"), 1)
                V.tensor_scalar(maskf[:, :, :], maskf[:, :, :], 0.0, None, ALU.not_equal).then_inc(s("mask_f"), 1)
                dve.wait_ge(s("mask_f"), 2)
                V.tensor_scalar(maskn[:, :, :], maskf[:, :, :], -1.0, NEG, ALU.add, ALU.mult).then_inc(s("mask_f"), 1)

            def l_soft(h):
                n = 5 * h
                a = banks[4 + 3 * h][:, 0:TPH * SEQ].rearrange("p (t k) -> p t k", k=SEQ)
                ts = slice(TPH * h, TPH * (h + 1))
                dve.wait_ge(s("la_ps"), h + 1)
                dve.wait_ge(s("mask_f"), 3)
                if h:
                    dve.wait_ge(s("lT_ps"), h)
                V.tensor_tensor(att[:, :, :], a, maskf[:, ts, :], ALU.mult).then_inc(s("la_d"), 1)
                dve.wait_ge(s("la_d"), n + 1)
                V.tensor_tensor(att[:, :, :], att[:, :, :], maskn[:, ts, :], ALU.add).then_inc(s("la_d"), 1)
                dve.wait_ge(s("la_d"), n + 2)
                V.tensor_reduce(amax[:, :], att[:, :, :], AX.X, ALU.max).then_inc(s("la_d"), 1)
                dve.wait_ge(s("la_d"), n + 3)
                V.tensor_tensor(att[:, :, :], att[:, :, :], amax[:, :, None].to_broadcast([P, TPH, SEQ]),
                                ALU.subtract).then_inc(s("la_d"), 1)

            def l_sum(h):
                dve.wait_ge(s("la_exp"), h + 1)
                V.tensor_reduce(asum[:, :], att[:, :, :], AX.X, ALU.add).then_inc(s("la_d"), 1)
                dve.wait_ge(s("la_d"), 5 * h + 5)
                V.reciprocal(amax[:, :], asum[:, :]).then_inc(s("lrec"), 1)
                dve.wait_ge(s("lrec"), 2 * h + 1)
                V.tensor_scalar(asum[:, :], amax[:, :], tg[:, 1:2], None, ALU.mult).then_inc(s("lrec"), 1)

            def l_out(h):
                dve.wait_ge(s("lrec"), 2 * h + 2)
                dve.wait_ge(s("lo_ps"), h + 1)
                for t in range(TPH):
                    V.scalar_tensor_tensor(xres[:, TPH * h + t, :], banks[2 + 3 * h][:, tile(t)], asum[:, t:t + 1],
                                           xres[:, TPH * h + t, :], ALU.mult, ALU.add).then_inc(s("lo_out"), 1)
                dve.wait_ge(s("lo_out"), TPH * (h + 1))

            cdn = [0]

            def cstep(ins):
                ins.then_inc(s("cd"), 1)
                cdn[0] += 1

            def cwait():
                dve.wait_ge(s("cd"), cdn[0])

            def router_a(h):
                ts = slice(TPH * h, TPH * (h + 1))
                dve.wait_ge(s("cl_ps"), h + 1)
                V.tensor_copy(lgc[:, ts, :], banks[3 + 3 * h][:, 0:TPH * (E1 + 1)]
                              .rearrange("p (t e) -> p t e", t=TPH)).then_inc(s("cl_sb"), 1)
                dve.wait_ge(s("cl_sb"), 2 * h + 1)
                cwait()
                for t in range(TPH):
                    cstep(V.max(topc[:, t, :], lgc[:, TPH * h + t, 0:E1]))
                cwait()
                for t in range(TPH):
                    cstep(V.match_replace(rep[:, t, :], topc[:, t, :], lgc[:, TPH * h + t, 0:E1], LOW))
                cstep(V.tensor_tensor(wex[:, :, :], lgc[:, ts, 0:E1], topc[:, :, 0:1].to_broadcast([P, TPH, E1]),
                                      ALU.subtract))
                assert cdn[0] == CD * h + CD_EXP
                cwait()
                V.tensor_tensor(chosen[:, ts, :], rep[:, :, :], lgc[:, ts, 0:E1],
                                ALU.not_equal).then_inc(s("cl_sb"), 1)

            def router_pos(h):
                ts = slice(TPH * h, TPH * (h + 1))
                dve.wait_ge(s("cl_sb"), 2 * h + 2)
                dve.wait_ge(s("pos_ps"), h + 1)
                if h:
                    dve.wait_ge(s("pos_sb"), h)
                V.scalar_tensor_tensor(post[:, :, :], chosen[:, ts, :], -BIG,
                                       banks[4 + 3 * h][:, 0:TPH * E1].rearrange("p (t e) -> p t e", t=TPH),
                                       ALU.mult, ALU.add).then_inc(s("post"), 1)
                dve.wait_ge(s("post"), h + 1)
                V.tensor_scalar(pos16[:, :, ts, :], post[:, :, :].rearrange("p t (g e) -> p g t e", e=2 * DG), BIG,
                                float(2 * CAP), ALU.add, ALU.min).then_inc(s("pos_sb"), 1)

            def router_b(h):
                ts = slice(TPH * h, TPH * (h + 1))
                dve.wait_ge(s("cl_sb"), 2 * h + 2)
                dve.wait_ge(s("cexp"), h + 1)
                cstep(V.tensor_tensor(wex[:, :, :], wex[:, :, :], chosen[:, ts, :], ALU.mult))
                cwait()
                cstep(V.tensor_reduce(csum[:, :], wex[:, :, :], AX.X, ALU.add))
                cwait()
                cstep(V.reciprocal(g1[:, :], csum[:, :]))
                cwait()
                cstep(V.tensor_tensor(wex[:, :, :], wex[:, :, :], g1[:, :, None].to_broadcast([P, TPH, E1]), ALU.mult))
                cwait()
                cstep(V.tensor_copy(wc3[:, ts, :, 0], wex[:, :, :]))
                cwait()
                cstep(V.tensor_tensor(wres[:, :, :], wex[:, :, :], wc3[:, ts, :, 0], ALU.subtract))
                cwait()
                cstep(V.tensor_copy(wc3[:, ts, :, 1], wres[:, :, :]))
                cwait()
                cstep(V.tensor_tensor(wc3[:, ts, :, 2], wres[:, :, :], wc3[:, ts, :, 1], ALU.subtract))
                assert cdn[0] == CD * (h + 1), cdn[0]

            def dispatch(g):
                if g == 0:
                    dve.wait_ge(s("pos_sb"), 2)
                V.tensor_tensor(disp[:, g, :, :, :].rearrange("p t q (c e) -> p (t q) c e", e=2),
                                slotc[:, None, :, :].to_broadcast([P, TILES * DG, CAP, 2]),
                                pos16[:, g, :, :].rearrange("p t (q e) -> p (t q) e", e=2)[:, :, None, :]
                                .to_broadcast([P, TILES * DG, CAP, 2]), ALU.is_equal).then_inc(s("disp"), 1)

            def shared(k):
                h, f = k // 2, k % 2
                dve.wait_ge(s("sh_th"), k + 1)
                if h and f == 0:
                    dve.wait_ge(s("sd_ps"), h)
                V.scalar_tensor_tensor(shg[:, f, :], sth[:, :], 1.0, banks[3 * h][:, :], ALU.add,
                                       ALU.mult).then_inc(s("sh_a"), 1)
                dve.wait_ge(s("sh_a"), k + 1)
                V.scalar_tensor_tensor(shg[:, f, :], shg[:, f, :], 0.5, banks[3 * h + 1][:, :], ALU.mult,
                                       ALU.mult).then_inc(s("sh_act"), 1)

            def shared_gate(h):
                ts = slice(TPH * h, TPH * (h + 1))
                dve.wait_ge(s("ctanh"), h + 1)
                V.tensor_scalar(sg[:, ts], sg[:, ts], 0.5, 0.5, ALU.mult, ALU.add).then_inc(s("sgv"), 1)
                dve.wait_ge(s("sgv"), 2 * h + 1)
                V.tensor_scalar(sg[:, ts], sg[:, ts], tg[:, 3:4], None, ALU.mult).then_inc(s("sgv"), 1)

            def shared_out(h):
                dve.wait_ge(s("sd_ps"), h + 1)
                dve.wait_ge(s("sgv"), 2 * h + 2)
                for t in range(TPH):
                    T = TPH * h + t
                    V.scalar_tensor_tensor(xres[:, T, :], banks[2 + 3 * h][:, tile(t)], sg[:, T:T + 1], xres[:, T, :],
                                           ALU.mult, ALU.add).then_inc(s("sd_out"), 1)
            for n in range(4 * E0):
                scaled(n)
                if 1 <= n <= 2 * E0:
                    low(n - 1)
                if n == 6:
                    gate_a(1)
                if n == 8:
                    gate_b(1)
                if n == 14:
                    mask()
                if n == E0 + 3:
                    attn_a(0)
                if n == E0 + 6:
                    attn_b(0)
                if n == 2 * E0 + 6:
                    attn_a(1)
                if n == 2 * E0 + 8:
                    attn_b(1)
                if n == 3 * E0 + 3:
                    residual(0)
                    ln(4)
                if n == 3 * E0 + 10:
                    l_soft(0)
                if n == 3 * E0 + 11:
                    l_sum(0)
                if n == 3 * E0 + 15:
                    l_out(0)
                    ln(5)
            residual(1)
            ln(6)
            router_a(0)
            l_soft(1)
            l_sum(1)
            router_pos(0)
            router_b(0)
            shared(0)
            l_out(1)
            ln(7)
            shared_gate(0)
            shared(1)
            router_a(1)
            router_pos(1)
            dispatch(0)
            router_b(1)
            shared(2)
            shared_out(0)
            dispatch(1)
            shared_gate(1)
            shared(3)
            shared_out(1)
            dispatch(2)
            dve.wait_ge(s("act0"), 1)

            def slot_weights(g):
                qs = slice(GRP * g, GRP * (g + 1))
                dve.wait_ge(s("ws_ps"), g + 1)
                V.tensor_reduce(wslot2[:, qs, :], banks[2][:, 0:6 * GRP].rearrange("p (q e k) -> p q e k", e=2, k=3),
                                AX.X, ALU.add).then_inc(s("ws_sb"), 1)
                dve.wait_ge(s("ws_sb"), 3 * g + 1)
                V.tensor_scalar(wslot[:, qs], wslot2[:, qs, 0], parity[:, 0:1], None, ALU.mult).then_inc(s("ws_sb"), 1)
                dve.wait_ge(s("ws_sb"), 3 * g + 2)
                V.scalar_tensor_tensor(wslot[:, qs], wslot2[:, qs, 1], parity[:, 1:2], wslot[:, qs], ALU.mult,
                                       ALU.add).then_inc(s("ws_sb"), 1)

            def low_out(g):
                dve.wait_ge(s("dn_hi"), GRP * (g + 1))
                dve.wait_ge(s("ws_sb"), 3 * (g + 1))
                for n in range(GRP * g, GRP * (g + 1)):
                    V.scalar_tensor_tensor(esp[:, n % EPR, 1, :], banks[4][:, tile(n % GRP)], wslot[:, n:n + 1],
                                           esp[:, n % EPR, 0, :].bitcast(F32), ALU.mult,
                                           ALU.subtract).then_inc(s("dn_lo"), 1)

            def disp_T(n):
                dve.wait_ge(s("dT_ps"), n + 1)
                if n >= EPR:
                    dve.wait_ge(s("sc_g"), n - EPR + 1)
                V.tensor_copy(dispT[:, n % EPR, :], banks[7][:, :].bitcast(F16)).then_inc(s("dT_sb"), 1)

            def tokens(g):
                dve.wait_ge(s("xl_sb"), g + 1)
                if g >= 2:
                    dve.wait_ge(s("up_ps"), g - 1)
                V.tensor_tensor(xeT[:, g % 2, :, :].rearrange("p q n -> p (q n)"), banks[0][:, :], xlow[:, :],
                                ALU.add).then_inc(s("xe_sb"), 1)
            tokens(0)
            slot_weights(0)
            for g in range(NGRP):
                r = g % 2
                dve.wait_ge(s("up_th"), g + 1)
                if g:
                    dve.wait_ge(s("up_act"), 2 * g)
                V.scalar_tensor_tensor(ab[:, :], th[:, :], 1.0, banks[3][:, 0:256], ALU.add,
                                       ALU.mult).then_inc(s("up_a"), 1)
                dve.wait_ge(s("up_a"), g + 1)
                if g >= 2:
                    dve.wait_ge(s("dn_ps"), g - 1)
                for i in range(2):
                    V.scalar_tensor_tensor(actb[seq(i), r, :, :, i],
                                           ab[seq(i), :].rearrange("p (q c) -> p q c", q=GRP), 0.5,
                                           banks[3][seq(i), 256:512].rearrange("p (q c) -> p q c", q=GRP),
                                           ALU.mult, ALU.mult).then_inc(s("up_act"), 1)
                if 2 * g + 3 < EP // DG:
                    dispatch(2 * g + 3)
                low_out(g)
                disp_T(GRP * g + 3)
                if g + 1 < NGRP:
                    tokens(g + 1)
                    slot_weights(g + 1)
                if 2 * g + 4 < EP // DG:
                    dispatch(2 * g + 4)
            for t in range(TILES):
                dve.wait_ge(s("yt_ps"), t // TPH + 1)
                dve.wait_ge(s("sd_out"), TILES)
                V.scalar_tensor_tensor(xres[:, t, :], banks[t // TPH][:, tile(t % TPH)], tg[:, 3:4], xres[:, t, :],
                                       ALU.mult, ALU.add).then_inc(s("fin"), 1)

        @block.tensor
        def _(pe):
            def mm(out, lhsT, rhs, start=True, stop=True):
                return nc.tensor.matmul(out, lhsT, rhs, start=start, stop=stop)

            pe.wait_ge(ld["ctxT"], 16)
            pe.wait_ge(ld["wkv"], 2 * 16)
            for h in range(HALVES):
                mm(banks[h][:, :], wk[:, :], ctxT[:, half(h)]).then_inc(s("kT_ps"), 1)
            def values(k):
                for j in range(4):
                    b = 4 * k + j
                    for i in range(2):
                        last = mm(banks[2 + k][seq(i), tile(j)], ctxT[:, seq(b)], wv[:, :])
                last.then_inc(s("v_ps"), 1)

            def lnT(n, bank):
                h = LN_HALF[n]
                for t in range(TPH):
                    pe.wait_ge(s("ln_out"), TPH * n + t + 1)
                    last = nc.tensor.transpose(bank[:, tile(t)], hn[:, TPH * h + t, :], ident[:, :])
                last.then_inc(s("hT_ps"), 1)
            def queries(h):
                pe.wait_ge(s("hT_sb"), h + 1)
                pe.wait_ge(s("kT_sb"), 1)
                mm(banks[6 * h][:, :], wq[:, :], hT[:, half(h)]).then_inc(s("q_ps"), 1)
            values(0)
            values(1)
            pe.wait_ge(s("consts"), NCONST)
            pe.wait_ge(ld["wqo"], 3 * 16)
            lnT(0, banks[6])
            values(2)
            queries(0)
            values(3)

            def scores(t, k):
                n = t // 2 + 1
                b = 2 * t + k
                pe.wait_ge(s("kexp_d"), KD * n)
                pe.wait_ge(s("kexp_a"), (PAIRS - KD) * n)
                pe.wait_ge(s("q_sb"), 2 * (t // TPH + 1))
                if t == 0:
                    pe.wait_ge(s("kT_sb"), k + 1)
                elif t == 1:
                    pe.wait_ge(s("v_sb"), 5)
                else:
                    pe.wait_ge(s("sc_sub"), 2 * (t - 2) + k + 1)
                mm(banks[2 * (t % 2) + k][:, :], qexp[:, b, :, :].rearrange("p e q -> p (e q)"),
                   kexp[:, b // 4, b % 4, :, :].rearrange("p j k -> p (j k)")).then_inc(s("sc_ps"), 1)

            def probs_T(t):
                pe.wait_ge(s("sc_exp"), t + 1)
                if t == 0:
                    pe.wait_ge(s("v_sb"), 9)
                else:
                    pe.wait_ge(s("pT_sb"), 2 * t)
                for j in range(PAIRS):
                    last = nc.tensor.transpose(banks[4 + j // 4][:, tile(j % 4)], prob[:, t % 2, tile(j)], ident[:, :])
                last.then_inc(s("pT_ps"), 1)

            def pv(t):
                pe.wait_ge(s("pT_sb"), 2 * (t + 1))
                if t:
                    pe.wait_ge(s("pv_sb"), 2 * t)
                for j in range(PAIRS):
                    last = mm(banks[6][:, 36 * j:36 * j + 36], probT[:, tile(j)],
                              vblk[:, 2 * CHUNKS * t + j, :, :, :].rearrange("p i e d -> p (i e d)"))
                last.then_inc(s("pv_ps"), 1)

            def heads_T(t):
                pe.wait_ge(s("pv_sb"), 2 * (t + 1))
                if t:
                    pe.wait_ge(s("y_out"), t)
                else:
                    pe.wait_ge(s("sn_pre"), 1)
                nc.tensor.transpose(banks[7][:, 0:P], ohead[:, :], ident[:, :]).then_inc(s("oT_ps"), 1)

            def project(t):
                pe.wait_ge(s("oT_sb"), t + 1)
                for k in range(2):
                    for i in range(2):
                        last = mm(banks[7][seq(k), P:2 * P], oheadT[seq(k), seq(i)], wo[seq(k), i, :], start=i == 0,
                                  stop=i == 1)
                last.then_inc(s("y_ps"), 1)

            def gate_lg(h):
                pe.wait_ge(s("hT_sb"), 3 + h)
                pe.wait_ge(s("sn"), 1)
                for t in range(TPH):
                    last = mm(banks[LG_BANK[h]][:, E0 * t:E0 * (t + 1)], hT[:, tile(TPH * h + t)], simm[:, :])
                last.then_inc(s("lg_ps"), 1)

            def gate_T(h):
                pe.wait_ge(s("w3"), h + 1)
                out = banks[WT_BANK[h]][0:3 * E0, 0:HT // 2].bitcast(BF16)
                for t in range(TPH):
                    last = nc.tensor.transpose(out[:, tile(t)], w3[:, TPH * h + t, :], identb[:, :])
                last.then_inc(s("wT_ps"), 1)

            for t in range(TILES + 2):
                if t < TILES:
                    scores(t, 0)
                if t < 2:
                    scores(t, 1)
                if t == 0:
                    lnT(1, banks[7])
                    queries(1)
                if t == 1:
                    pe.wait_ge(s("sim2"), 1)
                    mm(banks[7][:, 256:256 + E0], ones[:, :], sim2[:, :]).then_inc(s("sn_ps"), 1)
                if 1 <= t <= TILES:
                    probs_T(t - 1)
                if t >= 2:
                    heads_T(t - 2)
                if 2 <= t < TILES:
                    scores(t, 1)
                if t == TILES - 1:
                    pe.wait_ge(s("sc_sub"), 2 * TILES - 2)
                    lnT(2, banks[0])
                if 1 <= t <= TILES:
                    pv(t - 1)
                if t >= 2:
                    project(t - 2)
                if t == TILES - 1:
                    gate_lg(0)
            gate_T(0)

            def spread(n):
                h = (n // E0) % 2
                if n == 0:
                    pe.wait_ge(s("sel"), NSEL)
                pe.wait_ge(s("wT_sb"), min(n // E0, 1) + 1)
                if n == 1:
                    pe.wait_ge(s("gd"), GD)
                last_use = spread_before(n)
                if last_use is not None:
                    pe.wait_ge(s("z_sb"), last_use + 1)
                elif n >= 2 * E0:
                    pe.wait_ge(s("ob_sb"), (n - E0) // E0)
                    pe.wait_ge(s("aT_sb"), (n - E0) // E0)
                mm(banks[spread_bank(n)][:, :], selw[:, n % E0, :], wT[:, half(h)]).then_inc(s("wb_ps"), 1)

            def experts(n):
                h, e = (n // E0) % 2, n % E0
                base = 2 + 3 * h
                cols = slice(e * P, (e + 1) * P)
                if n < 2 * E0:
                    pe.wait_ge(s("z_lo"), n + 1)
                    if n == 0:
                        pe.wait_ge(s("split_lo"), 3 * NSPLIT)
                    if n == E0:
                        pe.wait_ge(s("gd"), 2 * GD)
                    for i in range(3):
                        out = banks[base + i][:, :]
                        mm(out, wsp[:, 0, i, cols], zsp[:, n % ZSP, 0, :], start=e == 0, stop=False)
                        mm(out, wsp[:, 0, i, cols], zsp[:, n % ZSP, 1, :], start=False, stop=False)
                        last = mm(out, wsp[:, 1, i, cols], zsp[:, n % ZSP, 0, :], start=False, stop=e == E0 - 1)
                else:
                    pe.wait_ge(s("z_sb"), n + 1)
                    if e == 0:
                        pe.wait_ge(ld["oexp"], 16)
                    last = mm(banks[base + 1][:, :], oexp[:, e, :], z[:, n % ZR, :], start=e == 0, stop=e == E0 - 1)
                last.then_inc(s("zuse"), 1)

            def attn_a(h):
                base = 2 + 3 * h
                pe.wait_ge(s("qkv_sb"), 3 * (h + 1))
                for i in range(8):
                    last = nc.tensor.transpose(banks[base + i // 4][0:SEQ, tile(i % 4)], qkvT[:, 2, seq(i)],
                                               ident[:, :])
                last.then_inc(s("v2_ps"), 1)
                for t in range(TPH):
                    for i in range(2):
                        last = mm(banks[base + 2][seq(i), SEQ * t:SEQ * (t + 1)], qkvT[:, 0, seq(2 * t + i)],
                                  qkvT[:, 1, seq(2 * t + i)])
                last.then_inc(s("at_ps"), 1)

            def attn_T(h):
                pe.wait_ge(s("at_d"), 5 * (h + 1))
                for t in range(TPH):
                    last = nc.tensor.transpose(banks[4 + 3 * h][0:SEQ, tile(t)], att[:, t, :], ident[:, :])
                last.then_inc(s("aT_ps"), 1)

            def attn_o(h):
                pe.wait_ge(s("aT_sb"), h + 1)
                pe.wait_ge(s("v2_sb"), 2 * (h + 1))
                for b in range(8):
                    last = mm(banks[2 + 3 * h][:, seq(b)], vk[0:SEQ, b, :], attT[0:SEQ, seq(b)])
                last.then_inc(s("ob_ps"), 1)

            def out_T(h):
                pe.wait_ge(s("acc_sb"), h + 1)
                for t in range(TPH):
                    last = nc.tensor.transpose(banks[4 + 3 * h][:, tile(t)], accT[:, tile(t)], ident[:, :])
                last.then_inc(s("tr_ps"), 1)

            def l_scores(h):
                pe.wait_ge(s("hT_sb"), 5 + 2 * h)
                pe.wait_ge(s("tr_out"), TPH * (h + 1))
                for t in range(TPH):
                    for i in range(2):
                        b = 2 * (TPH * h + t) + i
                        last = mm(banks[4 + 3 * h][seq(i), SEQ * t:SEQ * (t + 1)], hT[:, seq(b)], ctxT[:, seq(b)])
                last.then_inc(s("la_ps"), 1)

            def l_T(h):
                pe.wait_ge(s("la_exp"), h + 1)
                for t in range(TPH):
                    last = nc.tensor.transpose(banks[3 + 3 * h][0:SEQ, tile(t)], att[:, t, :], ident[:, :])
                last.then_inc(s("lT_ps"), 1)

            def l_values(h):
                pe.wait_ge(s("lT_sb"), h + 1)
                pe.wait_ge(ld["ctxk"], 16)
                for t in range(TPH):
                    for i in range(2):
                        b = 2 * (TPH * h + t) + i
                        last = mm(banks[2 + 3 * h][seq(i), tile(t)], attT[0:SEQ, seq(2 * t + i)], ctxk[:, b, :])
                last.then_inc(s("lo_ps"), 1)

            def gather(d):
                pe.wait_ge(s("disp"), d + 1)
                if d // 2:
                    pe.wait_ge(s("xe_sb"), d // 2)
                else:
                    pe.wait_ge(s("xh_lo"), 2)
                    pe.wait_ge(s("sh_act"), 2)
                for k in range(2):
                    for t in range(TILES):
                        last = mm(banks[k][:, 256 * (d % 2):256 * (d % 2 + 1)], xh[:, t, k, :],
                                  disp[:, d, t, :, :].rearrange("p q s -> p (q s)"), start=t == 0,
                                  stop=t == TILES - 1)
                last.then_inc(s("ga_ps"), 1)

            def weights(g):
                if g:
                    pe.wait_ge(s("ws_sb"), 3 * (g - 1) + 1)
                else:
                    pe.wait_ge(s("cd"), 2 * CD)
                    pe.wait_ge(s("sd_out"), TPH)
                for q in range(GRP):
                    n = GRP * g + q
                    for t in range(TILES):
                        last = mm(banks[2][:, 6 * q:6 * q + 6], disp[:, n // DG, t, n % DG, :],
                                  wc3[:, t, 2 * n:2 * n + 2, :].rearrange("p e k -> p (e k)"),
                                  start=t == 0, stop=t == TILES - 1)
                last.then_inc(s("ws_ps"), 1)

            def ln_T3():
                pe.wait_ge(s("y_out"), TILES)
                lnT(3, banks[5])

            def logits(h):
                pe.wait_ge(ld["gw"], 32)
                pe.wait_ge(s("hT_sb"), 6 + 2 * h)
                for t in range(TPH):
                    last = mm(banks[3 + 3 * h][:, (E1 + 1) * t:(E1 + 1) * (t + 1)], hT[:, tile(TPH * h + t)], gw[:, :])
                last.then_inc(s("cl_ps"), 1)

            def positions(h):
                pe.wait_ge(s("cl_sb"), 2 * h + 2)
                for t in range(TPH):
                    T = TPH * h + t
                    out = banks[4 + 3 * h][:, E1 * t:E1 * (t + 1)]
                    for k in range(T):
                        mm(out, ones16[:, :], chosen[:, k, :], start=k == 0, stop=False)
                    last = mm(out, upper16[:, :], chosen[:, T, :], start=T == 0, stop=True)
                last.then_inc(s("pos_ps"), 1)

            def shared(k):
                h, f = k // 2, k % 2
                pe.wait_ge(ld["shared"], 32)
                if k:
                    pe.wait_ge(s("sh_act"), k)
                mm(banks[3 * h][:, :], sgu[:, f * P:(f + 1) * P], hT[:, half(h)])
                mm(banks[3 * h + 1][:, :], sgu[:, SHARED + f * P:SHARED + (f + 1) * P], hT[:, half(h)])\
                    .then_inc(s("sh_ps"), 1)

            def shared_down(h):
                pe.wait_ge(s("sh_act"), 2 * (h + 1))
                for t in range(TPH):
                    for j in range(2):
                        last = mm(banks[2 + 3 * h][:, tile(t)], shg[:, j, tile(t)], sdn[:, j, :], start=j == 0,
                                  stop=j == 1)
                last.then_inc(s("sd_ps"), 1)
            spread(0)
            spread(1)
            ahead = 2
            for n in range(4 * E0):
                while ahead <= min(n + (2 if n < 2 * E0 - 1 else 3), 4 * E0 - 1):
                    spread(ahead)
                    ahead += 1
                experts(n)
                if n == 2:
                    ln_T3()
                if n == 3:
                    gate_lg(1)
                if n == 9:
                    gate_T(1)
                if n == E0:
                    attn_a(0)
                if n == E0 + 5:
                    attn_T(0)
                if n == E0 + 7:
                    attn_o(0)
                if n == 2 * E0 + 3:
                    attn_a(1)
                if n == 2 * E0 + 7:
                    attn_T(1)
                if n == 2 * E0 + 12:
                    attn_o(1)
                if n == 3 * E0:
                    out_T(0)
                if n == 3 * E0 + 6:
                    lnT(4, banks[2])
                if n == 3 * E0 + 8:
                    l_scores(0)
                if n == 3 * E0 + 12:
                    l_T(0)
                if n == 3 * E0 + 13:
                    l_values(0)
                if n == 3 * E0 + 15:
                    out_T(1)
            lnT(5, banks[2])
            logits(0)
            lnT(6, banks[5])
            l_scores(1)
            positions(0)
            shared(0)
            l_T(1)
            l_values(1)
            shared(1)
            lnT(7, banks[5])
            logits(1)
            shared_down(0)
            positions(1)
            shared(2)
            gather(0)
            shared(3)
            shared_down(1)
            gather(1)
            weights(0)
            def disp_T(n):
                if n:
                    pe.wait_ge(s("dT_sb"), n)
                out = banks[7][:, :].bitcast(F16)
                for t in range(TILES):
                    last = nc.tensor.transpose(out[:, tile(t)], disp[:, n // DG, t, n % DG, :], ident16[:, :])
                last.then_inc(s("dT_ps"), 1)

            def up(g):
                pe.wait_ge(ld_exp[g % 2], 32 * (g // 2 + 1))
                pe.wait_ge(s("xe_sb"), g + 1)
                if g:
                    pe.wait_ge(s("up_act"), 2 * g)
                for q in range(GRP):
                    for i in range(2):
                        x = xeT[:, g % 2, q, :].rearrange("p (c e) -> p c e", e=2)[:, :, i]
                        w = wguR[:, g % 2, 2 * q + i, :]
                        mm(banks[3][seq(i), SEQ * q:SEQ * (q + 1)], w[:, 0:INNER], x)
                        last = mm(banks[3][seq(i), 256 + SEQ * q:256 + SEQ * (q + 1)], w[:, INNER:P], x)
                last.then_inc(s("up_ps"), 1)

            def down(g):
                pe.wait_ge(s("up_act"), 2 * (g + 1))
                if g:
                    pe.wait_ge(s("dn_lo"), GRP * g)
                for q in range(GRP):
                    last = mm(banks[4][:, tile(q)], actb[:, g % 2, q, :, :].rearrange("p c e -> p (c e)"),
                              wdR[:, g % 2, q, :])
                last.then_inc(s("dn_ps"), 1)

            def scatter(n):
                pe.wait_ge(s("dn_lo"), n + 1)
                pe.wait_ge(s("dT_sb"), n + 1)
                for h in range(HALVES):
                    for k in range(2):
                        last = mm(banks[5 + h][:, :], esp[:, n % EPR, k, :], dispT[:, n % EPR, half(h)],
                                  start=n == 0 and k == 0, stop=n == EP - 1 and k == 1)
                last.then_inc(s("sc_g"), 1)
            pe.wait_ge(s("sd_out"), TILES)
            for g in range(NGRP):
                disp_T(GRP * g)
                up(g)
                disp_T(GRP * g + 1)
                if g + 1 < NGRP:
                    gather(2 * g + 2)
                disp_T(GRP * g + 2)
                down(g)
                if g + 1 < NGRP:
                    gather(2 * g + 3)
                disp_T(GRP * g + 3)
                if g + 1 < NGRP:
                    weights(g + 1)
                for q in range(GRP):
                    scatter(GRP * g + q)
            pe.wait_ge(s("xe_sb"), NGRP)
            for h in range(HALVES):
                pe.wait_ge(s("yT_sb"), h + 1)
                for t in range(TPH):
                    last = nc.tensor.transpose(banks[h][:, tile(t)], yT[:, tile(TPH * h + t)], ident[:, :])
                last.then_inc(s("yt_ps"), 1)


def kernel(**inputs):
    import numpy as np
    import concourse.bacc as bacc
    from concourse.bass_utils import run_bass_kernel_spmd

    a = {k: np.asarray(v) for k, v in inputs.items()}
    x, c = a["x"].reshape(TOKENS, P), a["ctx_1024"].reshape(TOKENS, P)
    laid = {
        "x": x, "ctx": c, "ctxT": c.T, "mask": a["mask_BxS2_ik1"], "g_xattn": a["g_xattn"], "g_ffn": a["g_ffn"],
        "WqT": a["L0_xattn_Wq"].T, "WkT": a["L0_xattn_Wk"].T, "WvT": a["L0_xattn_Wv"].T,
        "WoT": a["L0_xattn_Wo"].T.reshape(PAIRS, 2, HD, P).transpose(0, 2, 1, 3).reshape(PAIRS * HD, 2, P),
        "bo": a["L0_xattn_bo"], "sim": a["L0_ffn_sim_matrix"], "gates": a["L0_ffn_gates"],
        "q_proj": a["L0_ffn_q_proj"], "k_proj": a["L0_ffn_k_proj"], "v_proj": a["L0_ffn_v_proj"],
        "o_proj": a["L0_ffn_o_proj"], "gate_w": a["L1_ffn_gate_w"], "sgate_w": a["L1_ffn_shared_gate_w"],
        "sgu": a["L1_ffn_shared_gate_up_w"], "sdn": a["L1_ffn_shared_down_w"], "egu": a["L1_ffn_expert_gate_up_w"],
        "edn": a["L1_ffn_expert_down_w"],
    }
    laid = {k: np.ascontiguousarray(v) for k, v in laid.items()}
    nc = bacc.Bacc("TRN2", target_bir_lowering=False, num_devices=1, dynamic_dma_scratch_size=1024)
    d = {k: nc.dram_tensor("in_" + k, v.shape, mybir.dt.from_np(v.dtype), kind="ExternalInput").ap()
         for k, v in laid.items()}
    d["out"] = nc.dram_tensor("out_0", (TOKENS, P), F32, kind="ExternalOutput").ap()
    program(nc, d)
    r = run_bass_kernel_spmd(nc, [{"in_" + k: v for k, v in laid.items()}], core_ids=[0])
    return r.results[0]["out_0"].reshape(BATCH, SEQ, P)
```

```python
from contextlib import ExitStack

import concourse.bass as bass
from concourse import mybir

F32 = mybir.dt.float32
F16 = mybir.dt.float16
F32R = mybir.dt.float32r
BF16 = mybir.dt.bfloat16
I32 = mybir.dt.int32
U32 = mybir.dt.uint32
ALU = mybir.AluOpType
ACT = mybir.ActivationFunctionType
AX = mybir.AxisListType

P = 128
SEQ = 64
BATCH = 16
TOKENS = SEQ * BATCH
TILES = TOKENS // P
HALVES = 2
TPH = TILES // HALVES
HT = TPH * P
HEADS = 16
HD = P // HEADS
PAIRS = HEADS // 2
E0 = 16
E1 = 64
EP = E1 // 2
CAP = 64
INNER = 64
SHARED = 256
GRP = 4
NGRP = EP // GRP
EPS = 1e-5
TINY = 1e-24
NEG = 1e10
BIG = 512.0
LOW = -3.0e38
LO_SCALE = 2048.0
NCONST = 9
NSEL = 9
NSPLIT = E0 * P // 512
CHUNKS = PAIRS // 2
KD = 5
SH_BANK = (0, 3, 3, 6)
LN_HALF = (0, 1, 0, 1, 0, 0, 1, 1)
LN_PREV = (None, None, 0, 1, 2, 4, 3, 6)
SPLIT_AT = (0, 3, 5, 8, 3 * NSPLIT)
LG_BANK = (1, 7)
WT_BANK = (0, 6)
KEEP = E0 // 2
ZR = 4
ZSP = 3
DG = 2
EPR = 2 * GRP
GD, GD_EXP = 30, 18
CD, CD_EXP = 17, 9


def spread_bank(n):
    return n % 2 if n < 2 * E0 else (0, 1, 2, 4)[n % 4]


def disp_bank(n):
    return 7 if n <= EP - GRP else (7, 0, 1, 2)[n % GRP]


def program(nc, d):
    ctx = ExitStack()
    with ctx:
        def sb(name, shape, dt=F32):
            return ctx.enter_context(nc.sbuf_tensor(name, shape, dt))

        def sem(name):
            return ctx.enter_context(nc.semaphore(name))

        xres = sb("xres", [P, TILES, P])
        hn = sb("hn", [P, TILES, P])
        hT = sb("hT", [P, TOKENS])
        ctxT = sb("ctxT", [P, TOKENS])
        ctxk2 = sb("ctxk2", [P, BATCH * P])
        ctxk = ctxk2[0:SEQ, :].rearrange("p (b c) -> p b c", b=BATCH)
        wq, wk, wv = (sb(n, [P, P]) for n in ("wq", "wk", "wv"))
        wo = sb("wo", [P, 2, P])
        bo = sb("bo", [P, P])
        gates4 = sb("gates4", [P, 4])
        tg = sb("tg", [P, 4])
        simm = sb("simm", [P, E0])
        sim2 = sb("sim2", [P, E0])
        gt0 = sb("gt0", [P, E0])
        sig0 = sb("sig0", [P, E0])
        maski = sb("maski", [P, TILES, SEQ], I32)
        maskfn = sb("maskfn", [P, 2 * TILES * SEQ])
        maskf = maskfn[:, 0:TILES * SEQ].rearrange("p (t k) -> p t k", t=TILES)
        maskn = maskfn[:, TILES * SEQ:].rearrange("p (t k) -> p t k", t=TILES)
        gw = sb("gw", [P, E1 + 1])
        sgu = sb("sgu", [P, 2 * SHARED])
        sdn = sb("sdn", [P, 2, P])
        big = sb("big", [P, TILES * EP * CAP * 2], F16)
        bigf = big[:, :].bitcast(F32)
        KSIZE = BATCH * PAIRS * SEQ
        kexp = bigf[:, 0:KSIZE].rearrange("p (c b j k) -> p c b j k", b=4, j=PAIRS, k=SEQ)
        raw = bigf[:, KSIZE:KSIZE + 2 * E0 * P].rearrange("p (r n) -> p r n", r=2)
        qexp = bigf[:, KSIZE + 2 * E0 * P:KSIZE + 2 * E0 * P + 2 * TOKENS].rearrange("p (b e q) -> p b e q", b=BATCH, e=2)
        oexp = bigf[:, 0:E0 * P].rearrange("p (e c) -> p e c", e=E0)
        disp = big[:, :].rearrange("p (g t q s) -> p g t q s", g=EP // DG, t=TILES, q=DG)
        split = sb("split", [P, 2 * 3 * E0 * P], F32R)
        wsp = split[:, :].rearrange("p (k i n) -> p k i n", k=2, i=3)
        dispT = split[:, 0:EPR * TOKENS].rearrange("p (r n) -> p r n", r=EPR)
        esp = split[:, EPR * TOKENS:EPR * (TOKENS + 2 * P)].rearrange("p (r k n) -> p r k n", r=EPR, k=2)
        z = bigf[:, E0 * P:E0 * P + ZR * HT].rearrange("p (r n) -> p r n", r=ZR)
        wb = bigf[:, E0 * P + ZR * HT:E0 * P + (ZR + 2 * E0 - KEEP) * HT].rearrange("p (n c) -> p n c", c=HT)
        zsp = sb("zsp", [P, ZSP, 2, HT], F32R)
        work = sb("work", [P, 4 * HT * TPH])
        ident = sb("ident", [P, P])
        ident16 = sb("ident16", [P, P], F16)
        ones = sb("ones", [P, P])
        ones16 = sb("ones16", [P, P], F16)
        upper16 = sb("upper16", [P, P], F16)
        headm = sb("headm", [P, HEADS])
        pairm = sb("pairm", [P, PAIRS])
        oddm = sb("oddm", [P, 2])
        halfm = sb("halfm", [P, 2])
        parity = sb("parity", [P, 2])
        selc = sb("selc", [3 * E0, E0])
        identb = sb("identb", [P, P], BF16)
        io16 = sb("io16", [P, E0])
        slotc = sb("slotc", [P, CAP, 2], F16)
        selw = sb("selw", [E0 * 3, E0, P], BF16)
        mhalf = sb("mhalf", [P, E0])

        banks = [ctx.enter_context(nc.psum_tensor(f"bank{i}", [P, 512], F32)) for i in range(8)]

        o = 0

        def take(n):
            nonlocal o
            o += n
            return work[:, o - n:o]
        kT = take(TOKENS)
        vblk = take(BATCH * CHUNKS * 36).rearrange("p (n i e d) -> p n i e d", i=2, e=2, d=9)
        prob = take(2 * HEADS * SEQ).rearrange("p (r n) -> p r n", r=2)
        probT = take(HEADS * SEQ)
        ohead = take(P)
        oheadT = take(P)
        rsum = take(HEADS)
        smax = take(2 * HEADS).rearrange("p (r h) -> p r h", r=2)
        assert o <= work.shape[1]
        o = 0
        qkvT = take(3 * HT).rearrange("p (r n) -> p r n", r=3)
        vk = take(8 * P).rearrange("p (b n) -> p b n", b=8)
        att = take(TPH * SEQ).rearrange("p (t k) -> p t k", t=TPH)
        attT = take(HT)
        oT = take(2 * HT).rearrange("p (r n) -> p r n", r=2)
        accT = take(HT)
        room = work

        def take_c(n):
            nonlocal o
            o += n
            return room[:, o - n:o]
        xh = take_c(TILES * P).bitcast(F16).rearrange("p (t k c) -> p t k c", t=TILES, k=2)
        sth = take_c(HT)
        shg = take_c(2 * HT).rearrange("p (f n) -> p f n", f=2)
        wc3 = take_c(TILES * E1 * 3 // 2).bitcast(BF16).rearrange("p (t e k) -> p t e k", t=TILES, k=3)
        assert o <= room.shape[1]
        o = 0
        xeT = take_c(2 * GRP * P).rearrange("p (r q n) -> p r q n", r=2, q=GRP)
        yT = take_c(TOKENS)
        stats = sb("stats", [P, TPH, 6])
        mv = sb("mv", [P, TILES, 2])
        ve = sb("ve", [P, TPH])
        rstd = sb("rstd", [P, TILES])
        negm = sb("negm", [P, TILES])
        shift = sb("shift", [P, TILES])
        sq = sb("sq", [P, P])
        ss = sb("ss", [P, TPH])
        rn = sb("rn", [P, TPH])
        lg = sb("lg", [P, TPH, E0])
        top = sb("top", [P, TPH, 8])
        topi = sb("topi", [P, TPH, 8], U32)
        topf = sb("topf", [P, TPH, 8])
        ga = sb("ga", [P, TPH, E0])
        gb = sb("gb", [P, TPH, E0])
        gc = sb("gc", [P, TPH, E0])
        fbk = sb("fbk", [P, TPH, E0])
        g1 = sb("g1", [P, TPH])
        g2 = sb("g2", [P, TPH])
        w3 = sb("w3", [P, TILES, 3 * E0], BF16)
        wT = sb("wT", [3 * E0, TOKENS], BF16)
        amax = sb("amax", [P, TPH])
        asum = sb("asum", [P, TPH])
        lgc = sb("lgc", [P, TILES, E1 + 1])
        rep = sb("rep", [P, TPH, E1])
        topc = sb("topc", [P, TPH, 8])
        chosen = sb("chosen", [P, TILES, E1], F16)
        wex = sb("wex", [P, TPH, E1])
        wres = sb("wres", [P, TPH, E1])
        csum = sb("csum", [P, TPH])
        post = sb("post", [P, TPH, E1])
        pos16 = sb("pos16", [P, EP // DG, TILES, 2 * DG], F16)
        sg = sb("sg", [P, TILES])
        wslot2 = sb("wslot2", [P, EP, 2])
        wslot = sb("wslot", [P, EP])
        xlow = sb("xlow", [P, GRP * P])
        th = sb("th", [P, GRP * CAP])
        ab = sb("ab", [P, GRP * CAP])
        actb = maskfn[:, :].rearrange("p (r q c e) -> p r q c e", r=2, q=GRP, c=CAP)
        wguR = ctxk2[:, :].rearrange("p (r e f) -> p r e f", r=2, e=2 * GRP)
        wdR = ctxT[:, :].rearrange("p (r q h) -> p r q h", r=2, q=GRP)

        ld = {n: sem("ld_" + n) for n in ("x", "ctxT", "wkv", "wqo", "misc", "mask", "ctxk", "oexp", "gw", "shared")}
        ld_raw = [sem(f"ld_raw{i}") for i in range(3)]
        ld_exp = [sem(f"ld_exp{i}") for i in range(2)]
        s = {name: sem(name) for name in (
            "consts",
            "sel",
            "tanh_g",
            "xb",
            "sim2",
            "sn_ps",
            "sn_pre",
            "sn",
            "g_act",
            "g_dve",
            "split_hi",
            "split_lo",
            "ln_stats",
            "ln_aggr",
            "ln_var",
            "ln_neg",
            "ln_rstd",
            "ln_shift",
            "ln_out",
            "hT_ps",
            "hT_sb",
            "kT_ps",
            "kT_sb",
            "kexp_d",
            "kexp_a",
            "q_ps",
            "q_sb",
            "v_ps",
            "v_sb",
            "sc_ps",
            "sc_max",
            "sc_sub",
            "sc_exp",
            "pT_ps",
            "pT_sb",
            "pv_ps",
            "pv_rec",
            "pv_sb",
            "oT_ps",
            "oT_sb",
            "y_ps",
            "y_out",
            "sq_sum",
            "rnorm",
            "lg_ps",
            "gd",
            "w3",
            "wT_ps",
            "wT_sb",
            "wb_ps",
            "wb_sb",
            "z_sb",
            "z_hi",
            "z_lo",
            "zuse",
            "qkv_sb",
            "v2_ps",
            "v2_sb",
            "at_ps",
            "at_d",
            "at_exp",
            "aT_ps",
            "aT_sb",
            "ob_ps",
            "ob_sb",
            "acc_sb",
            "tr_ps",
            "tr_out",
            "mask_f",
            "la_ps",
            "la_d",
            "la_exp",
            "lT_ps",
            "lT_sb",
            "lo_ps",
            "lrec",
            "lo_out",
            "cl_ps",
            "cl_sb",
            "cd",
            "cexp",
            "ctanh",
            "sgv",
            "pos_ps",
            "post",
            "pos_sb",
            "xh_hi",
            "xh_r",
            "xh_lo",
            "sh_ps",
            "sh_th",
            "sh_a",
            "sh_act",
            "sd_ps",
            "sd_out",
            "disp",
            "ga_ps",
            "xl_sb",
            "xe_sb",
            "ws_ps",
            "ws_sb",
            "act0",
            "up_ps",
            "up_th",
            "up_a",
            "up_act",
            "dn_ps",
            "dn_hi",
            "dn_lo",
            "dT_ps",
            "dT_sb",
            "dT_last",
            "sc_g",
            "sc_end",
            "yT_sb",
            "yt_ps",
            "fin",
            "out",
        )}

        block = ctx.enter_context(nc.Block())

        def seq(b):
            return slice(b * SEQ, (b + 1) * SEQ)

        def half(h):
            return slice(h * HT, (h + 1) * HT)

        def tile(t):
            return slice(t * P, (t + 1) * P)

        @block.sync
        def _(sp):
            sp.dma_start(ctxT[:, :], d["ctxT"]).then_inc(ld["ctxT"], 16)
            sp.dma_start(wk[:, :], d["WkT"]).then_inc(ld["wkv"], 16)
            sp.dma_start(wv[:, :], d["WvT"]).then_inc(ld["wkv"], 16)
            sp.dma_start(xres[:, :, :], d["x"].rearrange("(t p) c -> p t c", p=P)).then_inc(ld["x"], 16)
            sp.dma_start(wq[:, :], d["WqT"]).then_inc(ld["wqo"], 16)
            for i in range(2):
                sp.dma_start(wo[seq(i), :, :], d["WoT"]).then_inc(ld["wqo"], 16)
            sp.dma_start(bo[:, :], d["bo"].partition_broadcast(P)).then_inc(ld["misc"], 16)
            sp.dma_start(gates4[:, 0:2], d["g_xattn"].partition_broadcast(P)).then_inc(ld["misc"], 16)
            sp.dma_start(gates4[:, 2:4], d["g_ffn"].partition_broadcast(P)).then_inc(ld["misc"], 16)
            sp.dma_start(gt0[:, :], d["gates"].partition_broadcast(P)).then_inc(ld["misc"], 16)
            sp.dma_start(simm[:, :], d["sim"]).then_inc(ld["misc"], 16)
            m = d["mask"].rearrange("(t b) k -> b t k", b=2)
            for i in range(3):
                if i == 2:
                    sp.wait_ge(s["split_lo"], NSPLIT)
                sp.dma_start(raw[:, i % 2, :].rearrange("p (e h) -> p e h", e=E0),
                             d["qkv"[i] + "_proj"].rearrange("e c h -> c e h")).then_inc(ld_raw[i], 16)
            for b in range(2):
                sp.dma_start(maski[seq(b), :, :], m[b].partition_broadcast(SEQ)).then_inc(ld["mask"], 16)
            sp.dma_start(ctxk[:, :, :], d["ctx"].rearrange("(b k) c -> k b c", k=SEQ)).then_inc(ld["ctxk"], 16)
            sp.dma_start(gw[:, 0:E1], d["gate_w"]).then_inc(ld["gw"], 16)
            sp.dma_start(gw[:, E1:E1 + 1], d["sgate_w"]).then_inc(ld["gw"], 16)
            sp.dma_start(sgu[:, :], d["sgu"]).then_inc(ld["shared"], 16)
            sp.dma_start(sdn[:, :, :], d["sdn"].rearrange("(f p) h -> p f h", p=P)).then_inc(ld["shared"], 16)
            sp.wait_ge(s["sc_ps"], 2 * TILES)
            sp.dma_start(oexp[:, :, :], d["o_proj"].rearrange("e h c -> h e c")).then_inc(ld["oexp"], 16)
            sp.wait_ge(s["lo_ps"], 2)
            for g in range(NGRP):
                if g >= 2:
                    sp.wait_ge(s["up_ps"], g - 1)
                    sp.wait_ge(s["dn_ps"], g - 1)
                sp.dma_start(wguR[:, g % 2, :, :], d["egu"][2 * GRP * g:2 * GRP * (g + 1)]
                             .rearrange("e c f -> c e f")).then_inc(ld_exp[g % 2], 16)
                sp.dma_start(wdR[:, g % 2, :, :], d["edn"][2 * GRP * g:2 * GRP * (g + 1)]
                             .rearrange("(q e) i h -> (e i) q h", e=2)).then_inc(ld_exp[g % 2], 16)
            for h in range(HALVES):
                sp.wait_ge(s["fin"], TPH * (h + 1))
                sp.dma_start(d["out"][half(h), :].rearrange("(t p) c -> p t c", p=P),
                             xres[:, TPH * h:TPH * (h + 1), :]).then_inc(s["out"], 16)
            sp.wait_ge(s["out"], 16 * HALVES)

        @block.gpsimd
        def _(pool):
            done = [0]

            def const(ins):
                ins.then_inc(s["consts"], 1)
                done[0] += 1

            def settle():
                pool.wait_ge(s["consts"], done[0])

            const(nc.gpsimd.memset(ident[:, :], 0.0))
            settle()
            const(nc.gpsimd.affine_select(out=ident[:, :], in_=ident[:, :], compare_op=ALU.not_equal, fill=1.0,
                                          base=0, pattern=[[-1, P]], channel_multiplier=1))
            for x, v in ((ones, 1.0), (ones16, 1.0), (upper16, 1.0), (mhalf, -0.5)):
                const(nc.gpsimd.memset(x[:, :], v))
            const(nc.gpsimd.iota(slotc[:, :, :], [[1, CAP], [0, 2]], base=0, channel_multiplier=0,
                                 allow_small_or_imprecise_dtypes=True))
            const(nc.gpsimd.iota(io16[:, :], [[1, E0]], base=0, channel_multiplier=0,
                                 allow_small_or_imprecise_dtypes=True))
            settle()
            const(nc.gpsimd.affine_select(out=upper16[:, :], in_=upper16[:, :], compare_op=ALU.is_gt, fill=0.0,
                                          base=0, pattern=[[1, P]], channel_multiplier=-1))

            def rsqrt_ln(n):
                ts = slice(TPH * LN_HALF[n], TPH * (LN_HALF[n] + 1))
                pool.wait_ge(s["ln_var"], n + 1)
                nc.gpsimd.tensor_tensor(rstd[:, ts], ve[:, :], mhalf[:, 0:TPH], ALU.pow).then_inc(s["ln_rstd"], 1)
                pool.wait_ge(s["ln_rstd"], n + 1)
                pool.wait_ge(s["ln_neg"], n + 1)
                nc.gpsimd.tensor_tensor(shift[:, ts], negm[:, ts], rstd[:, ts], ALU.mult).then_inc(s["ln_shift"], 1)

            def norms(h):
                pool.wait_ge(s["sq_sum"], TPH * (h + 1))
                if h:
                    pool.wait_ge(s["gd"], GD * h)
                nc.gpsimd.tensor_scalar(rn[:, :], ss[:, :], TINY, None, ALU.max).then_inc(s["rnorm"], 1)
                pool.wait_ge(s["rnorm"], 2 * h + 1)
                nc.gpsimd.tensor_tensor(rn[:, :], rn[:, :], mhalf[:, 0:TPH], ALU.pow).then_inc(s["rnorm"], 1)

            def low_parts(i):
                for k in range(NSPLIT):
                    n = NSPLIT * i + k
                    pool.wait_ge(s["split_hi"], n + 1)
                    cut = slice(512 * k, 512 * (k + 1))
                    nc.gpsimd.tensor_tensor(wsp[:, 1, i, cut], raw[:, i % 2, cut], wsp[:, 0, i, cut].bitcast(F32),
                                            ALU.subtract).then_inc(s["split_lo"], 1)

            rsqrt_ln(0)
            rsqrt_ln(1)
            for i in range(3):
                low_parts(i)
                if i == 0:
                    pool.wait_ge(s["sn_pre"], 1)
                    nc.gpsimd.tensor_tensor(sim2[:, :], sim2[:, :], mhalf[:, :], ALU.pow).then_inc(s["sn_pre"], 1)
                    pool.wait_ge(s["sn_pre"], 2)
                    nc.gpsimd.tensor_tensor(simm[:, :], simm[:, :], sim2[:, :], ALU.mult).then_inc(s["sn"], 1)
            rsqrt_ln(2)
            norms(0)
            rsqrt_ln(3)
            norms(1)

            def low_tokens(h):
                ts = slice(TPH * h, TPH * (h + 1))
                pool.wait_ge(s["xh_hi"], h + 1)
                pool.wait_ge(s["hT_ps"], 6 + 2 * h)
                nc.gpsimd.tensor_tensor(hn[:, ts, :], hn[:, ts, :], xh[:, ts, 0, :], ALU.subtract).then_inc(s["xh_r"], 1)

            for n in range(4, 8):
                rsqrt_ln(n)
                if n > 5:
                    low_tokens(n - 6)
            pool.wait_ge(s["la_d"], 7)
            nc.gpsimd.memset(actb[:, :, :, :, :], 0.0).then_inc(s["act0"], 1)

        @block.scalar
        def _(act):
            A = nc.scalar.activation

            def copy(out, in_):
                return A(out, in_, ACT.Copy)

            def keys(c):
                for hd in range(KD, PAIRS):
                    A(kexp[:, c, :, hd, :], kT[:, 4 * SEQ * c:4 * SEQ * (c + 1)].rearrange("p (b k) -> p b k", k=SEQ),
                      ACT.Copy, scale=pairm[:, hd:hd + 1]).then_inc(s["kexp_a"], 1)

            def high_part(n):
                i, k = n // NSPLIT, n % NSPLIT
                act.wait_ge(ld_raw[i], 16)
                cut = slice(512 * k, 512 * (k + 1))
                copy(wsp[:, 0, i, cut], raw[:, i % 2, cut]).then_inc(s["split_hi"], 1)

            def ln_apply(n):
                h = LN_HALF[n]
                act.wait_ge(s["ln_shift"], n + 1)
                if n >= 2:
                    act.wait_ge(s["hT_ps"], LN_PREV[n] + 1)
                for t in range(TPH * h, TPH * (h + 1)):
                    A(hn[:, t, :], xres[:, t, :], ACT.Identity, bias=shift[:, t:t + 1],
                      scale=rstd[:, t:t + 1]).then_inc(s["ln_out"], 1)

            def k_out(h):
                act.wait_ge(s["kT_ps"], h + 1)
                copy(kT[:, half(h)], banks[h][:, :]).then_inc(s["kT_sb"], 1)

            def h_out(h):
                act.wait_ge(s["hT_ps"], h + 1)
                copy(hT[:, half(h)], banks[6 + h][:, :]).then_inc(s["hT_sb"], 1)

            def q_out(h):
                act.wait_ge(s["q_ps"], h + 1)
                for i in range(2):
                    A(qexp[:, 8 * h:8 * (h + 1), i, :], banks[6 * h][:, :].rearrange("p (b q) -> p b q", q=SEQ), ACT.Copy,
                      scale=oddm[:, i:i + 1]).then_inc(s["q_sb"], 1)

            k_out(0)
            act.wait_ge(s["sel"], NSEL)
            act.wait_ge(s["kT_sb"], 1)
            keys(0)
            ln_apply(0)
            k_out(1)
            h_out(0)
            q_out(0)
            ln_apply(1)
            h_out(1)
            q_out(1)
            act.wait_ge(ld["misc"], 5 * 16)
            A(tg[:, :], gates4[:, :], ACT.Tanh).then_inc(s["tanh_g"], 1)
            A(sig0[:, :], gt0[:, :], ACT.Tanh, scale=0.5).then_inc(s["g_act"], 1)
            act.wait_ge(s["kT_sb"], 2)

            def a_exp(t):
                act.wait_ge(s["sc_sub"], 2 * (t + 1))
                A(prob[:, t % 2, :], prob[:, t % 2, :], ACT.Exp, scale=float(P) ** -0.5).then_inc(s["sc_exp"], 1)

            def a_pT(t):
                act.wait_ge(s["pT_ps"], t + 1)
                if t >= 1:
                    act.wait_ge(s["pv_ps"], t)
                for k in range(2):
                    copy(probT[:, 512 * k:512 * (k + 1)], banks[4 + k][:, :]).then_inc(s["pT_sb"], 1)

            def a_oT(t):
                act.wait_ge(s["oT_ps"], t + 1)
                if t >= 1:
                    act.wait_ge(s["y_ps"], t)
                copy(oheadT[:, :], banks[7][:, 0:P]).then_inc(s["oT_sb"], 1)

            def ln_T(n, bank):
                act.wait_ge(s["hT_ps"], n + 1)
                copy(hT[:, half(LN_HALF[n])], bank[:, :]).then_inc(s["hT_sb"], 1)

            def squares(h):
                act.wait_ge(s["ln_out"], TPH * (3 + h))
                if h:
                    act.wait_ge(s["rnorm"], 1)
                for t in range(TPH):
                    if h or t:
                        act.wait_ge(s["sq_sum"], h * TPH + t)
                    A(sq[:, :], hn[:, TPH * h + t, :], ACT.Square,
                      accum_out=ss[:, t:t + 1]).then_inc(s["sq_sum"], 1)

            def gate_exp(h):
                act.wait_ge(s["gd"], GD * h + GD_EXP)
                A(gc[:, :, :], gc[:, :, :], ACT.Exp).then_inc(s["g_act"], 1)

            def gate_T(h):
                act.wait_ge(s["wT_ps"], h + 1)
                copy(wT[:, half(h)], banks[WT_BANK[h]][0:3 * E0, 0:HT // 2].bitcast(BF16)).then_inc(s["wT_sb"], 1)

            for t in range(TILES + 2):
                if 1 <= t <= TILES:
                    a_exp(t - 1)
                    if t == 1:
                        keys(1)
                    a_pT(t - 1)
                if t in (2, 4):
                    keys(1 + t // 2)
                if t == TILES + 1:
                    gate_T(0)
                if t >= 2:
                    a_oT(t - 2)
                if 1 <= t <= 4:
                    for n in range(SPLIT_AT[t - 1], SPLIT_AT[t]):
                        high_part(n)
                if t == TILES - 2:
                    ln_apply(2)
                if t == TILES - 1:
                    squares(0)
                    ln_T(2, banks[0])
                if t == TILES:
                    gate_exp(0)

            def keep(n):
                act.wait_ge(s["wb_ps"], n + 1)
                if n == KEEP:
                    act.wait_ge(s["split_lo"], 3 * NSPLIT)
                    act.wait_ge(s["sc_ps"], 2 * TILES)
                copy(wb[:, n - KEEP, :], banks[n % 2][:, :]).then_inc(s["wb_sb"], 1)

            def high(n):
                act.wait_ge(s["z_sb"], n + 1)
                if n >= ZSP:
                    act.wait_ge(s["zuse"], n - ZSP + 1)
                copy(zsp[:, n % ZSP, 0, :], z[:, n % ZR, :]).then_inc(s["z_hi"], 1)

            def qkv_out(h):
                act.wait_ge(s["zuse"], E0 * (h + 1))
                if h:
                    act.wait_ge(s["at_ps"], h)
                for i in range(3):
                    copy(qkvT[:, i, :], banks[2 + 3 * h + i][:, :]).then_inc(s["qkv_sb"], 1)

            def attn_v(h):
                act.wait_ge(s["v2_ps"], h + 1)
                if h:
                    act.wait_ge(s["ob_ps"], h)
                for i in range(2):
                    copy(vk[0:SEQ, 4 * i:4 * i + 4, :].rearrange("p b n -> p (b n)"),
                         banks[2 + 3 * h + i][0:SEQ, :]).then_inc(s["v2_sb"], 1)

            def attn_exp(h):
                act.wait_ge(s["at_d"], 5 * h + 2)
                A(att[:, :, :], att[:, :, :], ACT.Exp, scale=float(P) ** -0.5).then_inc(s["at_exp"], 1)

            def attn_T(h):
                act.wait_ge(s["aT_ps"], h + 1)
                if h:
                    act.wait_ge(s["ob_ps"], h)
                copy(attT[0:SEQ, :], banks[4 + 3 * h][0:SEQ, :]).then_inc(s["aT_sb"], 1)

            def attn_o(h):
                act.wait_ge(s["ob_ps"], h + 1)
                copy(oT[:, h, :], banks[2 + 3 * h][:, :]).then_inc(s["ob_sb"], 1)

            def out_T(h):
                act.wait_ge(s["zuse"], E0 * (3 + h))
                if h:
                    act.wait_ge(s["tr_ps"], h)
                copy(accT[:, :], banks[3 + 3 * h][:, :]).then_inc(s["acc_sb"], 1)

            def l_exp(h):
                act.wait_ge(s["la_d"], 5 * h + 4)
                A(att[:, :, :], att[:, :, :], ACT.Exp).then_inc(s["la_exp"], 1)

            def l_T(h):
                act.wait_ge(s["lT_ps"], h + 1)
                if h:
                    act.wait_ge(s["lo_ps"], h)
                copy(attT[0:SEQ, :], banks[3 + 3 * h][0:SEQ, :]).then_inc(s["lT_sb"], 1)

            def router_a(h):
                act.wait_ge(s["cl_sb"], 2 * h + 1)
                A(sg[:, TPH * h:TPH * (h + 1)], lgc[:, TPH * h:TPH * (h + 1), E1], ACT.Tanh,
                  scale=0.5).then_inc(s["ctanh"], 1)
                act.wait_ge(s["cd"], CD * h + CD_EXP)
                A(wex[:, :, :], wex[:, :, :], ACT.Exp).then_inc(s["cexp"], 1)

            def router_x(h):
                ts = slice(TPH * h, TPH * (h + 1))
                act.wait_ge(s["ln_out"], TPH * (6 + 2 * h))
                copy(xh[:, ts, 0, :], hn[:, ts, :]).then_inc(s["xh_hi"], 1)

            def router_b(h):
                act.wait_ge(s["xh_r"], h + 1)
                A(xh[:, TPH * h:TPH * (h + 1), 1, :], hn[:, TPH * h:TPH * (h + 1), :], ACT.Copy,
                  scale=LO_SCALE).then_inc(s["xh_lo"], 1)

            def shared(k):
                act.wait_ge(s["sh_ps"], k + 1)
                if k:
                    act.wait_ge(s["sh_a"], k)
                A(sth[:, :], banks[SH_BANK[k]][:, :], ACT.Tanh, scale=0.5).then_inc(s["sh_th"], 1)

            def disp_T(n):
                act.wait_ge(s["dT_ps"], n + 1)
                if n >= EPR:
                    act.wait_ge(s["sc_g"], n - EPR + 1)
                copy(dispT[:, n % EPR, :], banks[disp_bank(n)][:, :].bitcast(F16)).then_inc(s["dT_sb"], 1)

            def high_out(g):
                act.wait_ge(s["dn_ps"], g + 1)
                act.wait_ge(s["ws_sb"], 3 * (g + 1))
                if g >= 2:
                    act.wait_ge(s["sc_g"], GRP * (g - 1))
                for n in range(GRP * g, GRP * (g + 1)):
                    A(esp[:, n % EPR, 0, :], banks[4][:, tile(n % GRP)], ACT.Copy,
                      scale=wslot[:, n:n + 1]).then_inc(s["dn_hi"], 1)

            def tokens(g):
                act.wait_ge(s["ga_ps"], 2 * (g + 1))
                if g:
                    act.wait_ge(s["xe_sb"], g)
                A(xlow[:, :], banks[1][:, :], ACT.Copy, scale=1.0 / LO_SCALE).then_inc(s["xl_sb"], 1)

            for n in range(4 * E0):
                if n < 2 * E0:
                    high(n)
                if KEEP <= n + 2 < 2 * E0:
                    keep(n + 2)
                if n == 1:
                    ln_apply(3)
                if n == 2:
                    squares(1)
                if n == 5:
                    ln_T(3, banks[5])
                if n == 7:
                    gate_exp(1)
                if n == 10:
                    gate_T(1)
                if n == E0 + 1:
                    qkv_out(0)
                if n == E0 + 4:
                    attn_v(0)
                if n == E0 + 5:
                    attn_exp(0)
                if n == E0 + 6:
                    attn_T(0)
                if n == E0 + 14:
                    attn_o(0)
                if n == 2 * E0 + 1:
                    qkv_out(1)
                if n == 2 * E0 + 4:
                    attn_v(1)
                if n == 2 * E0 + 5:
                    attn_exp(1)
                if n == 2 * E0 + 9:
                    attn_T(1)
                    attn_o(1)
                if n == 3 * E0 + 4:
                    out_T(0)
                if n == 3 * E0 + 6:
                    ln_apply(4)
                    ln_T(4, banks[2])
                if n == 3 * E0 + 10:
                    l_exp(0)
                if n == 3 * E0 + 12:
                    l_T(0)
                    out_T(1)
                if n == 3 * E0 + 13:
                    ln_apply(5)
                if n == 3 * E0 + 15:
                    ln_T(5, banks[2])
            ln_apply(6)
            ln_T(6, banks[5])
            router_x(0)
            router_a(0)
            l_exp(1)
            router_b(0)
            l_T(1)
            shared(0)
            shared(1)
            ln_apply(7)
            router_x(1)
            ln_T(7, banks[5])
            shared(2)
            router_b(1)
            router_a(1)
            shared(3)
            tokens(0)
            for g in range(NGRP):
                if g + 1 < NGRP:
                    disp_T(GRP * g)
                act.wait_ge(s["up_ps"], g + 1)
                if g:
                    act.wait_ge(s["up_a"], g)
                A(th[:, :], banks[3][:, 0:256], ACT.Tanh, scale=0.5).then_inc(s["up_th"], 1)
                if g + 1 < NGRP:
                    disp_T(GRP * g + 1)
                    disp_T(GRP * g + 2)
                    high_out(g)
                    tokens(g + 1)
                else:
                    disp_T(EP - GRP)
                    high_out(g)
                    disp_T(EP - GRP + 1)
            for h in range(HALVES):
                act.wait_ge(s["sc_end"], h + 1)
                copy(yT[:, half(h)], banks[5 + h][:, :]).then_inc(s["yT_sb"], 1)

        @block.vector
        def _(dve):
            V = nc.vector

            def ln(n):
                h = LN_HALF[n]
                if n:
                    dve.wait_ge(s["ln_aggr"], TPH * n)
                for t in range(TPH):
                    V.bn_stats(stats[:, t, :], xres[:, TPH * h + t, :]).then_inc(s["ln_stats"], 1)
                for t in range(TPH):
                    dve.wait_ge(s["ln_stats"], TPH * n + t + 1)
                    V.bn_aggr(mv[:, TPH * h + t, :], stats[:, t, :]).then_inc(s["ln_aggr"], 1)
                dve.wait_ge(s["ln_aggr"], TPH * (n + 1))
                if n:
                    dve.wait_ge(s["ln_rstd"], n)
                V.tensor_scalar(ve[:, :], mv[:, TPH * h:TPH * (h + 1), 1], EPS, None, ALU.add).then_inc(s["ln_var"], 1)
                V.tensor_scalar(negm[:, TPH * h:TPH * (h + 1)], mv[:, TPH * h:TPH * (h + 1), 0], -1.0, None,
                                ALU.mult).then_inc(s["ln_neg"], 1)

            def keys(c):
                dve.wait_ge(s["kT_sb"], c // 2 + 1)
                for hd in range(KD):
                    V.tensor_scalar(kexp[:, c, :, hd, :],
                                    kT[:, 4 * SEQ * c:4 * SEQ * (c + 1)].rearrange("p (b k) -> p b k", k=SEQ),
                                    pairm[:, hd:hd + 1], None, ALU.mult).then_inc(s["kexp_d"], 1)

            dve.wait_ge(s["consts"], 2)
            for out, eye in ((headm[:, :], ident[:, :].rearrange("p (h d) -> p h d", d=HD)),
                             (halfm[:, :], ident[:, :].rearrange("p (h d) -> p h d", h=2)),
                             (parity[:, :], ident[:, :].rearrange("p (c e) -> p e c", e=2)),
                             (selc[:, :], ident[0:3 * E0, 0:3 * E0].rearrange("p (k e) -> p e k", e=E0))):
                V.tensor_reduce(out, eye, AX.X, ALU.add).then_inc(s["sel"], 1)
            V.tensor_copy(ident16[:, :], ident[:, :]).then_inc(s["sel"], 1)
            V.tensor_copy(identb[:, :], ident[:, :]).then_inc(s["sel"], 1)
            dve.wait_ge(s["sel"], 4)
            V.tensor_reduce(pairm[:, :], headm[:, :].rearrange("p (j e) -> p j e", e=2), AX.X, ALU.add).then_inc(s["sel"], 1)
            V.tensor_reduce(oddm[:, :], headm[:, :].rearrange("p (j e) -> p e j", e=2), AX.X, ALU.add).then_inc(s["sel"], 1)
            V.tensor_copy(selw[:, :, :], selc[:, :, None].to_broadcast([3 * E0, E0, P])).then_inc(s["sel"], 1)
            dve.wait_ge(ld["x"], 16)
            ln(0)
            dve.wait_ge(s["sel"], NSEL)
            keys(0)
            ln(1)
            V.tensor_copy(vblk[:, :, :, :, 8], halfm[:, None, :, None].to_broadcast([P, BATCH * CHUNKS, 2, 2]))\
                .then_inc(s["v_sb"], 1)
            for k in range(4):
                dve.wait_ge(s["v_ps"], k + 1)
                for i in range(2):
                    V.tensor_scalar(vblk[:, 4 * CHUNKS * k:4 * CHUNKS * (k + 1), i, :, 0:HD],
                                    banks[2 + k][:, :].rearrange("p (n i e d) -> p n i e d", i=2, e=2, d=HD)[:, :, i, :, :],
                                    halfm[:, i:i + 1], None, ALU.mult).then_inc(s["v_sb"], 1)
            dve.wait_ge(ld["misc"], 5 * 16)
            V.tensor_tensor(sim2[:, :], simm[:, :], simm[:, :], ALU.mult).then_inc(s["sim2"], 1)

            def a_soft(t):
                b = 2 * (t % 2)
                if t >= 2:
                    dve.wait_ge(s["pT_ps"], t - 1)
                    dve.wait_ge(s["sc_sub"], 2 * (t - 1))
                for k in range(2):
                    dve.wait_ge(s["sc_ps"], 2 * t + k + 1)
                    V.tensor_reduce(smax[:, t % 2, 8 * k:8 * k + 8],
                                    banks[b + k][:, :].rearrange("p (h k) -> p h k", k=SEQ),
                                    AX.X, ALU.max).then_inc(s["sc_max"], 1)
                    dve.wait_ge(s["sc_max"], 2 * t + 1 + k)
                    V.tensor_tensor(prob[:, t % 2, 512 * k:512 * (k + 1)].rearrange("p (h k) -> p h k", k=SEQ),
                                    banks[b + k][:, :].rearrange("p (h k) -> p h k", k=SEQ),
                                    smax[:, t % 2, 8 * k:8 * k + 8, None].to_broadcast([P, 8, SEQ]),
                                    ALU.subtract).then_inc(s["sc_sub"], 1)

            def a_norm(t):
                dve.wait_ge(s["pv_ps"], t + 1)
                if t:
                    dve.wait_ge(s["pv_sb"], 2 * t)
                po = banks[6][:, 0:2 * HEADS * 9].rearrange("p (n e d) -> p n e d", e=2, d=9)
                for i in range(2):
                    V.reciprocal(rsum[seq(i), :], po[seq(i), :, i, 8]).then_inc(s["pv_rec"], 1)
                if t >= 1:
                    dve.wait_ge(s["oT_ps"], t)
                for i in range(2):
                    dve.wait_ge(s["pv_rec"], 2 * t + i + 1)
                    V.tensor_tensor(ohead[seq(i), :].rearrange("p (n d) -> p n d", d=HD), po[seq(i), :, i, 0:HD],
                                    rsum[seq(i), :, None].to_broadcast([SEQ, HEADS, HD]),
                                    ALU.mult).then_inc(s["pv_sb"], 1)

            def a_res(t):
                dve.wait_ge(s["y_ps"], t + 1)
                dve.wait_ge(s["xb"], 2)
                V.scalar_tensor_tensor(xres[:, t, :], banks[7][:, P:2 * P], tg[:, 0:1], xres[:, t, :],
                                       ALU.mult, ALU.add).then_inc(s["y_out"], 1)

            gdn = [0]

            def gstep(ins):
                ins.then_inc(s["gd"], 1)
                gdn[0] += 1

            def gwait():
                dve.wait_ge(s["gd"], gdn[0])

            def gate_a(h):
                b3 = banks[LG_BANK[h]]
                dve.wait_ge(s["rnorm"], 2 * h + 2)
                dve.wait_ge(s["lg_ps"], h + 1)
                dve.wait_ge(s["g_dve"], 1)
                gwait()
                for t in range(TPH):
                    gstep(V.scalar_tensor_tensor(lg[:, t, :], b3[:, E0 * t:E0 * (t + 1)], rn[:, t:t + 1], sig0[:, :],
                                                 ALU.mult, ALU.subtract))
                gwait()
                for t in range(TPH):
                    gstep(V.max(top[:, t, :], lg[:, t, :]))
                gstep(V.tensor_scalar(ga[:, :, :], lg[:, :, :], 0.0, None, ALU.is_gt))
                gstep(V.tensor_scalar(gb[:, :, :], lg[:, :, :], 0.0, None, ALU.max))
                gwait()
                for t in range(TPH):
                    gstep(V.max_index(topi[:, t, :], top[:, t, :], lg[:, t, :]))
                gstep(V.tensor_scalar(g1[:, :], top[:, :, 0], 0.0, None, ALU.is_le))
                gstep(V.tensor_scalar(g2[:, :], top[:, :, 0], 0.0, None, ALU.max))
                gwait()
                gstep(V.tensor_copy(topf[:, :, :], topi[:, :, :]))
                gstep(V.tensor_tensor(gc[:, :, :], gb[:, :, :], g2[:, :, None].to_broadcast([P, TPH, E0]),
                                      ALU.subtract))
                assert gdn[0] == GD * h + GD_EXP

            def gate_b(h):
                gwait()
                gstep(V.tensor_tensor(gb[:, :, :], io16[:, None, :].to_broadcast([P, TPH, E0]),
                                      topf[:, :, 0:1].to_broadcast([P, TPH, E0]), ALU.is_equal))
                gstep(V.tensor_tensor(fbk[:, :, :], io16[:, None, :].to_broadcast([P, TPH, E0]),
                                      topf[:, :, 1:2].to_broadcast([P, TPH, E0]), ALU.is_equal))
                gwait()
                gstep(V.tensor_tensor(gb[:, :, :], gb[:, :, :], fbk[:, :, :], ALU.add))
                gwait()
                gstep(V.tensor_tensor(gb[:, :, :], gb[:, :, :], g1[:, :, None].to_broadcast([P, TPH, E0]), ALU.mult))
                gwait()
                gstep(V.tensor_tensor(gb[:, :, :], gb[:, :, :], ga[:, :, :], ALU.add))
                gwait()
                dve.wait_ge(s["g_act"], 2 + h)
                gstep(V.tensor_tensor(gb[:, :, :], gb[:, :, :], gc[:, :, :], ALU.mult))
                gwait()
                gstep(V.tensor_reduce(g1[:, :], gb[:, :, :], AX.X, ALU.add))
                gwait()
                gstep(V.reciprocal(g2[:, :], g1[:, :]))
                gwait()
                gstep(V.tensor_tensor(gb[:, :, :], gb[:, :, :], g2[:, :, None].to_broadcast([P, TPH, E0]), ALU.mult))
                part = [w3[:, TPH * h:TPH * (h + 1), i * E0:(i + 1) * E0] for i in range(3)]
                gwait()
                gstep(V.tensor_copy(part[0], gb[:, :, :]))
                gwait()
                gstep(V.tensor_tensor(gb[:, :, :], gb[:, :, :], part[0], ALU.subtract))
                gwait()
                gstep(V.tensor_copy(part[1], gb[:, :, :]))
                gwait()
                V.tensor_tensor(part[2], gb[:, :, :], part[1], ALU.subtract).then_inc(s["w3"], 1)
                assert gdn[0] == GD * (h + 1), gdn[0]

            for t in range(TILES + 2):
                if t < TILES:
                    a_soft(t)
                if t == TILES:
                    gate_a(0)
                    gate_b(0)
                if 1 <= t <= TILES:
                    a_norm(t - 1)
                if 2 <= t <= TILES:
                    a_res(t - 2)
                if t == 1:
                    dve.wait_ge(s["sn_ps"], 1)
                    V.tensor_scalar(sim2[:, :], banks[7][:, 256:256 + E0], TINY, None, ALU.max).then_inc(s["sn_pre"], 1)
                if t == 0:
                    dve.wait_ge(s["tanh_g"], 1)
                    V.tensor_scalar(bo[:, :], bo[:, :], tg[:, 0:1], None, ALU.mult).then_inc(s["xb"], 1)
                    dve.wait_ge(s["g_act"], 1)
                    V.tensor_scalar(sig0[:, :], sig0[:, :], 0.5, 0.5, ALU.mult, ALU.add).then_inc(s["g_dve"], 1)
                    dve.wait_ge(s["xb"], 1)
                    dve.wait_ge(s["ln_out"], TILES)
                    V.tensor_tensor(xres[:, :, :], xres[:, :, :], bo[:, None, :].to_broadcast([P, TILES, P]),
                                    ALU.add).then_inc(s["xb"], 1)
                if t in (0, 2, 4):
                    keys(1 + t // 2)
                if t == TPH + 1:
                    dve.wait_ge(s["y_out"], TPH)
                    ln(2)

            def ln_3():
                a_res(TILES - 1)
                dve.wait_ge(s["y_out"], TILES)
                ln(3)

            def scaled(n):
                kept = n - KEEP if KEEP <= n < 2 * E0 else n - 2 * E0 - KEEP if n >= 2 * E0 + KEEP else None
                if kept is not None:
                    dve.wait_ge(s["wb_sb"], kept + 1)
                else:
                    dve.wait_ge(s["wb_ps"], n + 1)
                if ZR <= n < 2 * E0 + ZR:
                    dve.wait_ge(s["z_lo"], n - ZR + 1)
                if n >= 2 * E0 + ZR:
                    dve.wait_ge(s["zuse"], n - ZR + 1)
                h = (n // E0) % 2
                if n in (0, E0):
                    dve.wait_ge(s["hT_sb"], 3 + h)
                if n in (2 * E0, 3 * E0):
                    dve.wait_ge(s["ob_sb"], h + 1)
                src = hT[:, half(h)] if n < 2 * E0 else oT[:, h, :]
                weights = banks[spread_bank(n)][:, :] if kept is None else wb[:, kept, :]
                V.tensor_tensor(z[:, n % ZR, :], weights, src, ALU.mult).then_inc(s["z_sb"], 1)

            def low(n):
                dve.wait_ge(s["z_hi"], n + 1)
                V.tensor_tensor(zsp[:, n % ZSP, 1, :], z[:, n % ZR, :], zsp[:, n % ZSP, 0, :].bitcast(F32),
                                ALU.subtract).then_inc(s["z_lo"], 1)

            def attn_a(h):
                a = banks[4 + 3 * h][:, 0:TPH * SEQ].rearrange("p (t k) -> p t k", k=SEQ)
                n = 5 * h
                dve.wait_ge(s["at_ps"], h + 1)
                if h:
                    dve.wait_ge(s["at_d"], n)
                V.tensor_reduce(amax[:, :], a, AX.X, ALU.max).then_inc(s["at_d"], 1)
                dve.wait_ge(s["at_d"], n + 1)
                if h:
                    dve.wait_ge(s["aT_ps"], h)
                V.tensor_tensor(att[:, :, :], a, amax[:, :, None].to_broadcast([P, TPH, SEQ]),
                                ALU.subtract).then_inc(s["at_d"], 1)

            def attn_b(h):
                n = 5 * h
                dve.wait_ge(s["at_exp"], h + 1)
                V.tensor_reduce(asum[:, :], att[:, :, :], AX.X, ALU.add).then_inc(s["at_d"], 1)
                dve.wait_ge(s["at_d"], n + 3)
                V.reciprocal(amax[:, :], asum[:, :]).then_inc(s["at_d"], 1)
                dve.wait_ge(s["at_d"], n + 4)
                V.tensor_tensor(att[:, :, :], att[:, :, :], amax[:, :, None].to_broadcast([P, TPH, SEQ]),
                                ALU.mult).then_inc(s["at_d"], 1)

            def residual(h):
                dve.wait_ge(s["tr_ps"], h + 1)
                for t in range(TPH):
                    V.scalar_tensor_tensor(xres[:, TPH * h + t, :], banks[4 + 3 * h][:, tile(t)], tg[:, 2:3],
                                           xres[:, TPH * h + t, :], ALU.mult, ALU.add).then_inc(s["tr_out"], 1)
                dve.wait_ge(s["tr_out"], TPH * (h + 1))

            def mask():
                dve.wait_ge(ld["mask"], 32)
                V.tensor_copy(maskf[:, :, :], maski[:, :, :]).then_inc(s["mask_f"], 1)
                dve.wait_ge(s["mask_f"], 1)
                V.tensor_scalar(maskf[:, :, :], maskf[:, :, :], 0.0, None, ALU.not_equal).then_inc(s["mask_f"], 1)
                dve.wait_ge(s["mask_f"], 2)
                V.tensor_scalar(maskn[:, :, :], maskf[:, :, :], -1.0, NEG, ALU.add, ALU.mult).then_inc(s["mask_f"], 1)

            def l_soft(h):
                n = 5 * h
                a = banks[4 + 3 * h][:, 0:TPH * SEQ].rearrange("p (t k) -> p t k", k=SEQ)
                ts = slice(TPH * h, TPH * (h + 1))
                dve.wait_ge(s["la_ps"], h + 1)
                dve.wait_ge(s["mask_f"], 3)
                if h:
                    dve.wait_ge(s["lT_ps"], h)
                V.tensor_tensor(att[:, :, :], a, maskf[:, ts, :], ALU.mult).then_inc(s["la_d"], 1)
                dve.wait_ge(s["la_d"], n + 1)
                V.tensor_tensor(att[:, :, :], att[:, :, :], maskn[:, ts, :], ALU.add).then_inc(s["la_d"], 1)
                dve.wait_ge(s["la_d"], n + 2)
                V.tensor_reduce(amax[:, :], att[:, :, :], AX.X, ALU.max).then_inc(s["la_d"], 1)
                dve.wait_ge(s["la_d"], n + 3)
                V.tensor_tensor(att[:, :, :], att[:, :, :], amax[:, :, None].to_broadcast([P, TPH, SEQ]),
                                ALU.subtract).then_inc(s["la_d"], 1)

            def l_sum(h):
                dve.wait_ge(s["la_exp"], h + 1)
                V.tensor_reduce(asum[:, :], att[:, :, :], AX.X, ALU.add).then_inc(s["la_d"], 1)
                dve.wait_ge(s["la_d"], 5 * h + 5)
                V.reciprocal(amax[:, :], asum[:, :]).then_inc(s["lrec"], 1)
                dve.wait_ge(s["lrec"], 2 * h + 1)
                V.tensor_scalar(asum[:, :], amax[:, :], tg[:, 1:2], None, ALU.mult).then_inc(s["lrec"], 1)

            def l_out(h):
                dve.wait_ge(s["lrec"], 2 * h + 2)
                dve.wait_ge(s["lo_ps"], h + 1)
                for t in range(TPH):
                    V.scalar_tensor_tensor(xres[:, TPH * h + t, :], banks[2 + 3 * h][:, tile(t)], asum[:, t:t + 1],
                                           xres[:, TPH * h + t, :], ALU.mult, ALU.add).then_inc(s["lo_out"], 1)
                dve.wait_ge(s["lo_out"], TPH * (h + 1))

            cdn = [0]

            def cstep(ins):
                ins.then_inc(s["cd"], 1)
                cdn[0] += 1

            def cwait():
                dve.wait_ge(s["cd"], cdn[0])

            def router_a(h):
                ts = slice(TPH * h, TPH * (h + 1))
                dve.wait_ge(s["cl_ps"], h + 1)
                V.tensor_copy(lgc[:, ts, :], banks[3 + 3 * h][:, 0:TPH * (E1 + 1)]
                              .rearrange("p (t e) -> p t e", t=TPH)).then_inc(s["cl_sb"], 1)
                dve.wait_ge(s["cl_sb"], 2 * h + 1)
                cwait()
                for t in range(TPH):
                    cstep(V.max(topc[:, t, :], lgc[:, TPH * h + t, 0:E1]))
                cwait()
                for t in range(TPH):
                    cstep(V.match_replace(rep[:, t, :], topc[:, t, :], lgc[:, TPH * h + t, 0:E1], LOW))
                cstep(V.tensor_tensor(wex[:, :, :], lgc[:, ts, 0:E1], topc[:, :, 0:1].to_broadcast([P, TPH, E1]),
                                      ALU.subtract))
                assert cdn[0] == CD * h + CD_EXP
                cwait()
                V.tensor_tensor(chosen[:, ts, :], rep[:, :, :], lgc[:, ts, 0:E1],
                                ALU.not_equal).then_inc(s["cl_sb"], 1)

            def router_pos(h):
                ts = slice(TPH * h, TPH * (h + 1))
                dve.wait_ge(s["cl_sb"], 2 * h + 2)
                dve.wait_ge(s["pos_ps"], h + 1)
                if h:
                    dve.wait_ge(s["pos_sb"], h)
                V.scalar_tensor_tensor(post[:, :, :], chosen[:, ts, :], -BIG,
                                       banks[4 + 3 * h][:, 0:TPH * E1].rearrange("p (t e) -> p t e", t=TPH),
                                       ALU.mult, ALU.add).then_inc(s["post"], 1)
                dve.wait_ge(s["post"], h + 1)
                V.tensor_scalar(pos16[:, :, ts, :], post[:, :, :].rearrange("p t (g e) -> p g t e", e=2 * DG), BIG,
                                float(2 * CAP), ALU.add, ALU.min).then_inc(s["pos_sb"], 1)

            def router_b(h):
                ts = slice(TPH * h, TPH * (h + 1))
                dve.wait_ge(s["cl_sb"], 2 * h + 2)
                dve.wait_ge(s["cexp"], h + 1)
                cstep(V.tensor_tensor(wex[:, :, :], wex[:, :, :], chosen[:, ts, :], ALU.mult))
                cwait()
                cstep(V.tensor_reduce(csum[:, :], wex[:, :, :], AX.X, ALU.add))
                cwait()
                cstep(V.reciprocal(g1[:, :], csum[:, :]))
                cwait()
                cstep(V.tensor_tensor(wex[:, :, :], wex[:, :, :], g1[:, :, None].to_broadcast([P, TPH, E1]), ALU.mult))
                cwait()
                cstep(V.tensor_copy(wc3[:, ts, :, 0], wex[:, :, :]))
                cwait()
                cstep(V.tensor_tensor(wres[:, :, :], wex[:, :, :], wc3[:, ts, :, 0], ALU.subtract))
                cwait()
                cstep(V.tensor_copy(wc3[:, ts, :, 1], wres[:, :, :]))
                cwait()
                cstep(V.tensor_tensor(wc3[:, ts, :, 2], wres[:, :, :], wc3[:, ts, :, 1], ALU.subtract))
                assert cdn[0] == CD * (h + 1), cdn[0]

            def dispatch(g):
                if g == 0:
                    dve.wait_ge(s["pos_sb"], 2)
                V.tensor_tensor(disp[:, g, :, :, :].rearrange("p t q (c e) -> p (t q) c e", e=2),
                                slotc[:, None, :, :].to_broadcast([P, TILES * DG, CAP, 2]),
                                pos16[:, g, :, :].rearrange("p t (q e) -> p (t q) e", e=2)[:, :, None, :]
                                .to_broadcast([P, TILES * DG, CAP, 2]), ALU.is_equal).then_inc(s["disp"], 1)

            def shared(k):
                h, f = k // 2, k % 2
                dve.wait_ge(s["sh_th"], k + 1)
                if h and f == 0:
                    dve.wait_ge(s["sd_ps"], h)
                V.scalar_tensor_tensor(shg[:, f, :], sth[:, :], 1.0, banks[SH_BANK[k]][:, :], ALU.add,
                                       ALU.mult).then_inc(s["sh_a"], 1)
                dve.wait_ge(s["sh_a"], k + 1)
                V.scalar_tensor_tensor(shg[:, f, :], shg[:, f, :], 0.5, banks[SH_BANK[k] + 1][:, :], ALU.mult,
                                       ALU.mult).then_inc(s["sh_act"], 1)

            def shared_gate(h):
                ts = slice(TPH * h, TPH * (h + 1))
                dve.wait_ge(s["ctanh"], h + 1)
                V.tensor_scalar(sg[:, ts], sg[:, ts], 0.5, 0.5, ALU.mult, ALU.add).then_inc(s["sgv"], 1)
                dve.wait_ge(s["sgv"], 2 * h + 1)
                V.tensor_scalar(sg[:, ts], sg[:, ts], tg[:, 3:4], None, ALU.mult).then_inc(s["sgv"], 1)

            def shared_out(h):
                dve.wait_ge(s["sd_ps"], h + 1)
                dve.wait_ge(s["sgv"], 2 * h + 2)
                for t in range(TPH):
                    T = TPH * h + t
                    V.scalar_tensor_tensor(xres[:, T, :], banks[2 + 3 * h][:, tile(t)], sg[:, T:T + 1], xres[:, T, :],
                                           ALU.mult, ALU.add).then_inc(s["sd_out"], 1)

            def slot_weights(g):
                qs = slice(GRP * g, GRP * (g + 1))
                dve.wait_ge(s["ws_ps"], g + 1)
                V.tensor_reduce(wslot2[:, qs, :], banks[2][:, 0:6 * GRP].rearrange("p (q e k) -> p q e k", e=2, k=3),
                                AX.X, ALU.add).then_inc(s["ws_sb"], 1)
                dve.wait_ge(s["ws_sb"], 3 * g + 1)
                V.tensor_scalar(wslot[:, qs], wslot2[:, qs, 0], parity[:, 0:1], None, ALU.mult).then_inc(s["ws_sb"], 1)
                dve.wait_ge(s["ws_sb"], 3 * g + 2)
                V.scalar_tensor_tensor(wslot[:, qs], wslot2[:, qs, 1], parity[:, 1:2], wslot[:, qs], ALU.mult,
                                       ALU.add).then_inc(s["ws_sb"], 1)

            def low_out(g):
                dve.wait_ge(s["dn_hi"], GRP * (g + 1))
                dve.wait_ge(s["ws_sb"], 3 * (g + 1))
                for n in range(GRP * g, GRP * (g + 1)):
                    V.scalar_tensor_tensor(esp[:, n % EPR, 1, :], banks[4][:, tile(n % GRP)], wslot[:, n:n + 1],
                                           esp[:, n % EPR, 0, :].bitcast(F32), ALU.mult,
                                           ALU.subtract).then_inc(s["dn_lo"], 1)

            def disp_T(n):
                dve.wait_ge(s["dT_ps"], n + 1)
                if n >= EPR:
                    dve.wait_ge(s["sc_g"], n - EPR + 1)
                V.tensor_copy(dispT[:, n % EPR, :], banks[disp_bank(n)][:, :].bitcast(F16))\
                    .then_inc(s["dT_sb"] if n < EP - GRP else s["dT_last"], 1)

            def tokens(g):
                dve.wait_ge(s["xl_sb"], g + 1)
                if g >= 2:
                    dve.wait_ge(s["up_ps"], g - 1)
                V.tensor_tensor(xeT[:, g % 2, :, :].rearrange("p q n -> p (q n)"), banks[0][:, :], xlow[:, :],
                                ALU.add).then_inc(s["xe_sb"], 1)

            for n in range(4 * E0):
                scaled(n)
                if 1 <= n <= 2 * E0:
                    low(n - 1)
                if n == 1:
                    ln_3()
                if n == 7:
                    gate_a(1)
                if n == 9:
                    gate_b(1)
                if n == E0 + 2:
                    attn_a(0)
                if n == E0 + 4:
                    mask()
                if n == E0 + 7:
                    attn_b(0)
                if n == 2 * E0 + 6:
                    attn_a(1)
                if n == 2 * E0 + 7:
                    attn_b(1)
                if n == 3 * E0 + 3:
                    residual(0)
                if n == 3 * E0 + 4:
                    ln(4)
                if n == 3 * E0 + 10:
                    l_soft(0)
                if n == 3 * E0 + 12:
                    l_sum(0)
                if n == 3 * E0 + 15:
                    l_out(0)
            ln(5)
            residual(1)
            ln(6)
            router_a(0)
            router_pos(0)
            l_soft(1)
            l_sum(1)
            l_out(1)
            ln(7)
            shared(0)
            router_b(0)
            shared(1)
            shared_gate(0)
            router_a(1)
            shared_out(0)
            router_pos(1)
            dispatch(0)
            dispatch(1)
            shared(2)
            shared(3)
            dispatch(2)
            tokens(0)
            shared_gate(1)
            router_b(1)
            dve.wait_ge(s["act0"], 1)
            for g in range(NGRP):
                r = g % 2
                dve.wait_ge(s["up_th"], g + 1)
                if g:
                    dve.wait_ge(s["up_act"], 2 * g)
                V.scalar_tensor_tensor(ab[:, :], th[:, :], 1.0, banks[3][:, 0:256], ALU.add,
                                       ALU.mult).then_inc(s["up_a"], 1)
                dve.wait_ge(s["up_a"], g + 1)
                if g >= 2:
                    dve.wait_ge(s["dn_ps"], g - 1)
                for i in range(2):
                    V.scalar_tensor_tensor(actb[seq(i), r, :, :, i],
                                           ab[seq(i), :].rearrange("p (q c) -> p q c", q=GRP), 0.5,
                                           banks[3][seq(i), 256:512].rearrange("p (q c) -> p q c", q=GRP),
                                           ALU.mult, ALU.mult).then_inc(s["up_act"], 1)
                if g == 0:
                    slot_weights(0)
                    shared_out(1)
                if 2 * g + 3 < EP // DG:
                    dispatch(2 * g + 3)
                if g + 1 == NGRP:
                    disp_T(EP - 2)
                low_out(g)
                disp_T(GRP * g + 3)
                if g + 1 < NGRP:
                    tokens(g + 1)
                    slot_weights(g + 1)
                if 2 * g + 4 < EP // DG:
                    dispatch(2 * g + 4)
            for t in range(TILES):
                dve.wait_ge(s["yt_ps"], t // TPH + 1)
                dve.wait_ge(s["sd_out"], TILES)
                V.scalar_tensor_tensor(xres[:, t, :], banks[t // TPH][:, tile(t % TPH)], tg[:, 3:4], xres[:, t, :],
                                       ALU.mult, ALU.add).then_inc(s["fin"], 1)

        @block.tensor
        def _(pe):
            def mm(out, lhsT, rhs, start=True, stop=True):
                return nc.tensor.matmul(out, lhsT, rhs, start=start, stop=stop)

            pe.wait_ge(ld["ctxT"], 16)
            pe.wait_ge(ld["wkv"], 2 * 16)
            for h in range(HALVES):
                mm(banks[h][:, :], wk[:, :], ctxT[:, half(h)]).then_inc(s["kT_ps"], 1)

            def values(k):
                for j in range(4):
                    b = 4 * k + j
                    for i in range(2):
                        last = mm(banks[2 + k][seq(i), tile(j)], ctxT[:, seq(b)], wv[:, :])
                last.then_inc(s["v_ps"], 1)

            def lnT(n, bank):
                h = LN_HALF[n]
                for t in range(TPH):
                    pe.wait_ge(s["ln_out"], TPH * n + t + 1)
                    last = nc.tensor.transpose(bank[:, tile(t)], hn[:, TPH * h + t, :], ident[:, :])
                last.then_inc(s["hT_ps"], 1)

            def queries(h):
                pe.wait_ge(s["hT_sb"], h + 1)
                pe.wait_ge(s["kT_sb"], 1)
                mm(banks[6 * h][:, :], wq[:, :], hT[:, half(h)]).then_inc(s["q_ps"], 1)

            values(0)
            values(1)
            pe.wait_ge(s["consts"], NCONST)
            pe.wait_ge(ld["wqo"], 3 * 16)
            lnT(0, banks[6])
            values(2)
            queries(0)
            values(3)

            def scores(t, k):
                n = t // 2 + 1
                b = 2 * t + k
                pe.wait_ge(s["kexp_d"], KD * n)
                pe.wait_ge(s["kexp_a"], (PAIRS - KD) * n)
                pe.wait_ge(s["q_sb"], 2 * (t // TPH + 1))
                if t == 0:
                    pe.wait_ge(s["kT_sb"], k + 1)
                elif t == 1:
                    pe.wait_ge(s["v_sb"], 5)
                else:
                    pe.wait_ge(s["sc_sub"], 2 * (t - 2) + k + 1)
                mm(banks[2 * (t % 2) + k][:, :], qexp[:, b, :, :].rearrange("p e q -> p (e q)"),
                   kexp[:, b // 4, b % 4, :, :].rearrange("p j k -> p (j k)")).then_inc(s["sc_ps"], 1)

            def probs_T(t):
                pe.wait_ge(s["sc_exp"], t + 1)
                if t == 0:
                    pe.wait_ge(s["v_sb"], 9)
                else:
                    pe.wait_ge(s["pT_sb"], 2 * t)
                for j in range(PAIRS):
                    last = nc.tensor.transpose(banks[4 + j // 4][:, tile(j % 4)], prob[:, t % 2, tile(j)], ident[:, :])
                last.then_inc(s["pT_ps"], 1)

            def pv(t):
                pe.wait_ge(s["pT_sb"], 2 * (t + 1))
                if t:
                    pe.wait_ge(s["pv_sb"], 2 * t)
                for j in range(PAIRS):
                    last = mm(banks[6][:, 36 * j:36 * j + 36], probT[:, tile(j)],
                              vblk[:, 2 * CHUNKS * t + j, :, :, :].rearrange("p i e d -> p (i e d)"))
                last.then_inc(s["pv_ps"], 1)

            def heads_T(t):
                pe.wait_ge(s["pv_sb"], 2 * (t + 1))
                if t:
                    pe.wait_ge(s["y_out"], t)
                else:
                    pe.wait_ge(s["sn_pre"], 1)
                nc.tensor.transpose(banks[7][:, 0:P], ohead[:, :], ident[:, :]).then_inc(s["oT_ps"], 1)

            def project(t):
                pe.wait_ge(s["oT_sb"], t + 1)
                for k in range(2):
                    for i in range(2):
                        last = mm(banks[7][seq(k), P:2 * P], oheadT[seq(k), seq(i)], wo[seq(k), i, :], start=i == 0,
                                  stop=i == 1)
                last.then_inc(s["y_ps"], 1)

            def gate_lg(h):
                pe.wait_ge(s["hT_sb"], 3 + h)
                pe.wait_ge(s["sn"], 1)
                for t in range(TPH):
                    last = mm(banks[LG_BANK[h]][:, E0 * t:E0 * (t + 1)], hT[:, tile(TPH * h + t)], simm[:, :])
                last.then_inc(s["lg_ps"], 1)

            def gate_T(h):
                pe.wait_ge(s["w3"], h + 1)
                out = banks[WT_BANK[h]][0:3 * E0, 0:HT // 2].bitcast(BF16)
                for t in range(TPH):
                    last = nc.tensor.transpose(out[:, tile(t)], w3[:, TPH * h + t, :], identb[:, :])
                last.then_inc(s["wT_ps"], 1)

            def spread(n):
                h = (n // E0) % 2
                if n == 0:
                    pe.wait_ge(s["sel"], NSEL)
                pe.wait_ge(s["wT_sb"], min(n // E0, 1) + 1)
                if n == 1:
                    pe.wait_ge(s["gd"], GD)
                if n in (2 * E0 + 2, 2 * E0 + 3):
                    pe.wait_ge(s["ob_sb"], 1)
                    pe.wait_ge(s["aT_sb"], 1)
                elif n >= 2:
                    last_use = n - (2 if n < 2 * E0 + 2 else 4)
                    if last_use < KEEP:
                        pe.wait_ge(s["z_sb"], last_use + 1)
                    elif last_use < 2 * E0:
                        pe.wait_ge(s["wb_sb"], last_use + 1 - KEEP)
                    else:
                        pe.wait_ge(s["z_sb"], last_use + 1)
                mm(banks[spread_bank(n)][:, :], selw[:, n % E0, :], wT[:, half(h)]).then_inc(s["wb_ps"], 1)

            for t in range(TILES + 2):
                if t < TILES:
                    scores(t, 0)
                if t < 2:
                    scores(t, 1)
                if t == 0:
                    lnT(1, banks[7])
                    queries(1)
                if t == 1:
                    pe.wait_ge(s["sim2"], 1)
                    mm(banks[7][:, 256:256 + E0], ones[:, :], sim2[:, :]).then_inc(s["sn_ps"], 1)
                if 1 <= t <= TILES:
                    probs_T(t - 1)
                if t == TILES + 1:
                    gate_T(0)
                if t >= 2:
                    heads_T(t - 2)
                if 2 <= t < TILES:
                    scores(t, 1)
                if t == TILES - 1:
                    pe.wait_ge(s["sc_sub"], 2 * TILES - 2)
                    lnT(2, banks[0])
                if 1 <= t <= TILES:
                    pv(t - 1)
                if t == TILES + 1:
                    spread(0)
                    spread(1)
                if t >= 2:
                    project(t - 2)
                if t == TILES - 1:
                    gate_lg(0)

            def experts(n):
                h, e = (n // E0) % 2, n % E0
                base = 2 + 3 * h
                cols = slice(e * P, (e + 1) * P)
                if n < 2 * E0:
                    pe.wait_ge(s["z_lo"], n + 1)
                    if n == 0:
                        pe.wait_ge(s["split_lo"], 3 * NSPLIT)
                    if n == E0:
                        pe.wait_ge(s["gd"], 2 * GD)
                    for i in range(3):
                        out = banks[base + i][:, :]
                        mm(out, wsp[:, 0, i, cols], zsp[:, n % ZSP, 0, :], start=e == 0, stop=False)
                        mm(out, wsp[:, 0, i, cols], zsp[:, n % ZSP, 1, :], start=False, stop=False)
                        last = mm(out, wsp[:, 1, i, cols], zsp[:, n % ZSP, 0, :], start=False, stop=e == E0 - 1)
                else:
                    pe.wait_ge(s["z_sb"], n + 1)
                    if e == 0:
                        pe.wait_ge(ld["oexp"], 16)
                    last = mm(banks[base + 1][:, :], oexp[:, e, :], z[:, n % ZR, :], start=e == 0, stop=e == E0 - 1)
                last.then_inc(s["zuse"], 1)

            def attn_a(h):
                base = 2 + 3 * h
                pe.wait_ge(s["qkv_sb"], 3 * (h + 1))
                for i in range(8):
                    last = nc.tensor.transpose(banks[base + i // 4][0:SEQ, tile(i % 4)], qkvT[:, 2, seq(i)],
                                               ident[:, :])
                last.then_inc(s["v2_ps"], 1)
                for t in range(TPH):
                    for i in range(2):
                        last = mm(banks[base + 2][seq(i), SEQ * t:SEQ * (t + 1)], qkvT[:, 0, seq(2 * t + i)],
                                  qkvT[:, 1, seq(2 * t + i)])
                last.then_inc(s["at_ps"], 1)

            def attn_T(h):
                pe.wait_ge(s["at_d"], 5 * (h + 1))
                for t in range(TPH):
                    last = nc.tensor.transpose(banks[4 + 3 * h][0:SEQ, tile(t)], att[:, t, :], ident[:, :])
                last.then_inc(s["aT_ps"], 1)

            def attn_o(h):
                pe.wait_ge(s["aT_sb"], h + 1)
                pe.wait_ge(s["v2_sb"], 2 * (h + 1))
                for b in range(8):
                    last = mm(banks[2 + 3 * h][:, seq(b)], vk[0:SEQ, b, :], attT[0:SEQ, seq(b)])
                last.then_inc(s["ob_ps"], 1)

            def out_T(h):
                pe.wait_ge(s["acc_sb"], h + 1)
                for t in range(TPH):
                    last = nc.tensor.transpose(banks[4 + 3 * h][:, tile(t)], accT[:, tile(t)], ident[:, :])
                last.then_inc(s["tr_ps"], 1)

            def l_scores(h):
                pe.wait_ge(s["hT_sb"], 5 + 2 * h)
                pe.wait_ge(s["tr_out"], TPH * (h + 1))
                for t in range(TPH):
                    for i in range(2):
                        b = 2 * (TPH * h + t) + i
                        last = mm(banks[4 + 3 * h][seq(i), SEQ * t:SEQ * (t + 1)], hT[:, seq(b)], ctxT[:, seq(b)])
                last.then_inc(s["la_ps"], 1)

            def l_T(h):
                pe.wait_ge(s["la_exp"], h + 1)
                for t in range(TPH):
                    last = nc.tensor.transpose(banks[3 + 3 * h][0:SEQ, tile(t)], att[:, t, :], ident[:, :])
                last.then_inc(s["lT_ps"], 1)

            def l_values(h):
                pe.wait_ge(s["lT_sb"], h + 1)
                pe.wait_ge(ld["ctxk"], 16)
                for t in range(TPH):
                    for i in range(2):
                        b = 2 * (TPH * h + t) + i
                        last = mm(banks[2 + 3 * h][seq(i), tile(t)], attT[0:SEQ, seq(2 * t + i)], ctxk[:, b, :])
                last.then_inc(s["lo_ps"], 1)

            def gather(d):
                pe.wait_ge(s["disp"], d + 1)
                if d // 2:
                    pe.wait_ge(s["xe_sb"], d // 2)
                else:
                    pe.wait_ge(s["xh_lo"], 2)
                    pe.wait_ge(s["sh_act"], 1)
                for k in range(2):
                    for t in range(TILES):
                        last = mm(banks[k][:, 256 * (d % 2):256 * (d % 2 + 1)], xh[:, t, k, :],
                                  disp[:, d, t, :, :].rearrange("p q s -> p (q s)"), start=t == 0,
                                  stop=t == TILES - 1)
                last.then_inc(s["ga_ps"], 1)

            def weights(g):
                if g:
                    pe.wait_ge(s["ws_sb"], 3 * (g - 1) + 1)
                else:
                    pe.wait_ge(s["cd"], 2 * CD)
                    pe.wait_ge(s["sd_out"], TPH)
                for q in range(GRP):
                    n = GRP * g + q
                    for t in range(TILES):
                        last = mm(banks[2][:, 6 * q:6 * q + 6], disp[:, n // DG, t, n % DG, :],
                                  wc3[:, t, 2 * n:2 * n + 2, :].rearrange("p e k -> p (e k)"),
                                  start=t == 0, stop=t == TILES - 1)
                last.then_inc(s["ws_ps"], 1)

            def ln_T3():
                pe.wait_ge(s["y_out"], TILES)
                lnT(3, banks[5])

            def logits(h):
                pe.wait_ge(ld["gw"], 32)
                pe.wait_ge(s["hT_sb"], 6 + 2 * h)
                for t in range(TPH):
                    last = mm(banks[3 + 3 * h][:, (E1 + 1) * t:(E1 + 1) * (t + 1)], hT[:, tile(TPH * h + t)], gw[:, :])
                last.then_inc(s["cl_ps"], 1)

            def positions(h):
                pe.wait_ge(s["cl_sb"], 2 * h + 2)
                for t in range(TPH):
                    T = TPH * h + t
                    out = banks[4 + 3 * h][:, E1 * t:E1 * (t + 1)]
                    for k in range(T):
                        mm(out, ones16[:, :], chosen[:, k, :], start=k == 0, stop=False)
                    last = mm(out, upper16[:, :], chosen[:, T, :], start=T == 0, stop=True)
                last.then_inc(s["pos_ps"], 1)

            def shared(k):
                h, f = k // 2, k % 2
                pe.wait_ge(ld["shared"], 32)
                if k in (1, 3):
                    pe.wait_ge(s["cl_sb"], k)
                    pe.wait_ge(s["post"], k // 2 + 1)
                if k == 2:
                    pe.wait_ge(s["sh_act"], 2)
                mm(banks[SH_BANK[k]][:, :], sgu[:, f * P:(f + 1) * P], hT[:, half(h)])
                mm(banks[SH_BANK[k] + 1][:, :], sgu[:, SHARED + f * P:SHARED + (f + 1) * P], hT[:, half(h)])\
                    .then_inc(s["sh_ps"], 1)

            def shared_down(h):
                pe.wait_ge(s["sh_act"], 2 * (h + 1))
                for t in range(TPH):
                    for j in range(2):
                        last = mm(banks[2 + 3 * h][:, tile(t)], shg[:, j, tile(t)], sdn[:, j, :], start=j == 0,
                                  stop=j == 1)
                last.then_inc(s["sd_ps"], 1)

            def disp_T(n):
                if n == EP - 1:
                    pe.wait_ge(s["ws_sb"], 3 * (NGRP - 1) + 1)
                elif 0 < n <= EP - GRP:
                    pe.wait_ge(s["dT_sb"], n)
                out = banks[disp_bank(n)][:, :].bitcast(F16)
                for t in range(TILES):
                    last = nc.tensor.transpose(out[:, tile(t)], disp[:, n // DG, t, n % DG, :], ident16[:, :])
                last.then_inc(s["dT_ps"], 1)

            def up(g):
                pe.wait_ge(ld_exp[g % 2], 32 * (g // 2 + 1))
                pe.wait_ge(s["xe_sb"], g + 1)
                if g:
                    pe.wait_ge(s["up_act"], 2 * g)
                for q in range(GRP):
                    for f in range(2):
                        for i in range(2):
                            x = xeT[:, g % 2, q, :].rearrange("p (c e) -> p c e", e=2)[:, :, i]
                            last = mm(banks[3][seq(i), 256 * f + SEQ * q:256 * f + SEQ * (q + 1)],
                                      wguR[:, g % 2, 2 * q + i, f * INNER:(f + 1) * INNER], x)
                last.then_inc(s["up_ps"], 1)

            def down(g):
                pe.wait_ge(s["up_act"], 2 * (g + 1))
                if g:
                    pe.wait_ge(s["dn_lo"], GRP * g)
                for q in range(GRP):
                    last = mm(banks[4][:, tile(q)], actb[:, g % 2, q, :, :].rearrange("p c e -> p (c e)"),
                              wdR[:, g % 2, q, :])
                last.then_inc(s["dn_ps"], 1)

            def scatter_half(n, h):
                for k in range(2):
                    last = mm(banks[5 + h][:, :], esp[:, n % EPR, k, :], dispT[:, n % EPR, half(h)],
                              start=n == 0 and k == 0, stop=n == EP - 1 and k == 1)
                return last

            def scatter(n):
                pe.wait_ge(s["dn_lo"], n + 1)
                pe.wait_ge(s["dT_sb"], n + 1)
                for h in range(HALVES):
                    last = scatter_half(n, h)
                last.then_inc(s["sc_g"], 1)

            def scatter_last(h):
                for n in range(EP - GRP, EP):
                    pe.wait_ge(s["dn_lo"], n + 1)
                    if n < EP - 2:
                        pe.wait_ge(s["dT_sb"], n + 1)
                    else:
                        pe.wait_ge(s["dT_last"], n - EP + 3)
                    last = scatter_half(n, h)
                last.then_inc(s["sc_end"], 1)

            ahead = 2
            for n in range(4 * E0):
                while ahead <= min(n + (2 if n < KEEP else 3), 2 * E0 + KEEP - 1):
                    spread(ahead)
                    ahead += 1
                experts(n)
                if n == 3:
                    ln_T3()
                if n == 4:
                    gate_lg(1)
                if n == 9:
                    gate_T(1)
                if n == E0:
                    attn_a(0)
                if n == E0 + 5:
                    attn_T(0)
                if n == E0 + 10:
                    attn_o(0)
                if n == 2 * E0 + 3:
                    attn_a(1)
                if n == 2 * E0 + 7:
                    attn_T(1)
                if n == 2 * E0 + 12:
                    attn_o(1)
                if n == 3 * E0:
                    out_T(0)
                if n == 3 * E0 + 6:
                    lnT(4, banks[2])
                if n == 3 * E0 + 7:
                    l_scores(0)
                if n == 3 * E0 + 10:
                    l_T(0)
                if n == 3 * E0 + 13:
                    l_values(0)
                if n == 3 * E0 + 15:
                    out_T(1)
            lnT(5, banks[2])
            logits(0)
            lnT(6, banks[5])
            l_scores(1)
            positions(0)
            shared(0)
            l_T(1)
            shared(1)
            l_values(1)
            lnT(7, banks[5])
            logits(1)
            shared_down(0)
            positions(1)
            shared(2)
            shared(3)
            gather(0)
            gather(1)
            shared_down(1)
            pe.wait_ge(s["sh_act"], 4)
            for g in range(NGRP - 1):
                disp_T(GRP * g)
                up(g)
                disp_T(GRP * g + 1)
                gather(2 * g + 2)
                if g == 0:
                    weights(0)
                disp_T(GRP * g + 2)
                down(g)
                gather(2 * g + 3)
                disp_T(GRP * g + 3)
                weights(g + 1)
                if g == 0:
                    pe.wait_ge(s["sd_out"], TILES)
                for q in range(GRP if g < NGRP - 2 else GRP // 2):
                    scatter(GRP * g + q)
            up(NGRP - 1)
            for n in range(EP - GRP, EP):
                disp_T(n)
            down(NGRP - 1)
            for n in range(EP - GRP - GRP // 2, EP - GRP):
                scatter(n)
            for h in range(HALVES):
                scatter_last(h)
            for h in range(HALVES):
                pe.wait_ge(s["yT_sb"], h + 1)
                for t in range(TPH):
                    last = nc.tensor.transpose(banks[h][:, tile(t)], yT[:, tile(TPH * h + t)], ident[:, :])
                last.then_inc(s["yt_ps"], 1)


def kernel(**inputs):
    import numpy as np
    import concourse.bacc as bacc
    from concourse.bass_utils import run_bass_kernel_spmd

    a = {k: np.asarray(v) for k, v in inputs.items()}
    x, c = a["x"].reshape(TOKENS, P), a["ctx_1024"].reshape(TOKENS, P)
    laid = {
        "x": x, "ctx": c, "ctxT": c.T, "mask": a["mask_BxS2_ik1"], "g_xattn": a["g_xattn"], "g_ffn": a["g_ffn"],
        "WqT": a["L0_xattn_Wq"].T, "WkT": a["L0_xattn_Wk"].T, "WvT": a["L0_xattn_Wv"].T,
        "WoT": a["L0_xattn_Wo"].T.reshape(PAIRS, 2, HD, P).transpose(0, 2, 1, 3).reshape(PAIRS * HD, 2, P),
        "bo": a["L0_xattn_bo"], "sim": a["L0_ffn_sim_matrix"], "gates": a["L0_ffn_gates"],
        "q_proj": a["L0_ffn_q_proj"], "k_proj": a["L0_ffn_k_proj"], "v_proj": a["L0_ffn_v_proj"],
        "o_proj": a["L0_ffn_o_proj"], "gate_w": a["L1_ffn_gate_w"], "sgate_w": a["L1_ffn_shared_gate_w"],
        "sgu": a["L1_ffn_shared_gate_up_w"], "sdn": a["L1_ffn_shared_down_w"], "egu": a["L1_ffn_expert_gate_up_w"],
        "edn": a["L1_ffn_expert_down_w"],
    }
    laid = {k: np.ascontiguousarray(v) for k, v in laid.items()}
    nc = bacc.Bacc("TRN2", target_bir_lowering=False, num_devices=1, dynamic_dma_scratch_size=1024)
    d = {k: nc.dram_tensor("in_" + k, v.shape, mybir.dt.from_np(v.dtype), kind="ExternalInput").ap()
         for k, v in laid.items()}
    d["out"] = nc.dram_tensor("out_0", (TOKENS, P), F32, kind="ExternalOutput").ap()
    program(nc, d)
    r = run_bass_kernel_spmd(nc, [{"in_" + k: v for k, v in laid.items()}], core_ids=[0])
    return r.results[0]["out_0"].reshape(BATCH, SEQ, P)
```
